# Optimizing a Trainium2 kernel written in Bass

```python
import numpy as np
import jax
import jax.numpy as jnp

def _softmax(x, axis=-1):
    return jax.nn.softmax(x, axis=axis)

def _gelu(x):
    return jax.nn.gelu(x, approximate=True)

def _silu(x):
    return jax.nn.silu(x)

def _sigmoid(x):
    return jax.nn.sigmoid(x)

def _layernorm(x, axis=-1, eps=1e-05):
    m = jnp.mean(x, axis=axis, keepdims=True)
    v = jnp.var(x, axis=axis, keepdims=True)
    return (x - m) / jnp.sqrt(v + eps)

def _scatter_add(tgt, idx, src, axis=0):
    return tgt.at[idx].add(src)

def _segment_sum(src, seg, n):
    return jax.ops.segment_sum(src, seg, n)
kernel_name = 'mk_seq_postln_d2_jaxref_r8_5dfd17'

def setup_inputs(seed: int=0):
    np.random.seed(seed)
    _w = jnp.asarray

    def _L0_attn_setup():
        import jax, jax.numpy as jnp
        import numpy as np
        NUM_HEADS = 16
        DIM = 128
        HARMONICS = 32
        B, L = (2, 256)

        def holo_linear(x, basis, phase, amp):
            resonance = jnp.einsum('bli,hi->blh', x, basis)
            w = amp * jnp.cos(phase)
            return jnp.einsum('blh,oh->blo', resonance, w)
        key = jax.random.key(seed)
        ks = jax.random.split(key, 13)
        two_pi = 2.0 * np.pi

        def make_proj(k0, k1):
            basis = jax.random.normal(k0, (HARMONICS, DIM), dtype=jnp.float32)
            basis = basis / jnp.linalg.norm(basis, axis=1, keepdims=True)
            phase = jax.random.normal(k1, (DIM, HARMONICS), dtype=jnp.float32) * two_pi
            amp = jnp.ones((DIM, HARMONICS), dtype=jnp.float32) / HARMONICS
            return (basis, phase, amp)
        x = jax.random.normal(ks[0], (B, L, DIM), dtype=jnp.float32)
        bq, pq, aq = make_proj(ks[1], ks[2])
        bk, pk, ak = make_proj(ks[3], ks[4])
        bv, pv, av = make_proj(ks[5], ks[6])
        bo, po, ao = make_proj(ks[7], ks[8])
        return {'x': x, 'basis_q': bq, 'phase_q': pq, 'amp_q': aq, 'basis_k': bk, 'phase_k': pk, 'amp_k': ak, 'basis_v': bv, 'phase_v': pv, 'amp_v': av, 'basis_o': bo, 'phase_o': po, 'amp_o': ao}
    _L0_attn_in = _L0_attn_setup()

    def _L0_ffn_setup():
        import math
        import jax, jax.numpy as jnp
        import numpy as np
        H = 128
        F = 512
        E = 8
        TOP_K = 2
        CAP_FACTOR = 1.25
        MIN_CAP = 4
        SHARED_SCALE = 0.1

        def _top2_gating(logits, capacity):
            N, nE = logits.shape
            gates = jax.nn.softmax(logits, axis=-1)
            idx1 = jnp.argmax(gates, axis=-1)
            mask1 = jax.nn.one_hot(idx1, nE, dtype=gates.dtype)
            idx2 = jnp.argmax(gates * (1.0 - mask1), axis=-1)
            mask2 = jax.nn.one_hot(idx2, nE, dtype=gates.dtype)
            pos1 = jnp.cumsum(mask1, axis=0) - mask1
            mask1 = mask1 * (pos1 < capacity)
            pos2 = jnp.cumsum(mask2, axis=0) - mask2 + jnp.sum(mask1, axis=0, keepdims=True)
            mask2 = mask2 * (pos2 < capacity)
            g1 = jnp.sum(gates * mask1, axis=-1)
            g2 = jnp.sum(gates * mask2, axis=-1)
            denom = jnp.maximum(g1 + g2, jnp.finfo(gates.dtype).eps)
            g1, g2 = (g1 / denom, g2 / denom)
            loc1 = jnp.sum(pos1 * mask1, axis=-1).astype(jnp.int32)
            loc2 = jnp.sum(pos2 * mask2, axis=-1).astype(jnp.int32)
            oh1 = jax.nn.one_hot(loc1, capacity, dtype=gates.dtype)
            oh2 = jax.nn.one_hot(loc2, capacity, dtype=gates.dtype)
            combine = (g1[:, None] * mask1)[:, :, None] * oh1[:, None, :] + (g2[:, None] * mask2)[:, :, None] * oh2[:, None, :]
            dispatch = (combine > 0).astype(gates.dtype)
            return (combine, dispatch)
        key = jax.random.key(seed)
        ks = jax.random.split(key, 10)
        s_h = 1.0 / math.sqrt(H)
        s_f = 1.0 / math.sqrt(F)
        return {'hidden_states': jax.random.normal(ks[0], (2, 256, H), jnp.float32), 'router_w': jax.random.uniform(ks[1], (H, E), jnp.float32, -s_h, s_h), 'w1': jax.random.uniform(ks[2], (E, H, F), jnp.float32, -s_h, s_h), 'b1': jax.random.uniform(ks[3], (E, F), jnp.float32, -s_h, s_h), 'w2': jax.random.uniform(ks[4], (E, F, H), jnp.float32, -s_f, s_f), 'b2': jax.random.uniform(ks[5], (E, H), jnp.float32, -s_f, s_f), 'sw1': jax.random.uniform(ks[6], (H, F), jnp.float32, -s_h, s_h), 'sb1': jax.random.uniform(ks[7], (F,), jnp.float32, -s_h, s_h), 'sw2': jax.random.uniform(ks[8], (F, H), jnp.float32, -s_f, s_f), 'sb2': jax.random.uniform(ks[9], (H,), jnp.float32, -s_f, s_f)}
    _L0_ffn_in = _L0_ffn_setup()

    def _L1_attn_setup():
        import jax, jax.numpy as jnp
        import numpy as np
        D_MODEL = 128
        D_STATE = 16
        D_CONV = 4
        EXPAND = 2
        D_INNER = EXPAND * D_MODEL
        DT_RANK = (D_MODEL + 15) // 16
        BATCH = 2
        SEQLEN = 256
        key = jax.random.key(seed)
        ks = jax.random.split(key, 8)
        s = lambda k, shape, scale: jax.random.normal(k, shape, dtype=jnp.float32) * scale
        return {'x': s(ks[0], (BATCH, SEQLEN, D_MODEL), 1.0), 'W_in': s(ks[1], (D_MODEL, 2 * D_INNER), D_MODEL ** (-0.5)), 'conv_w': s(ks[2], (D_INNER, 1, D_CONV), 0.3), 'conv_b': jnp.zeros((D_INNER,), dtype=jnp.float32), 'W_x': s(ks[3], (D_INNER, DT_RANK + 2 * D_STATE), D_INNER ** (-0.5)), 'W_dt': s(ks[4], (DT_RANK, D_INNER), 2.0 * DT_RANK ** (-0.5)), 'b_dt': s(ks[5], (D_INNER,), 0.1), 'A_log': jnp.log(jnp.tile(jnp.arange(1, D_STATE + 1, dtype=jnp.float32), (D_INNER, 1))), 'D': jnp.ones((D_INNER,), dtype=jnp.float32), 'W_out': s(ks[6], (D_INNER, D_MODEL), D_INNER ** (-0.5))}
    _L1_attn_in = _L1_attn_setup()

    def _L1_ffn_setup():
        import jax, jax.numpy as jnp
        import numpy as np
        B, S, DIM = (4, 512, 128)
        BASE_COUPLING = 0.1
        NUM_CYCLES = 3

        def _gelu(x):
            return jax.nn.gelu(x, approximate=False)

        def _coupling_net(h, w1, b1, w2, b2, w3, b3, w4, b4):
            h = _gelu(h @ w1 + b1)
            h = _gelu(h @ w2 + b2)
            h = _gelu(h @ w3 + b3)
            return jax.nn.sigmoid(h @ w4 + b4)

        def _global_net(h, w1, b1, w2, b2, w3, b3):
            h = _gelu(h @ w1 + b1)
            h = _gelu(h @ w2 + b2)
            return jax.nn.sigmoid(h @ w3 + b3)

        def _twist(x):
            o_r, o_i, p_r, p_i = jnp.split(x, 4, axis=-1)
            return jnp.concatenate([p_r, -p_i, -o_r, o_i], axis=-1)
        key = jax.random.key(seed)
        ks = jax.random.split(key, 9)
        d = DIM

        def w(k, fan_in, fan_out):
            return jax.random.normal(k, (fan_in, fan_out), dtype=jnp.float32) / np.sqrt(fan_in).astype(np.float32)
        inp = {'x': jax.random.normal(ks[0], (B, S, d), dtype=jnp.float32)}
        cn_dims = [(d, d), (d, d // 2), (d // 2, d // 4), (d // 4, 1)]
        for i, (a, b) in enumerate(cn_dims):
            inp[f'cn_w{i + 1}'] = w(ks[1 + i], a, b)
            inp[f'cn_b{i + 1}'] = jnp.zeros((b,), dtype=jnp.float32)
        gc_dims = [(d, d // 2), (d // 2, d // 4), (d // 4, 1)]
        for i, (a, b) in enumerate(gc_dims):
            inp[f'gc_w{i + 1}'] = w(ks[5 + i], a, b)
            inp[f'gc_b{i + 1}'] = jnp.zeros((b,), dtype=jnp.float32)
        inp['adaptive_range'] = jnp.full((1,), 0.2, dtype=jnp.float32)
        return inp
    _L1_ffn_in = _L1_ffn_setup()
    _d = {'L0_attn_x': _L0_attn_in['x'], 'L0_attn_basis_q': _L0_attn_in['basis_q'], 'L0_attn_phase_q': _L0_attn_in['phase_q'], 'L0_attn_amp_q': _L0_attn_in['amp_q'], 'L0_attn_basis_k': _L0_attn_in['basis_k'], 'L0_attn_phase_k': _L0_attn_in['phase_k'], 'L0_attn_amp_k': _L0_attn_in['amp_k'], 'L0_attn_basis_v': _L0_attn_in['basis_v'], 'L0_attn_phase_v': _L0_attn_in['phase_v'], 'L0_attn_amp_v': _L0_attn_in['amp_v'], 'L0_attn_basis_o': _L0_attn_in['basis_o'], 'L0_attn_phase_o': _L0_attn_in['phase_o'], 'L0_attn_amp_o': _L0_attn_in['amp_o'], 'L0_ffn_router_w': _L0_ffn_in['router_w'], 'L0_ffn_w1': _L0_ffn_in['w1'], 'L0_ffn_b1': _L0_ffn_in['b1'], 'L0_ffn_w2': _L0_ffn_in['w2'], 'L0_ffn_b2': _L0_ffn_in['b2'], 'L0_ffn_sw1': _L0_ffn_in['sw1'], 'L0_ffn_sb1': _L0_ffn_in['sb1'], 'L0_ffn_sw2': _L0_ffn_in['sw2'], 'L0_ffn_sb2': _L0_ffn_in['sb2'], 'L1_attn_W_in': _L1_attn_in['W_in'], 'L1_attn_conv_w': _L1_attn_in['conv_w'], 'L1_attn_conv_b': _L1_attn_in['conv_b'], 'L1_attn_W_x': _L1_attn_in['W_x'], 'L1_attn_W_dt': _L1_attn_in['W_dt'], 'L1_attn_b_dt': _L1_attn_in['b_dt'], 'L1_attn_A_log': _L1_attn_in['A_log'], 'L1_attn_D': _L1_attn_in['D'], 'L1_attn_W_out': _L1_attn_in['W_out'], 'L1_ffn_cn_w1': _L1_ffn_in['cn_w1'], 'L1_ffn_cn_b1': _L1_ffn_in['cn_b1'], 'L1_ffn_cn_w2': _L1_ffn_in['cn_w2'], 'L1_ffn_cn_b2': _L1_ffn_in['cn_b2'], 'L1_ffn_cn_w3': _L1_ffn_in['cn_w3'], 'L1_ffn_cn_b3': _L1_ffn_in['cn_b3'], 'L1_ffn_cn_w4': _L1_ffn_in['cn_w4'], 'L1_ffn_cn_b4': _L1_ffn_in['cn_b4'], 'L1_ffn_gc_w1': _L1_ffn_in['gc_w1'], 'L1_ffn_gc_b1': _L1_ffn_in['gc_b1'], 'L1_ffn_gc_w2': _L1_ffn_in['gc_w2'], 'L1_ffn_gc_b2': _L1_ffn_in['gc_b2'], 'L1_ffn_gc_w3': _L1_ffn_in['gc_w3'], 'L1_ffn_gc_b3': _L1_ffn_in['gc_b3'], 'L1_ffn_adaptive_range': _L1_ffn_in['adaptive_range']}
    _x0 = _d['L0_attn_x']
    _d['L0_attn_x'] = jax.random.normal(jax.random.fold_in(jax.random.key(seed), 1), (2, 1024, 128), dtype=_x0.dtype)
    del _x0
    return _d

def reference(L0_attn_x, L0_attn_basis_q, L0_attn_phase_q, L0_attn_amp_q, L0_attn_basis_k, L0_attn_phase_k, L0_attn_amp_k, L0_attn_basis_v, L0_attn_phase_v, L0_attn_amp_v, L0_attn_basis_o, L0_attn_phase_o, L0_attn_amp_o, L0_ffn_router_w, L0_ffn_w1, L0_ffn_b1, L0_ffn_w2, L0_ffn_b2, L0_ffn_sw1, L0_ffn_sb1, L0_ffn_sw2, L0_ffn_sb2, L1_attn_W_in, L1_attn_conv_w, L1_attn_conv_b, L1_attn_W_x, L1_attn_W_dt, L1_attn_b_dt, L1_attn_A_log, L1_attn_D, L1_attn_W_out, L1_ffn_cn_w1, L1_ffn_cn_b1, L1_ffn_cn_w2, L1_ffn_cn_b2, L1_ffn_cn_w3, L1_ffn_cn_b3, L1_ffn_cn_w4, L1_ffn_cn_b4, L1_ffn_gc_w1, L1_ffn_gc_b1, L1_ffn_gc_w2, L1_ffn_gc_b2, L1_ffn_gc_w3, L1_ffn_gc_b3, L1_ffn_adaptive_range):

    def _L0_attn_ref(x, basis_q, phase_q, amp_q, basis_k, phase_k, amp_k, basis_v, phase_v, amp_v, basis_o, phase_o, amp_o):
        import jax, jax.numpy as jnp
        import numpy as np
        NUM_HEADS = 16
        DIM = 128
        HARMONICS = 32
        B, L = (2, 256)

        def holo_linear(x, basis, phase, amp):
            resonance = jnp.einsum('bli,hi->blh', x, basis)
            w = amp * jnp.cos(phase)
            return jnp.einsum('blh,oh->blo', resonance, w)
        Bsz, Ls, C = x.shape
        head_dim = C // NUM_HEADS
        scale = head_dim ** (-0.5)

        def split_heads(t):
            return t.reshape(Bsz, Ls, NUM_HEADS, head_dim).transpose(0, 2, 1, 3)
        q = split_heads(holo_linear(x, basis_q, phase_q, amp_q))
        k = split_heads(holo_linear(x, basis_k, phase_k, amp_k))
        v = split_heads(holo_linear(x, basis_v, phase_v, amp_v))
        attn = jnp.einsum('bhqd,bhkd->bhqk', q, k) * scale
        attn = jax.nn.softmax(attn, axis=-1)
        out = jnp.einsum('bhqk,bhkd->bhqd', attn, v)
        out = out.transpose(0, 2, 1, 3).reshape(Bsz, Ls, C)
        return holo_linear(out, basis_o, phase_o, amp_o)

    def _L0_ffn_ref(hidden_states, router_w, w1, b1, w2, b2, sw1, sb1, sw2, sb2):
        import math
        import jax, jax.numpy as jnp
        import numpy as np
        H = 128
        F = 512
        E = 8
        TOP_K = 2
        CAP_FACTOR = 1.25
        MIN_CAP = 4
        SHARED_SCALE = 0.1

        def _top2_gating(logits, capacity):
            N, nE = logits.shape
            gates = jax.nn.softmax(logits, axis=-1)
            idx1 = jnp.argmax(gates, axis=-1)
            mask1 = jax.nn.one_hot(idx1, nE, dtype=gates.dtype)
            idx2 = jnp.argmax(gates * (1.0 - mask1), axis=-1)
            mask2 = jax.nn.one_hot(idx2, nE, dtype=gates.dtype)
            pos1 = jnp.cumsum(mask1, axis=0) - mask1
            mask1 = mask1 * (pos1 < capacity)
            pos2 = jnp.cumsum(mask2, axis=0) - mask2 + jnp.sum(mask1, axis=0, keepdims=True)
            mask2 = mask2 * (pos2 < capacity)
            g1 = jnp.sum(gates * mask1, axis=-1)
            g2 = jnp.sum(gates * mask2, axis=-1)
            denom = jnp.maximum(g1 + g2, jnp.finfo(gates.dtype).eps)
            g1, g2 = (g1 / denom, g2 / denom)
            loc1 = jnp.sum(pos1 * mask1, axis=-1).astype(jnp.int32)
            loc2 = jnp.sum(pos2 * mask2, axis=-1).astype(jnp.int32)
            oh1 = jax.nn.one_hot(loc1, capacity, dtype=gates.dtype)
            oh2 = jax.nn.one_hot(loc2, capacity, dtype=gates.dtype)
            combine = (g1[:, None] * mask1)[:, :, None] * oh1[:, None, :] + (g2[:, None] * mask2)[:, :, None] * oh2[:, None, :]
            dispatch = (combine > 0).astype(gates.dtype)
            return (combine, dispatch)
        B, S, h = hidden_states.shape
        x = hidden_states.reshape(-1, h)
        N = x.shape[0]
        capacity = min(max(MIN_CAP, math.ceil(TOP_K * CAP_FACTOR * N / E)), N)
        logits = x @ router_w
        combine, dispatch = _top2_gating(logits, capacity)
        expert_in = jnp.einsum('nec,nh->ech', dispatch, x)
        hmid = jax.nn.silu(jnp.einsum('ech,ehf->ecf', expert_in, w1) + b1[:, None, :])
        expert_out = jnp.einsum('ecf,efh->ech', hmid, w2) + b2[:, None, :]
        y = jnp.einsum('nec,ech->nh', combine, expert_out)
        shared = jax.nn.silu(x @ sw1 + sb1) @ sw2 + sb2
        out = y + SHARED_SCALE * shared
        return out.reshape(B, S, h)

    def _L1_attn_ref(x, W_in, conv_w, conv_b, W_x, W_dt, b_dt, A_log, D, W_out):
        import jax, jax.numpy as jnp
        import numpy as np
        D_MODEL = 128
        D_STATE = 16
        D_CONV = 4
        EXPAND = 2
        D_INNER = EXPAND * D_MODEL
        DT_RANK = (D_MODEL + 15) // 16
        BATCH = 2
        SEQLEN = 256
        dt_rank = W_dt.shape[0]
        d_state = A_log.shape[1]
        Bsz, L, _ = x.shape
        d_inner = conv_w.shape[0]
        xr = x @ W_in
        xi, res = jnp.split(xr, 2, axis=-1)
        xc = jax.lax.conv_general_dilated(xi.transpose(0, 2, 1), conv_w, window_strides=(1,), padding=[(conv_w.shape[-1] - 1, 0)], feature_group_count=d_inner) + conv_b[None, :, None]
        u = jax.nn.silu(xc.transpose(0, 2, 1))
        dbc = u @ W_x
        delta_r = dbc[..., :dt_rank]
        Bm = dbc[..., dt_rank:dt_rank + d_state]
        Cm = dbc[..., dt_rank + d_state:]
        delta = jax.nn.softplus(delta_r @ W_dt + b_dt)
        A = -jnp.exp(A_log)
        deltaA = jnp.exp(delta[..., None] * A)
        dBu = delta[..., None] * Bm[:, :, None, :] * u[..., None]

        def step(h, inp):
            dA_t, dBu_t, C_t = inp
            h = dA_t * h + dBu_t
            y_t = jnp.einsum('bdn,bn->bd', h, C_t)
            return (h, y_t)
        h0 = jnp.zeros((Bsz, d_inner, d_state), dtype=x.dtype)
        _, ys = jax.lax.scan(step, h0, (deltaA.transpose(1, 0, 2, 3), dBu.transpose(1, 0, 2, 3), Cm.transpose(1, 0, 2)))
        y = ys.transpose(1, 0, 2) + u * D
        y = y * jax.nn.silu(res)
        return y @ W_out

    def _L1_ffn_ref(x, cn_w1, cn_b1, cn_w2, cn_b2, cn_w3, cn_b3, cn_w4, cn_b4, gc_w1, gc_b1, gc_w2, gc_b2, gc_w3, gc_b3, adaptive_range):
        import jax, jax.numpy as jnp
        import numpy as np
        B, S, DIM = (4, 512, 128)
        BASE_COUPLING = 0.1
        NUM_CYCLES = 3

        def _gelu(x):
            return jax.nn.gelu(x, approximate=False)

        def _coupling_net(h, w1, b1, w2, b2, w3, b3, w4, b4):
            h = _gelu(h @ w1 + b1)
            h = _gelu(h @ w2 + b2)
            h = _gelu(h @ w3 + b3)
            return jax.nn.sigmoid(h @ w4 + b4)

        def _global_net(h, w1, b1, w2, b2, w3, b3):
            h = _gelu(h @ w1 + b1)
            h = _gelu(h @ w2 + b2)
            return jax.nn.sigmoid(h @ w3 + b3)

        def _twist(x):
            o_r, o_i, p_r, p_i = jnp.split(x, 4, axis=-1)
            return jnp.concatenate([p_r, -p_i, -o_r, o_i], axis=-1)
        global_context = x.mean(axis=1, keepdims=True)
        gf = _global_net(global_context, gc_w1, gc_b1, gc_w2, gc_b2, gc_w3, gc_b3)
        out = x
        for _ in range(NUM_CYCLES):
            tf = _coupling_net(out, cn_w1, cn_b1, cn_w2, cn_b2, cn_w3, cn_b3, cn_w4, cn_b4)
            combined = 0.7 * gf + 0.3 * tf
            coupling = BASE_COUPLING + adaptive_range * (combined - 0.5) * 2.0
            out = out + coupling * _twist(out)
        return out
    x = L0_attn_x
    x = _layernorm(x + _L0_attn_ref(x, L0_attn_basis_q, L0_attn_phase_q, L0_attn_amp_q, L0_attn_basis_k, L0_attn_phase_k, L0_attn_amp_k, L0_attn_basis_v, L0_attn_phase_v, L0_attn_amp_v, L0_attn_basis_o, L0_attn_phase_o, L0_attn_amp_o), axis=-1)
    x = _layernorm(x + _L0_ffn_ref(x, L0_ffn_router_w, L0_ffn_w1, L0_ffn_b1, L0_ffn_w2, L0_ffn_b2, L0_ffn_sw1, L0_ffn_sb1, L0_ffn_sw2, L0_ffn_sb2), axis=-1)
    x = _layernorm(x + _L1_attn_ref(x, L1_attn_W_in, L1_attn_conv_w, L1_attn_conv_b, L1_attn_W_x, L1_attn_W_dt, L1_attn_b_dt, L1_attn_A_log, L1_attn_D, L1_attn_W_out), axis=-1)
    x = _layernorm(x + _L1_ffn_ref(x, L1_ffn_cn_w1, L1_ffn_cn_b1, L1_ffn_cn_w2, L1_ffn_cn_b2, L1_ffn_cn_w3, L1_ffn_cn_b3, L1_ffn_cn_w4, L1_ffn_cn_b4, L1_ffn_gc_w1, L1_ffn_gc_b1, L1_ffn_gc_w2, L1_ffn_gc_b2, L1_ffn_gc_w3, L1_ffn_gc_b3, L1_ffn_adaptive_range), axis=-1)
    return x

_drawn_inputs = setup_inputs


def setup_inputs(seed=0):
    import zlib

    import numpy as np

    out = dict(_drawn_inputs(seed))
    spreads = {'L0_attn_amp_q': (0.03125, 0.6),
     'L0_attn_amp_k': (0.03125, 0.6),
     'L0_attn_amp_v': (0.03125, 0.6),
     'L0_attn_amp_o': (0.03125, 0.6),
     'L1_attn_conv_b': (0.0, 0.1),
     'L1_attn_D': (1.0, 0.2),
     'L1_ffn_cn_b1': (0.0, 0.8),
     'L1_ffn_cn_b2': (0.0, 2.0),
     'L1_ffn_cn_b3': (0.0, 2.0),
     'L1_ffn_gc_b1': (0.0, 2.0),
     'L1_ffn_gc_b2': (0.0, 2.0)}
    factors = {'L0_attn_basis_q': 8.0,
     'L0_attn_phase_q': 8.0,
     'L0_attn_basis_k': 8.0,
     'L0_attn_phase_k': 8.0,
     'L0_attn_basis_v': 8.0,
     'L0_attn_phase_v': 8.0,
     'L0_attn_basis_o': 8.0,
     'L0_attn_phase_o': 8.0,
     'L0_ffn_b1': 4.491,
     'L0_ffn_b2': 2.975,
     'L0_ffn_sw1': 3.165,
     'L0_ffn_sb1': 8.0,
     'L0_ffn_sw2': 3.03,
     'L0_ffn_sb2': 8.0,
     'L1_attn_b_dt': 8.0,
     'L1_attn_A_log': 33.997,
     'L1_ffn_cn_w1': 7.53,
     'L1_ffn_cn_w2': 5.926,
     'L1_ffn_cn_w3': 5.948,
     'L1_ffn_cn_w4': 5.553,
     'L1_ffn_gc_w1': 8.0,
     'L1_ffn_gc_w2': 64.0,
     'L1_ffn_gc_w3': 64.0}
    for name, (base, spread) in spreads.items():
        noise = np.random.default_rng([zlib.crc32(name.encode()), seed]).standard_normal(out[name].shape)
        drawn = base * np.exp(spread * noise) if base else spread * noise
        out[name] = jnp.asarray(drawn.astype(out[name].dtype))
    for name, factor in factors.items():
        out[name] = (out[name] * factor).astype(out[name].dtype)
    return out
```

```python
from contextlib import ExitStack

import concourse.bass as bass
from concourse import mybir

F32 = mybir.dt.float32
BF16 = mybir.dt.bfloat16
I32 = mybir.dt.int32
U32 = mybir.dt.uint32
ALU = mybir.AluOpType
ACT = mybir.ActivationFunctionType
AX = mybir.AxisListType.X

P = 128
B, L, C = 2, 1024, 128
NTOK = B * L
NT = NTOK // P
CH = 512
NCH = NTOK // CH
HEADS, HD, HARM = 16, 8, 32
UNITS = B * HEADS
KT = L // P
SCALE = HD ** -0.5
EPS = 1e-5
TWO_PI = 6.283185307179586
PI_HI = 6.28125
PI_MID = 0.0019350051879882812
PI_LO = TWO_PI - PI_HI - PI_MID
ROUND = 12582912.0
EXP, FF, CAP = 8, 512, 640
FT, ST = FF // P, CAP // P
SLOTS = EXP * CAP
SHARED_SCALE = 0.1
EXP_FLOOR = -87.3
GATE_EPS = 1.1920929e-07
DIN, ST_N, TAPS, RANK = 256, 16, 4, 8
DT = DIN // P
CREDIT = 4
LOG_RATE_MAX = 80.0
CYCLES = 3
CN_DIMS = ((P, P), (P, P // 2), (P // 2, P // 4), (P // 4, 1))
ARENA = 31 * 1024
B1_ROW, SB1_ROW, CONVB_ROW, BDT_ROW, D_ROW, CNB1_ROW, BROWS = 0, 32, 36, 38, 40, 42, 43
NPROB = 4
ITEMS, T_AT = 17, 4
MAXT_READ = 16 + T_AT + 1
LAST_READ = 16 + ITEMS + ITEMS * (UNITS - 2) + 1


class Chain:

    def __init__(self, eng, sem):
        self.eng, self.sem, self.n = eng, sem, 0

    def __call__(self, ins):
        self.mark(ins)
        self.wait()

    def mark(self, ins):
        ins.then_inc(self.sem, 1)
        self.n += 1
        return ins

    def wait(self):
        self.eng.wait_ge(self.sem, self.n)


def build(nc, a, out):
    ctx = ExitStack()
    with ctx:
        def sb(name, shape, dt=F32):
            return ctx.enter_context(nc.sbuf_tensor(name, shape, dt))

        def sem(name):
            return ctx.enter_context(nc.semaphore(name))

        def dram(name, shape, dt=F32):
            return nc.dram_tensor(name, shape, dt, kind="Internal").ap()

        pair = [ctx.enter_context(nc.psum_tensor(f"pair{i}", [P, 2 * CH], F32)) for i in range(4)]
        bank = [pair[i // 2][:, (i % 2) * CH:(i % 2 + 1) * CH] for i in range(8)]
        ring_bank, pv_bank, st_pair = bank[0:2], bank[2:4], pair[2:4]

        q_parts_d = dram("q_parts_d", [UNITS, 3, HD, L], BF16)
        k_parts_d = dram("k_parts_d", [UNITS, 3, HD, L], BF16)
        head_out_d = dram("head_out_d", [UNITS, 2, HD + 1, L])

        slot_x_d = dram("slot_x_d", [SLOTS + NTOK, C])
        slot_y_d = dram("slot_y_d", [SLOTS, C])

        brow = sb("brow", [BROWS, P])
        biasT = sb("biasT", [P, BROWS])
        zero = sb("zero", [P, 1280])
        ident = sb("ident", [P, P])
        ident_b = sb("ident_b", [P, P], BF16)
        xres = sb("xres", [P, NT, C])
        xT = sb("xT", [P, NTOK])
        wph = sb("wph", [P, 4, HARM])
        wam = sb("wam", [P, 4, HARM])
        wtmp = sb("wtmp", [P, 3, P])
        basis = sb("basis", [P, C])
        wcosT = sb("wcosT", [P, P])
        weff = sb("weff", [P, 4, C])
        expand = sb("expand", [HEADS, P])
        AR = sb("arena", [P, ARENA])
        used = [0]

        def ar(nfloat):
            at = used[0]
            used[0] += nfloat
            assert used[0] <= ARENA, used[0]
            return AR[:, at:at + nfloat]

        q_split = ar(3 * NTOK // 2).bitcast(BF16).rearrange("p (a n) -> p a n", a=3)
        k_split = ar(3 * NTOK // 2).bitcast(BF16).rearrange("p (a n) -> p a n", a=3)
        resid = ar(NTOK).rearrange("p (c n) -> p c n", c=4)
        vtok = ar(NT * HEADS * HD).rearrange("p (b h k d) -> p b h k d", b=B, h=HEADS, k=KT)
        qbuf = ar(4 * L // 2).bitcast(BF16).rearrange("p (s n) -> p s n", s=4)
        kbuf = ar(4 * L // 2).bitcast(BF16).rearrange("p (s n) -> p s n", s=4)
        probs = ar(NPROB * L).rearrange("p (s n) -> p s n", s=NPROB)
        vst = ar(2 * KT * 32).rearrange("p (s k m) -> p s k m", s=2, k=KT)
        pvs = ar(2 * CH).rearrange("p (s n) -> p s n", s=2)
        mx = ar(2 * 16).rearrange("p (s t h) -> p s t h", s=2, t=KT)
        rowmax = ar(2 * 8).rearrange("p (s n) -> p s n", s=2)
        neg1 = ar(8)
        mneg = ar(4 * 8).rearrange("p (s n) -> p s n", s=4)
        mparts = ar(2 * 12).bitcast(BF16).rearrange("p (s n) -> p s n", s=2)
        mT = ar(2 * 64).bitcast(BF16).rearrange("p (s n) -> p s n", s=2)
        used[0] = 0
        o_par = ar(2 * NTOK).rearrange("p (s n) -> p s n", s=2)
        den = ar(2 * NTOK).rearrange("p (s n) -> p s n", s=2)
        onorm = ar(NTOK)

        used[0] = 7 * NTOK
        acc = ar(NTOK).rearrange("p (t c) -> p t c", t=NT)
        picked = ar(2 * NTOK).rearrange("p (w t c) -> p w t c", w=2, t=NT)
        used[0] = 0
        w1r = ar(2 * FF).rearrange("p (s f) -> p s f", s=2)
        w2r = ar(2 * FT * C).rearrange("p (s f c) -> p s f c", s=2, f=FT)
        xer = ar(2 * ST * C).rearrange("p (s t c) -> p s t c", s=2, t=ST)
        xeT = ar(2 * CAP).rearrange("p (s n) -> p s n", s=2)
        hT = ar(FT * CAP).rearrange("p (f n) -> p f n", f=FT)
        yer = ar(2 * ST * C).rearrange("p (s t c) -> p s t c", s=2, t=ST)
        hsT = ar(2 * FT * CH).rearrange("p (s f n) -> p s f n", s=2, f=FT)
        sw1 = sb("sw1", [P, FF])
        sw2 = sb("sw2", [P, FT, C])
        sb2 = sb("sb2", [P, C])
        b2all = sb("b2all", [P, EXP, C])
        rw = sb("rw", [P, EXP])
        before = sb("before", [P, P], BF16)
        ones_b = sb("ones_b", [P, P], BF16)
        rank = sb("rank", [P, EXP, NT])
        first = sb("first", [P, 2, EXP, NT])
        carry = sb("carry", [P, 2 * EXP * NT])
        spill = sb("spill", [P, 2, NT])
        R = {n: sb("r_" + n, [P, EXP, NT]) for n in ("lg", "ls", "ex", "gates", "t1", "t2")}
        RW = {n: sb("rw_" + n, [P, 2, EXP, NT]) for n in ("mask", "incl", "pos", "keep", "t")}
        mask_b = sb("mask_b", [P, 2, EXP, NT], BF16)
        rt = sb("rt", [P, 6, NT])
        rt2 = sb("rt2", [P, 6, 2, NT])
        cap1 = sb("cap1", [P, EXP])
        slot_i = sb("slot_i", [P, 2, 2, NT], I32)

        used[0] = 0
        xpad = ar(B * (L + TAPS - 1)).rearrange("p (b n) -> p b n", b=B)
        uu = ar(B * DT * L).rearrange("p (g n) -> p g n", g=B * DT)
        delta = ar(B * DT * L).rearrange("p (g n) -> p g n", g=B * DT)
        du = ar(B * DT * L).rearrange("p (g n) -> p g n", g=B * DT)
        gate = ar(B * DT * L).rearrange("p (g n) -> p g n", g=B * DT)
        bc_parts = ar(NTOK // 2).bitcast(BF16)
        low = xT[:, :]
        ring0 = used[0]
        dA = ar(3 * L).rearrange("p (s n) -> p s n", s=3)
        Bs = ar(2 * L).rearrange("p (s n) -> p s n", s=2)
        dBu = ar(2 * L).rearrange("p (s n) -> p s n", s=2)
        hh = ar(2 * L).rearrange("p (s n) -> p s n", s=2)
        hC = ar(2 * L).rearrange("p (s n) -> p s n", s=2)
        used[0] = ring0
        sp_t = ar(2 * L).rearrange("p (s n) -> p s n", s=2)
        sp_l = ar(2 * L).rearrange("p (s n) -> p s n", s=2)
        sp_r = ar(2 * L).rearrange("p (s n) -> p s n", s=2)
        sp_d = ar(2 * L).rearrange("p (s n) -> p s n", s=2)
        bc_r = ar(NTOK)
        bc_p2 = ar(NTOK // 2).bitcast(BF16)
        used[0] = 0
        m1 = ar(NTOK).rearrange("p (c n) -> p c n", c=NCH)
        m2 = ar(NTOK).rearrange("p (c n) -> p c n", c=NCH)
        m3 = ar(NTOK).rearrange("p (c n) -> p c n", c=NCH)
        tf = ar(NTOK).rearrange("p (c n) -> p c n", c=NCH)
        tw_in = ar(NTOK).rearrange("p (c n) -> p c n", c=NCH)
        cpl = ar(NTOK).rearrange("p (c n) -> p c n", c=NCH)
        prod = ar(NTOK).rearrange("p (c n) -> p c n", c=NCH)
        win = sb("win", [P, 2 * DIN])
        cwb = sb("cwb", [P, DIN * TAPS])
        wconv = sb("wconv", [P, TAPS, DIN])
        wx = sb("wx", [P, DT, RANK + 2 * ST_N])
        wx3 = sb("wx3", [P, DT, 104])
        wdt = sb("wdt", [P, DIN])
        alog = sb("alog", [P, DT, ST_N])
        wout = sb("wout", [P, DT, C])
        sel = sb("sel", [96, 2 * ST_N, P], BF16)
        cw = [sb(f"cw{j}", sh) for j, sh in ((1, [P, P]), (2, [P, P]), (3, [P, P]), (4, [P, 1]))]
        cb2, cb3, cb4 = sb("cb2", [P, 1]), sb("cb3", [P, 1]), sb("cb4", [P, 1])
        gw = [sb(f"gw{j}", sh) for j, sh in ((1, [P, 64]), (2, [64, 32]), (3, [32, 1]))]
        gb1, gb2, gb3 = sb("gb1", [64, 1]), sb("gb2", [32, 1]), sb("gb3", [P, 1])
        w4b, gw3b = sb("w4b", [P, P]), sb("gw3b", [32, P])
        rng = sb("rng", [P, 1])
        sgn = sb("sgn", [P, 1])
        gmean = sb("gmean", [P, 2, B])
        g1, g2, gf = sb("g1", [64, B]), sb("g2", [32, B]), sb("gf", [P, B])
        c_in = sb("c_in", [P, 4, B])

        ln_stats = sb("ln_stats", [P, NT, 6])
        lnv = sb("lnv", [P, NT, 2])

        S = {}

        def s_(name):
            if name not in S:
                S[name] = sem(name)
            return S[name]

        def ln_start(dve, v, ch, t0, n):
            for t in range(t0, t0 + n):
                ch.mark(v.bn_stats(ln_stats[:, t, :], xres[:, t, :]))
            ch.wait()
            for t in range(t0, t0 + n):
                ch.mark(v.bn_aggr(lnv[:, t, :], ln_stats[:, t, :]))
            ch.wait()
            v.tensor_scalar(lnv[:, t0:t0 + n, 1], lnv[:, t0:t0 + n, 1], EPS, None, ALU.add).then_inc(s_("ln_var"), 1)

        def ln_end(dve, v, ch, t0, n, count, ready):
            dve.wait_ge(s_("ln_sqrt"), count)
            ch(v.reciprocal(lnv[:, t0:t0 + n, 1], lnv[:, t0:t0 + n, 1]))
            for t in range(t0, t0 + n):
                last = v.tensor_scalar(xres[:, t, :], xres[:, t, :], lnv[:, t, 0:1], lnv[:, t, 1:2], ALU.subtract, ALU.mult)
                last.then_inc(s_(ready), 1)

        block = ctx.enter_context(nc.Block())

        @block.sync
        def _(sp):
            for b in range(B):
                sp.dma_start(xres[:, b * 8:b * 8 + 8, :],
                             a["L0_attn_x"][b].rearrange("(t p) c -> p t c", p=P)).then_inc(s_("x_loaded"), 16)
            for j, n in enumerate("qkvo"):
                sp.dma_start(wph[:, j, :], a[f"L0_attn_phase_{n}"]).then_inc(s_("rot_loaded"), 16)
                sp.dma_start(wam[:, j, :], a[f"L0_attn_amp_{n}"]).then_inc(s_("rot_loaded"), 16)
                sp.dma_start(basis[32 * j:32 * j + 32, :], a[f"L0_attn_basis_{n}"]).then_inc(s_("rot_loaded"), 16)
            for row, n, src in ((B1_ROW, 32, a["L0_ffn_b1"].rearrange("e (f p) -> (e f) p", p=P)),
                                (SB1_ROW, 4, a["L0_ffn_sb1"].rearrange("(f p) -> f p", p=P)),
                                (CONVB_ROW, 2, a["L1_attn_conv_b"].rearrange("(f p) -> f p", p=P)),
                                (BDT_ROW, 2, a["L1_attn_b_dt"].rearrange("(f p) -> f p", p=P)),
                                (D_ROW, 2, a["L1_attn_D"].rearrange("(f p) -> f p", p=P)),
                                (CNB1_ROW, 1, a["L1_ffn_cn_b1"].rearrange("(f p) -> f p", p=P))):
                sp.dma_start(brow[row:row + n, :], src).then_inc(s_("brow_loaded"), 16)
            for b in range(B):
                for which, (split, dst) in enumerate(((q_split, q_parts_d), (k_split, k_parts_d))):
                    sp.wait_ge(s_("split_done"), 4 * b + 2 * which + 2)
                    for part in range(3):
                        sp.dma_start(dst[b * HEADS:(b + 1) * HEADS, part],
                                     split[:, part, b * L:(b + 1) * L]).then_inc(s_("parts_stored"), 16)
            sp.wait_ge(s_("zero_ready"), 1)
            for k in range(4):
                sp.dma_start(slot_x_d[k * 1280:(k + 1) * 1280, :].rearrange("(p r) c -> p (r c)", p=P), zero[:, :])\
                    .then_inc(s_("slots_zeroed"), 16)
            sp.dma_start(sw1[:, :], a["L0_ffn_sw1"]).then_inc(s_("ffn_loaded"), 16)
            sp.dma_start(sw2[:, :, :], a["L0_ffn_sw2"].rearrange("(f p) c -> p f c", p=P)).then_inc(s_("ffn_loaded"), 16)
            sp.dma_start(sb2[:, :], bass.AP(tensor=a["L0_ffn_sb2"].tensor, offset=0, ap=[[0, P], [1, C]]))\
                .then_inc(s_("ffn_loaded"), 16)
            sp.dma_start(b2all[:, :, :], bass.AP(tensor=a["L0_ffn_b2"].tensor, offset=0, ap=[[0, P], [C, EXP], [1, C]]))\
                .then_inc(s_("ffn_loaded"), 16)
            sp.dma_start(rw[:, :], a["L0_ffn_router_w"]).then_inc(s_("ffn_loaded"), 16)
            m, f = "L1_attn_", "L1_ffn_"
            for dst, src in ((win[:, :], a[m + "W_in"]),
                             (cwb[:, :], bass.AP(tensor=a[m + "conv_w"].tensor, offset=0, ap=[[0, P], [1, DIN * TAPS]])),
                             (wx[:, :, :], a[m + "W_x"].rearrange("(t p) c -> p t c", p=P)),
                             (wdt[96:96 + RANK, :], a[m + "W_dt"]),
                             (alog[:, :, :], a[m + "A_log"].rearrange("(t p) c -> p t c", p=P)),
                             (wout[:, :, :], a[m + "W_out"].rearrange("(t p) c -> p t c", p=P))):
                sp.dma_start(dst, src).then_inc(s_("mixer_loaded"), 16)

            def column(t):
                return t.rearrange("(p o) -> p o", o=1)

            def everywhere(t):
                return bass.AP(tensor=t.tensor, offset=0, ap=[[0, P], [1, 1]])

            sp.wait_ge(s_("net_cleared"), 1)
            for dst, src in [(cw[j][0:r, 0:w], a[f + f"cn_w{j + 1}"]) for j, (r, w) in enumerate(CN_DIMS)] + \
                    [(gw[j][:, :], a[f + f"gc_w{j + 1}"]) for j in range(3)] + \
                    [(cb2[0:64, :], column(a[f + "cn_b2"])), (cb3[0:32, :], column(a[f + "cn_b3"])),
                     (gb1[:, :], column(a[f + "gc_b1"])), (gb2[:, :], column(a[f + "gc_b2"])),
                     (cb4[:, :], everywhere(a[f + "cn_b4"])), (gb3[:, :], everywhere(a[f + "gc_b3"])),
                     (rng[:, :], everywhere(a[f + "adaptive_range"]))]:
                sp.dma_start(dst, src).then_inc(s_("net_loaded"), 16)
            sp.wait_ge(s_("parts_stored"), 12 * 16)
            sp.wait_ge(s_("qk_cleared"), 1)

            def load_unit(u, slot):
                for part in range(3):
                    src = bass.AP(tensor=q_parts_d.tensor, offset=(u * 3 + part) * HD * L, ap=[[0, 3], [L, HD], [1, L]])
                    sp.dma_start(qbuf[24 * part:24 * part + 24, slot, :], src).then_inc(s_(f"unit_loaded{slot}"), 16)
                src = bass.AP(tensor=k_parts_d.tensor, offset=u * 3 * HD * L, ap=[[0, 3], [L, 3 * HD], [1, L]])
                sp.dma_start(kbuf[0:72, slot, :], src).then_inc(s_(f"unit_loaded{slot}"), 16)

            def load_max(count, slot, m):
                sp.wait_ge(s_("ring_read"), count)
                for part in range(3):
                    sp.dma_start(qbuf[96 + part:97 + part, slot, :],
                                 mT[8 * part:8 * part + 8, m, :]).then_inc(s_(f"max_loaded{slot}"), 16)

            def store_head(u, s):
                sp.wait_ge(s_("pv_copied"), u + 3)
                for par in range(2):
                    for qh in range(2):
                        g = 2 * par + qh
                        dst = bass.AP(tensor=head_out_d.tensor, offset=((u * 2 + par) * (HD + 1)) * L + qh * CH,
                                      ap=[[L, HD + 1], [1, CH]])
                        sp.dma_start(dst, pvs[32 * g:32 * g + HD + 1, s, :]).then_inc(s_(f"head_stored{s}"), 16)

            for s in range(4):
                sp.sem_inc(s_(f"max_loaded{s}"), 16)
            for s in range(2):
                sp.sem_inc(s_(f"head_stored{s}"), 16)
                sp.sem_inc(s_(f"ye_stored{s}"), 16)
            for u in range(3):
                load_unit(u, u)
            load_max(MAXT_READ, 0, 0)

            def unit(i, s, last):
                u = 4 * i + s
                if not (last and s > 0):
                    sp.wait_ge(s_("st_done"), KT * u + 1)
                    load_unit(u + 3, (s + 3) % 4)
                if not (last and s == 3):
                    load_max(LAST_READ if last and s == 2 else MAXT_READ + ITEMS * (u + 1), (s + 1) % 4, (s + 1) % 2)
                store_head(u, s % 2)

            with sp.Fori(0, UNITS // 4 - 1) as i:
                for s in range(4):
                    unit(i, s, False)
            for s in range(4):
                unit(UNITS // 4 - 1, s, True)
            for s in range(2):
                sp.wait_ge(s_(f"head_stored{s}"), 4 * 16 * UNITS // 2 + 16)
            for b in range(B):
                for par in range(2):
                    src = bass.AP(tensor=head_out_d.tensor, offset=(b * HEADS * 2 + par) * (HD + 1) * L,
                                  ap=[[2 * (HD + 1) * L, HEADS], [L, HD], [1, L]])
                    sp.dma_start(o_par[:, par, b * L:(b + 1) * L], src).then_inc(s_("o_loaded"), 16)
                    src = bass.AP(tensor=head_out_d.tensor, offset=((b * HEADS * 2 + par) * (HD + 1) + HD) * L,
                                  ap=[[2 * (HD + 1) * L, HEADS], [1, L]])
                    sp.dma_start(den[0:HEADS, par, b * L:(b + 1) * L], src).then_inc(s_("o_loaded"), 16)
            def load_weights(e, s):
                sp.dma_start(w1r[:, s, :], bass.AP(tensor=a["L0_ffn_w1"].tensor, offset=e * C * FF, ap=[[FF, C], [1, FF]]))\
                    .then_inc(s_(f"expert_loaded{s}"), 16)
                sp.dma_start(w2r[:, s, :, :], bass.AP(tensor=a["L0_ffn_w2"].tensor, offset=e * FF * C,
                                                      ap=[[C, P], [P * C, FT], [1, C]])).then_inc(s_(f"expert_loaded{s}"), 16)

            def load_slots(e, s):
                sp.dma_start(xer[:, s, :, :], bass.AP(tensor=slot_x_d.tensor, offset=e * CAP * C,
                                                      ap=[[C, P], [P * C, ST], [1, C]])).then_inc(s_(f"slots_loaded{s}"), 16)

            sp.wait_ge(s_("onorm_ready"), 4)
            for e in range(2):
                load_weights(e, e)
            sp.wait_ge(s_("scattered"), 2 * NT * 16)
            for e in range(2):
                load_slots(e, e)

            def expert_io(i, s, last):
                e = 2 * i + s
                if not last:
                    sp.wait_ge(s_("xeT_done"), e + 1)
                    load_slots(e + 2, s)
                sp.wait_ge(s_("ye_ready"), e + 2)
                sp.dma_start(bass.AP(tensor=slot_y_d.tensor, offset=e * CAP * C, ap=[[C, P], [P * C, ST], [1, C]]),
                             yer[:, s, :, :]).then_inc(s_(f"ye_stored{s}"), 16)
                if not last:
                    load_weights(e + 2, s)

            with sp.Fori(0, EXP // 2 - 1) as i:
                for s in range(2):
                    expert_io(i, s, False)
            for s in range(2):
                expert_io(EXP // 2 - 1, s, True)
            def twist(i, c):
                for dst, src in ((0, 64), (32, 96), (64, 0), (96, 32)):
                    sp.dma_start(tw_in[dst:dst + 32, c, :], xT[src:src + 32, c * CH:(c + 1) * CH])\
                        .then_inc(s_(f"twisted{c}"), 16)

            with sp.Fori(0, CYCLES) as i:
                for c in range(NCH):
                    sp.wait_ge(s_("state_ready"), NCH * i + c + 1)
                    twist(i, c)
            for gi in range(4):
                sp.wait_ge(s_("x4_ready"), 4 * gi + 4)
                sp.dma_start(out[gi // 2, (gi % 2) * CH:(gi % 2 + 1) * CH, :].rearrange("(t p) c -> p t c", p=P),
                             xres[:, 4 * gi:4 * gi + 4, :]).then_inc(s_("out_stored"), 16)
            sp.wait_ge(s_("out_stored"), 4 * 16)

        @block.gpsimd
        def _(pool):
            g = nc.gpsimd
            ch = Chain(pool, s_("pool_chain"))
            ch.mark(g.memset(ident[:], 0.0))
            ch.mark(g.memset(ident_b[:], 0.0))
            ch(g.memset(expand[:], 1.0))
            for m in (ident, ident_b):
                g.affine_select(out=m[:], in_=m[:], compare_op=ALU.not_equal, fill=1.0, base=0,
                                pattern=[[-1, P]], channel_multiplier=1).then_inc(s_("ident_ready"), 1)
            ch.mark(g.memset(ones_b[:], 1.0))
            g.memset(zero[:], 0.0).then_inc(s_("zero_ready"), 1)
            ch.wait()
            ch.mark(g.affine_select(out=before[:], in_=ones_b[:], compare_op=ALU.is_gt, fill=0.0, base=0,
                                    pattern=[[1, P]], channel_multiplier=-1))
            ch.mark(g.iota(rank[:], pattern=[[-1, EXP], [0, NT]], base=EXP, channel_multiplier=0,
                           allow_small_or_imprecise_dtypes=True))
            ch.mark(g.iota(first[:], pattern=[[0, 2], [CAP, EXP], [0, NT]], base=0, channel_multiplier=0,
                           allow_small_or_imprecise_dtypes=True))
            ch.mark(g.iota(spill[:], pattern=[[0, 2], [P, NT]], base=SLOTS, channel_multiplier=1,
                           allow_small_or_imprecise_dtypes=True))
            ch(g.memset(carry[:], 1.0))
            ch(g.memset(carry[:, :].rearrange("p (w t) -> p w t", t=NT)[:, :, 0:1], 0.0))
            ch.mark(g.memset(sel[:], 0.0))
            ch.wait()
            for at, value in ((0, 1.0), (32, -1.0), (64, -1.0), (96, 1.0)):
                ch(g.memset(sgn[at:at + 32, :], value))
            for tile in (*cw[1:], cb2, cb3):
                last = ch.mark(g.memset(tile[:, :], 0.0))
            ch.wait()
            pool.sem_inc(s_("net_cleared"), 1)
            for q in range(3):
                ch(g.affine_select(out=sel[:], in_=sel[:], compare_op=ALU.not_equal, fill=1.0, base=-32 * q,
                                   pattern=[[-1, 2 * ST_N], [0, P]], channel_multiplier=1))
            ch(g.affine_select(out=expand[:], in_=expand[:], compare_op=ALU.is_ge, fill=0.0, base=0,
                               pattern=[[1, P]], channel_multiplier=-HD))
            g.affine_select(out=expand[:], in_=expand[:], compare_op=ALU.is_ge, fill=0.0, base=HD - 1,
                            pattern=[[-1, P]], channel_multiplier=HD).then_inc(s_("ident_ready"), 1)
            ch.mark(g.memset(qbuf[64:128, :, :], 0.0))
            ch(g.memset(kbuf[64:96, :, :], 0.0))
            ch(g.memset(kbuf[96:128, :, :], 0.0))
            g.memset(kbuf[96:99, :, :], 1.0).then_inc(s_("qk_cleared"), 1)
            pool.wait_ge(s_("qk_cleared"), 1)
            ch.mark(g.memset(neg1[:, :], -1.0))
            ch(g.memset(vst[:, :, :, :], 0.0))
            ch(g.memset(vst[:, :, :, HD:HD + 1], 1.0))

            def stage_v(u, s):
                src = vtok[:, :, :, :, :].rearrange("p b h k d -> p (b h) k d")
                return g.tensor_copy(vst[:, s, :, 0:HD], src[:, bass.ds(u, 1), :, :].rearrange("p o k d -> p (o k) d"))

            def split_max(v, s, c):
                pool.wait_ge(s_("max_ready"), v + 1)
                c(g.tensor_tensor(mparts[:, s, 0:8], rowmax[:, s, :], neg1[:, :], ALU.mult))
                c(g.tensor_tensor(mneg[:, 1, :], rowmax[:, s, :], mparts[:, s, 0:8], ALU.add))
                c(g.tensor_tensor(mparts[:, s, 8:16], mneg[:, 1, :], neg1[:, :], ALU.mult))
                c(g.tensor_tensor(mneg[:, 2, :], mneg[:, 1, :], mparts[:, s, 8:16], ALU.add))
                g.tensor_tensor(mparts[:, s, 16:24], mneg[:, 2, :], neg1[:, :], ALU.mult)\
                    .then_inc(s_("max_split"), 1)

            pool.wait_ge(s_("v_copied"), 4)
            stage_v(0, 0).then_inc(s_("v_staged"), 1)
            base = ch.n

            class At:
                def __init__(self, start):
                    self.start, self.n = start, 0

                def __call__(self, ins):
                    ins.then_inc(s_("pool_chain"), 1)
                    self.n += 1
                    pool.wait_ge(s_("pool_chain"), self.start + self.n)

            split_max(0, 0, At(base))
            split_max(1, 1, At(base + 4))

            def unit(i, s, last):
                u = 4 * i + s
                if not (last and s == 3):
                    pool.wait_ge(s_("probs_free"), NPROB + KT * u)
                    stage_v(u + 1, (s + 1) % 2).then_inc(s_("v_staged"), 1)
                if not (last and s > 1):
                    pool.wait_ge(s_("ring_full"), MAXT_READ + ITEMS * u)
                    split_max(u + 2, s % 2, At(base + 8 + 4 * u))

            with pool.Fori(0, UNITS // 4 - 1) as i:
                for s in range(4):
                    unit(i, s, False)
            for s in range(4):
                unit(UNITS // 4 - 1, s, True)
            ch.n = base + 4 * UNITS
            pool.wait_ge(s_("onorm_ready"), 4)
            pool.wait_ge(s_("ffn_loaded"), 5 * 16)
            pool.wait_ge(s_("x1_ready"), NT)
            ch(g.tensor_scalar(sb2[:, :], sb2[:, :], SHARED_SCALE, None, ALU.mult))
            g.tensor_tensor(acc[:, :, :], xres[:, :, :], sb2[:, :].unsqueeze(1).to_broadcast([P, NT, C]), ALU.add)\
                .then_inc(s_("acc_ready"), 1)
            pool.wait_ge(s_("slots_zeroed"), 4 * 16)
            pool.wait_ge(s_("slot_ready"), 1)
            for w in range(2):
                for t in range(NT):
                    g.indirect_dma_start(out=slot_x_d[:, :], out_offset=bass.IndirectOffsetOnAxis(ap=slot_i[:, 0, w, t:t + 1], axis=0),
                                         in_=xres[:, t, :], in_offset=None).then_inc(s_("scattered"), 16)
            for s in range(2):
                pool.wait_ge(s_(f"ye_stored{s}"), EXP // 2 * 16 + 16)
            for t in range(NT):
                for w in range(2):
                    g.indirect_dma_start(out=picked[:, w, t, :], out_offset=None, in_=slot_y_d[:, :],
                                         in_offset=bass.IndirectOffsetOnAxis(ap=slot_i[:, 1, w, t:t + 1], axis=0))\
                        .then_inc(s_(f"picked{t // 4}"), 16)

            pool.wait_ge(s_("mixer_loaded"), 6 * 16)
            for k in range(3):
                ch.mark(g.tensor_copy(wx3[:, :, 32 * k:32 * k + 32], wx[:, :, RANK:RANK + 2 * ST_N]))
            g.tensor_copy(wx3[:, :, 96:104], wx[:, :, 0:RANK]).then_inc(s_("wx3_ready"), 1)
            ch.wait()
            pool.wait_ge(s_("wx3_ready"), 1)
            pool.wait_ge(s_("x2T_done"), 4)
            g.memset(xpad[:, :, 0:TAPS - 1], 0.0).then_inc(s_("pad_ready"), 1)
            for q in range(B * DT):
                pool.wait_ge(s_("sp_c"), q + 1)
                ch(g.tensor_tensor(sp_d[:, q % 2, :], sp_t[:, q % 2, :], sp_d[:, q % 2, :], ALU.subtract))
                pool.wait_ge(s_("sp_ln"), q + 1)
                g.tensor_tensor(sp_d[:, q % 2, :], sp_d[:, q % 2, :], sp_l[:, q % 2, :], ALU.add).then_inc(s_("sp_small"), 1)
            pool.wait_ge(s_("sp_small"), B * DT)
            pool.wait_ge(s_("du_ready"), B * DT)
            pool.sem_inc(s_("dBu_ready"), CREDIT)
            with pool.Fori(0, B * DT) as gg:
                for n in range(ST_N):
                    U = CREDIT + ST_N * gg + n + 1
                    pool.wait_ge(s_("b_copied"), U)
                    pool.wait_ge(s_("h_ready"), U - 2)
                    pool.sem_inc(s_("dBu_begun"), 1)
                    g.tensor_tensor(dBu[:, n % 2, :], du[:, bass.ds(gg, 1), :].rearrange("p o n -> p (o n)"), Bs[:, n % 2, :],
                                    ALU.mult).then_inc(s_("dBu_ready"), 1)

        @block.scalar
        def _(act):
            sc = nc.scalar
            ch = Chain(act, s_("act_chain"))
            act.wait_ge(s_("args_ready"), 1)
            sc.activation(wtmp[:, 1, :], wtmp[:, 0, :], ACT.Sin).then_inc(s_("sin_done"), 1)
            for c in range(0, NCH, 2):
                act.wait_ge(s_("xT_done"), c + 1)
                sc.copy(xT[:, c * CH:(c + 1) * CH], bank[c][:, :]).then_inc(s_("xT_copied_a"), 1)
            n = 0
            for b in range(B):
                for w, split in ((0, q_split), (1, k_split)):
                    for c in (2 * b, 2 * b + 1):
                        act.wait_ge(s_("qk_done"), n + 1)
                        sc.copy(split[:, 0, c * CH:(c + 1) * CH], bank[4 * w + c][:, :]).then_inc(s_("part1_done"), 1)
                        act.wait_ge(s_("resid_done"), n + 1)
                        sc.copy(split[:, 1, c * CH:(c + 1) * CH], resid[:, n % 4, :]).then_inc(s_("part2_done"), 1)
                        n += 1
            for c in range(NCH):
                act.wait_ge(s_("v_done"), c + 1)
                b, t0 = c // 2, 4 * (c % 2)
                sc.copy(vtok[:, b, :, t0:t0 + 4, :].rearrange("p h k d -> p k h d"),
                        bank[c][:, :].rearrange("p (k h d) -> p k h d", k=4, h=HEADS)).then_inc(s_("v_copied"), 1)

            def exps(G, kt, w):
                act.wait_ge(s_("st_done"), G + 2)
                act.wait_ge(s_("probs_free"), G + 1)
                sc.activation(probs[:, kt % NPROB, :], st_pair[kt % 2][:, :], ACT.Exp, scale=SCALE)\
                    .then_inc(s_("exp_done"), 1)

            act.sem_inc(s_("pv_copied"), 2)
            for G in range(2):
                exps(G, G, 0)

            def unit(i, s, last):
                u = 4 * i + s
                for j in range(KT):
                    if last and s == 3 and j >= KT - 2:
                        continue
                    exps(KT * u + j + 2, j + 2, s)
                act.wait_ge(s_("probs_free"), NPROB + KT * (u + 1))
                act.wait_ge(s_(f"head_stored{s % 2}"), 4 * 16 * (2 * i + s // 2) + 16)
                sc.copy(pvs[:, s % 2, :], pv_bank[s % 2][:, :]).then_inc(s_("pv_copied"), 1)

            with act.Fori(0, UNITS // 4 - 1) as i:
                for s in range(4):
                    unit(i, s, False)
            for s in range(4):
                unit(UNITS // 4 - 1, s, True)

            for gi in range(4):
                act.wait_ge(s_("ln_var"), gi + 1)
                sc.activation(lnv[:, 4 * gi:4 * gi + 4, 1], lnv[:, 4 * gi:4 * gi + 4, 1], ACT.Sqrt).then_inc(s_("ln_sqrt"), 1)

            for c in range(NCH):
                act.wait_ge(s_("x1T_done"), c + 1)
                sc.copy(xT[:, c * CH:(c + 1) * CH], bank[c][:, :]).then_inc(s_("x1T_copied"), 1)
            act.wait_ge(s_("logits_shifted"), 1)
            sc.activation(R["ex"][:, :, :], R["ls"][:, :, :], ACT.Exp).then_inc(s_("gate_exp"), 1)
            for c in range(NCH):
                if c >= 2:
                    act.wait_ge(s_("shared_done"), c - 1)
                for f in range(FT):
                    act.wait_ge(s_("shared_up"), c * FT + f + 1)
                    sc.activation(hsT[:, c % 2, f, :], bank[f][:, :], ACT.Silu, bias=biasT[:, SB1_ROW + f:SB1_ROW + f + 1])\
                        .then_inc(s_("shared_act"), 1)

            def expert_act(i, s):
                e = 2 * i + s
                act.wait_ge(s_("ye_done"), e + 1)
                for f in range(FT):
                    act.wait_ge(s_("up_done"), FT * e + f + 1)
                    sc.activation(hT[:, f, :].rearrange("p (h n) -> p h n", h=2),
                                  pair[1 + f % 2][:, :].rearrange("p (h n) -> p h n", h=2)[:, :, 0:CAP // 2],
                                  ACT.Silu, bias=biasT[:, bass.ds(FT * e + f, 1)]).then_inc(s_("up_act"), 1)

            with act.Fori(0, EXP // 2) as i:
                for s in range(2):
                    expert_act(i, s)
            for gi in range(4):
                act.wait_ge(s_("ln_var"), 4 + gi + 1)
                sc.activation(lnv[:, 4 * gi:4 * gi + 4, 1], lnv[:, 4 * gi:4 * gi + 4, 1], ACT.Sqrt).then_inc(s_("ln_sqrt"), 1)

            act.wait_ge(s_("pad_ready"), 1)
            for c in range(NCH):
                act.wait_ge(s_("x2T_done"), c + 1)
                at = TAPS - 1 + (c % 2) * CH
                sc.copy(xpad[:, c // 2, at:at + CH], bank[c][:, :]).then_inc(s_("x2T_copied"), 1)
            for q in range(B * DT):
                act.wait_ge(s_("conv_done"), q + 1)
                sc.activation(uu[:, q, :], pair[q % 2][:, :], ACT.Silu, bias=biasT[:, CONVB_ROW + q % 2:CONVB_ROW + q % 2 + 1])\
                    .then_inc(s_("u_ready"), 1)
                act.wait_ge(s_("gate_done"), q + 1)
                sc.activation(gate[:, q, :], pair[2 + q % 2][:, :], ACT.Silu).then_inc(s_("gate_ready"), 1)
            act.wait_ge(s_("a_clamped"), 1)
            sc.activation(alog[:, :, :], alog[:, :, :], ACT.Exp).then_inc(s_("a_exp"), 1)
            for b in range(B):
                act.wait_ge(s_("bc_done"), b + 1)
                sl = slice(b * L, (b + 1) * L)
                sc.copy(low[96:96 + RANK, sl], pair[b][96:96 + RANK, :]).then_inc(s_("low_ready"), 1)
                sc.copy(bc_parts[0:96, sl], pair[b][0:96, :]).then_inc(s_("bc_1"), 1)
                act.wait_ge(s_("bc_rest"), b + 1)
                sc.copy(bc_p2[0:96, sl], bc_r[0:96, sl]).then_inc(s_("bc_2"), 1)
            for q in range(B * DT):
                act.wait_ge(s_("delta_done"), q + 1)
                if q >= 2:
                    act.wait_ge(s_("delta_ready"), q - 1)
                bias = biasT[:, BDT_ROW + q % 2:BDT_ROW + q % 2 + 1]
                sc.activation(sp_l[:, q % 2, :], pair[2 + q % 2][:, :], ACT.Abs, bias=bias).then_inc(s_("sp_abs"), 1)
                act.wait_ge(s_("sp_abs"), q + 1)
                sc.activation(sp_t[:, q % 2, :], sp_l[:, q % 2, :], ACT.Exp, scale=-1.0).then_inc(s_("sp_exp"), 1)
                act.wait_ge(s_("sp_exp"), q + 1)
                sc.activation(sp_l[:, q % 2, :], sp_t[:, q % 2, :], ACT.Ln, bias=1.0).then_inc(s_("sp_ln"), 1)
            act.wait_ge(s_("a_ready"), 1)
            act.wait_ge(s_("delta_ready"), B * DT)
            act.wait_ge(s_("bc_ready"), B)
            act.sem_inc(s_("b_copied"), CREDIT)
            act.sem_inc(s_("dA_ready"), CREDIT)
            with act.Fori(0, B) as bb:
                with act.Fori(0, DT) as dd:
                    for n in range(ST_N):
                        U = CREDIT + ST_N * (DT * bb + dd) + n + 1
                        act.wait_ge(s_("b_ready"), U - CREDIT)
                        act.wait_ge(s_("dBu_ready"), U - 2)
                        sc.copy(Bs[:, n % 2, :], pair[0][:, :]).then_inc(s_("b_copied"), 1)
                        act.wait_ge(s_("h_ready"), U - 2)
                        sc.activation(dA[:, n % 2, :], delta[:, bass.ds(DT * bb + dd, 1), :].rearrange("p o n -> p (o n)"),
                                      ACT.Exp, scale=alog[:, bass.ds(dd, 1), n:n + 1].rearrange("p o n -> p (o n)"))\
                            .then_inc(s_("dA_ready"), 1)
            for gi in range(4):
                act.wait_ge(s_("ln_var"), 8 + gi + 1)
                sc.activation(lnv[:, 4 * gi:4 * gi + 4, 1], lnv[:, 4 * gi:4 * gi + 4, 1], ACT.Sqrt).then_inc(s_("ln_sqrt"), 1)

            for c in range(NCH):
                act.wait_ge(s_("x3T_done"), c + 1)
                sc.copy(xT[:, c * CH:(c + 1) * CH], bank[c][:, :]).then_inc(s_("state_ready"), 1)
            act.wait_ge(s_("net_loaded"), 14 * 16)
            act.wait_ge(s_("global_mm"), 1)
            sc.activation(g1[:, :], bank[4][0:64, 0:B], ACT.Gelu, bias=gb1[:, :]).then_inc(s_("global_act"), 1)
            act.wait_ge(s_("global_mm"), 2)
            sc.activation(g2[:, :], bank[5][0:32, 0:B], ACT.Gelu, bias=gb2[:, :]).then_inc(s_("global_act"), 1)
            act.sem_inc(s_("net_act"), 1)
            act.wait_ge(s_("global_mm"), 3)
            sc.activation(gf[:, :], bank[6][:, 0:B], ACT.Sigmoid, bias=gb3[:, :]).then_inc(s_("global_act"), 1)
            with act.Fori(0, CYCLES) as i:
                for st in range(4):
                    for c in range(NCH):
                        bias = (biasT[:, CNB1_ROW:CNB1_ROW + 1], cb2[:, :], cb3[:, :], cb4[:, :])[st]
                        dst = (m1, m2, m3, tf)[st]
                        act.wait_ge(s_("net_mm"), 16 * i + 4 * st + c + 1)
                        if st == 3:
                            act.wait_ge(s_("state_ready"), NCH * i + c + 1)
                        sc.activation(dst[:, c, :], bank[2 * c + st % 2][:, :], ACT.Sigmoid if st == 3 else ACT.Gelu,
                                      bias=bias).then_inc(s_("net_act"), 1)
            for gi in range(4):
                act.wait_ge(s_("ln_var"), 12 + gi + 1)
                sc.activation(lnv[:, 4 * gi:4 * gi + 4, 1], lnv[:, 4 * gi:4 * gi + 4, 1], ACT.Sqrt).then_inc(s_("ln_sqrt"), 1)

        @block.vector
        def _(dve):
            v = nc.vector
            ch = Chain(dve, s_("dve_chain"))
            dve.wait_ge(s_("rot_loaded"), 12 * 16)
            ph = wph[:, :, :].rearrange("p j h -> p (j h)")
            ch(v.tensor_scalar(wtmp[:, 1, :], ph, 1.0 / TWO_PI, 0.25, ALU.mult, ALU.add))
            ch(v.tensor_scalar(wtmp[:, 0, :], wtmp[:, 1, :], ROUND, None, ALU.add))
            ch(v.tensor_scalar(wtmp[:, 1, :], wtmp[:, 0, :], ROUND, None, ALU.subtract))
            ch(v.scalar_tensor_tensor(wtmp[:, 0, :], wtmp[:, 1, :], -PI_HI, ph, ALU.mult, ALU.add))
            ch(v.scalar_tensor_tensor(wtmp[:, 2, :], wtmp[:, 1, :], -PI_MID, wtmp[:, 0, :], ALU.mult, ALU.add))
            ch(v.scalar_tensor_tensor(wtmp[:, 0, :], wtmp[:, 1, :], -PI_LO, wtmp[:, 2, :], ALU.mult, ALU.add))
            ch(v.tensor_scalar(wtmp[:, 2, :], wtmp[:, 0, :], TWO_PI / 4, 3.1415925, ALU.add, ALU.min))
            v.tensor_scalar(wtmp[:, 0, :], wtmp[:, 2, :], -3.1415925, None, ALU.max).then_inc(s_("args_ready"), 1)
            for c in range(1, NCH, 2):
                dve.wait_ge(s_("xT_done"), c + 1)
                v.tensor_copy(xT[:, c * CH:(c + 1) * CH], bank[c][:, :]).then_inc(s_("xT_copied_v"), 1)
            dve.wait_ge(s_("sin_done"), 1)
            v.tensor_tensor(wtmp[:, 2, :], wtmp[:, 1, :], wam[:, :, :].rearrange("p j h -> p (j h)"), ALU.mult)\
                .then_inc(s_("wcos_ready"), 1)
            dve.wait_ge(s_("wcosT_done"), 2)
            v.tensor_copy(wcosT[:], bank[4][:, 0:P]).then_inc(s_("wcosT_copied"), 1)
            v.tensor_copy(biasT[:, :], bank[5][:, 0:BROWS]).then_inc(s_("biasT_ready"), 1)
            dve.wait_ge(s_("weff_done"), 1)
            for j in range(4):
                v.tensor_copy(weff[:, j, :], bank[4 + j][:, 256:256 + C]).then_inc(s_("weff_copied"), 1)
            n = 0
            for b in range(B):
                for w, split in ((0, q_split), (1, k_split)):
                    for c in (2 * b, 2 * b + 1):
                        dve.wait_ge(s_("part1_done"), n + 1)
                        if n >= 4:
                            dve.wait_ge(s_("split_done"), n - 3)
                        v.tensor_tensor(resid[:, n % 4, :], bank[4 * w + c][:, :], split[:, 0, c * CH:(c + 1) * CH],
                                        ALU.subtract).then_inc(s_("resid_done"), 1)
                        dve.wait_ge(s_("resid_done"), n + 1)
                        dve.wait_ge(s_("part2_done"), n + 1)
                        v.tensor_tensor(split[:, 2, c * CH:(c + 1) * CH], resid[:, n % 4, :],
                                        split[:, 1, c * CH:(c + 1) * CH], ALU.subtract).then_inc(s_("split_done"), 1)
                        n += 1

            def s_pass(vunit, mslot, item0, par0, with_max, m_unit, m_par):
                k = 0
                for n in range(16):
                    if n == 4 and with_max:
                        dve.wait_ge(s_("ring_full"), item0 + k + 1)
                        v.tensor_copy(mT[0:24, m_par, :], ring_bank[(par0 + k) % 2][0:24, 0:P])\
                            .then_inc(s_("ring_read"), 1)
                        k += 1
                    dve.wait_ge(s_("ring_full"), item0 + k + 1)
                    v.reduce_max(mx[:, mslot, n // 2, n % 2:n % 2 + 1], ring_bank[(par0 + k) % 2][:, :], AX)\
                        .then_inc(s_("ring_read"), 1)
                    k += 1
                if not isinstance(vunit, int) or vunit >= 2:
                    dve.wait_ge(s_("max_split"), vunit - 1)
                dve.wait_ge(s_("ring_read"), item0 + k)
                v.tensor_tensor(rowmax[:, mslot, :], mx[:, mslot, :, 0], mx[:, mslot, :, 1], ALU.max)\
                    .then_inc(s_("max_ready"), 1)

            s_pass(0, 0, 0, 0, False, None, None)
            s_pass(1, 1, 16, 0, True, 0, 0)

            def unit(i, s, last):
                u = 4 * i + s
                dve.wait_ge(s_(f"max_loaded{(s - 1) % 4}"), 48 * (i + (1 if s else 0)) + 16)
                if last and s >= 2:
                    if s == 2:
                        dve.wait_ge(s_("ring_full"), 33 + 17 * u + 1)
                        v.tensor_copy(mT[0:24, 1, :], ring_bank[(33 + 17 * s) % 2][0:24, 0:P])\
                            .then_inc(s_("ring_read"), 1)
                    return
                s_pass(u + 2, s % 2, 33 + 17 * u, 33 + 17 * s, True, u + 1, (s + 1) % 2)

            with dve.Fori(0, UNITS // 4 - 1) as i:
                for s in range(4):
                    unit(i, s, False)
            for s in range(4):
                unit(UNITS // 4 - 1, s, True)

            dve.wait_ge(s_("o_loaded"), 8 * 16)
            ch(v.tensor_tensor(den[0:HEADS, 0, :], den[0:HEADS, 0, :], den[0:HEADS, 1, :], ALU.add))
            v.reciprocal(den[0:HEADS, 1, :], den[0:HEADS, 0, :]).then_inc(s_("recip_ready"), 1)
            ch(v.tensor_tensor(o_par[:, 0, :], o_par[:, 0, :], o_par[:, 1, :], ALU.add))
            for c in range(NCH):
                dve.wait_ge(s_("recip_spread"), c + 1)
                v.tensor_tensor(onorm[:, c * CH:(c + 1) * CH], o_par[:, 0, c * CH:(c + 1) * CH], bank[c][:, :],
                                ALU.mult).then_inc(s_("onorm_ready"), 1)
            for gi in range(4):
                dve.wait_ge(s_("attn_done"), gi + 1)
                xg = xres[:, 4 * gi:4 * gi + 4, :]
                ch(v.tensor_tensor(xg, xg, bank[4 + gi][:, :].rearrange("p (t c) -> p t c", t=4), ALU.add))
                ln_start(dve, v, ch, 4 * gi, 4)
            for gi in range(4):
                ln_end(dve, v, ch, 4 * gi, 4, gi + 1, "x1_ready")

            et = lambda ap: ap.rearrange("p e t -> p t e")
            over_e = lambda ap: ap.unsqueeze(1).to_broadcast([P, EXP, NT])
            lg, ls, ex, gates, t1, t2 = (R[n][:, :, :] for n in ("lg", "ls", "ex", "gates", "t1", "t2"))
            mask, incl, pos, keep, tw = (RW[n][:, :, :, :] for n in ("mask", "incl", "pos", "keep", "t"))
            dve.wait_ge(s_("logits_done"), 1)
            ch(v.tensor_copy(lg, bank[4][:, 0:NT * EXP].rearrange("p (t e) -> p e t", e=EXP)))
            ch(v.reduce_max(rt[:, 0, :], et(lg), AX))
            v.tensor_tensor(ls, lg, over_e(rt[:, 0, :]), ALU.subtract).then_inc(s_("logits_shifted"), 1)
            dve.wait_ge(s_("logits_shifted"), 1)
            ch(v.scalar_tensor_tensor(t1, ls, 0.0, rank[:, :, :], ALU.is_equal, ALU.mult))
            ch(v.reduce_max(rt[:, 1, :], et(t1), AX))
            ch(v.tensor_tensor(mask[:, 0], t1, over_e(rt[:, 1, :]), ALU.is_equal))
            ch(v.tensor_scalar(t2, ls, EXP_FLOOR, None, ALU.max))
            ch(v.scalar_tensor_tensor(t1, mask[:, 0], EXP_FLOOR, t2, ALU.mult, ALU.add))
            ch(v.reduce_max(rt[:, 2, :], et(t1), AX))
            ch(v.tensor_tensor(t2, t1, over_e(rt[:, 2, :]), ALU.is_equal))
            ch(v.tensor_tensor(t1, t2, rank[:, :, :], ALU.mult))
            ch(v.reduce_max(rt[:, 3, :], et(t1), AX))
            ch(v.tensor_tensor(mask[:, 1], t1, over_e(rt[:, 3, :]), ALU.is_equal))
            v.tensor_copy(mask_b[:, :, :, :], mask).then_inc(s_("mask_ready"), 1)
            dve.wait_ge(s_("gate_exp"), 1)
            ch(v.tensor_reduce(rt[:, 4, :], et(ex), AX, ALU.add))
            ch(v.reciprocal(rt[:, 5, :], rt[:, 4, :]))
            ch(v.tensor_tensor(gates, ex, over_e(rt[:, 5, :]), ALU.mult))
            dve.wait_ge(s_("places_done"), 1)
            wet = lambda ap: ap.rearrange("p (w e t) -> p w e t", w=2, e=EXP)
            flat = lambda ap: ap.rearrange("p w e t -> p (w e t)")
            ch(v.tensor_tensor_scan(flat(incl), carry[:, :], bank[6][:, 0:2 * EXP * NT], 0.0, ALU.mult, ALU.add))
            ch(v.tensor_tensor(tw, incl, wet(bank[6][:, 0:2 * EXP * NT]), ALU.subtract))
            ch(v.tensor_tensor(pos, tw, wet(bank[5][:, 0:2 * EXP * NT]), ALU.add))
            ch(v.tensor_scalar(cap1[:, :], incl[:, 0, :, NT - 1], float(CAP), None, ALU.min))
            ch(v.tensor_tensor(pos[:, 1], pos[:, 1], cap1[:, :].unsqueeze(2).to_broadcast([P, EXP, NT]), ALU.add))
            ch(v.scalar_tensor_tensor(flat(keep), flat(pos), float(CAP), flat(mask), ALU.is_lt, ALU.mult))
            ch(v.tensor_tensor(tw, pos, first[:, :, :, :], ALU.add))
            ch(v.tensor_tensor(tw, tw, keep, ALU.mult))
            wte = lambda ap: ap.rearrange("p w e t -> p w t e")
            ch(v.tensor_reduce(rt2[:, 0], wte(tw), AX, ALU.add))
            ch(v.tensor_reduce(rt2[:, 1], wte(keep), AX, ALU.add))
            ch(v.tensor_scalar(rt2[:, 2], rt2[:, 1], -1.0, 1.0, ALU.mult, ALU.add))
            ch(v.tensor_tensor(rt2[:, 2], rt2[:, 2], spill[:, :, :], ALU.mult))
            ch(v.tensor_tensor(rt2[:, 2], rt2[:, 2], rt2[:, 0], ALU.add))
            ch(v.tensor_copy(slot_i[:, 0], rt2[:, 2]))
            v.tensor_copy(slot_i[:, 1], rt2[:, 0]).then_inc(s_("slot_ready"), 1)
            for w in range(2):
                ch(v.tensor_tensor(tw[:, w], gates, keep[:, w], ALU.mult))
            ch(v.tensor_reduce(rt2[:, 3], wte(tw), AX, ALU.add))
            ch(v.tensor_tensor(rt[:, 0, :], rt2[:, 3, 0, :], rt2[:, 3, 1, :], ALU.add))
            ch(v.tensor_scalar(rt[:, 1, :], rt[:, 0, :], GATE_EPS, None, ALU.max))
            ch(v.reciprocal(rt[:, 2, :], rt[:, 1, :]))
            ch(v.tensor_tensor(rt2[:, 4], rt2[:, 3], rt[:, 2, :].unsqueeze(1).to_broadcast([P, 2, NT]), ALU.mult))

            dve.wait_ge(s_("acc_ready"), 1)
            for c in range(NCH):
                dve.wait_ge(s_("shared_down"), c + 1)
                ag = acc[:, 4 * c:4 * c + 4, :]
                v.scalar_tensor_tensor(ag, bank[4 + c][:, :].rearrange("p (t c) -> p t c", t=4), SHARED_SCALE, ag,
                                       ALU.mult, ALU.add).then_inc(s_("shared_done"), 1)

            def copy_xeT(e, s, i):
                dve.wait_ge(s_("xeT_done"), e + 1)
                v.tensor_copy(xeT[:, s, :], pair[0][:, 0:CAP]).then_inc(s_("xeT_ready"), 1)

            def expert_out(e, s, i):
                dve.wait_ge(s_("ye_done"), e + 2)
                dve.wait_ge(s_(f"ye_stored{s}"), 16 * i + 16)
                v.tensor_tensor(yer[:, s, :, :], pair[3][:, 0:CAP].rearrange("p (t c) -> p t c", t=ST),
                                b2all[:, bass.ds(e, 1), :].to_broadcast([P, ST, C]), ALU.add).then_inc(s_("ye_ready"), 1)

            dve.wait_ge(s_("shared_done"), NCH)
            dve.sem_inc(s_("ye_ready"), 1)
            copy_xeT(0, 0, 0)
            with dve.Fori(0, EXP // 2 - 1) as i:
                for s in range(2):
                    copy_xeT(2 * i + s + 1, 1 - s, i)
                    expert_out(2 * i + s, s, i)
            copy_xeT(EXP - 1, 1, 0)
            expert_out(EXP - 2, 0, EXP // 2 - 1)
            expert_out(EXP - 1, 1, EXP // 2 - 1)

            for gi in range(4):
                dve.wait_ge(s_(f"picked{gi}"), 8 * 16)
                for w in range(2):
                    for t in range(4 * gi, 4 * gi + 4):
                        dst = acc if w == 0 else xres
                        ch.mark(v.scalar_tensor_tensor(dst[:, t, :], picked[:, w, t, :], rt2[:, 4, w, t:t + 1], acc[:, t, :],
                                                       ALU.mult, ALU.add))
                    ch.wait()
                ln_start(dve, v, ch, 4 * gi, 4)
            for gi in range(4):
                ln_end(dve, v, ch, 4 * gi, 4, 4 + gi + 1, "x2_ready")

            dve.wait_ge(s_("mixer_loaded"), 6 * 16)
            for k in range(TAPS):
                last = v.tensor_tensor(wconv[:, k, :], win[:, 0:DIN], cwb[:, :].rearrange("p (d k) -> p k d", k=TAPS)[:, k, :],
                                       ALU.mult)
                ch.mark(last)
            ch.wait()
            v.tensor_copy(c_in[:, 0, :], biasT[:, 0:B]).then_inc(s_("wconv_ready"), 1)
            v.tensor_scalar(alog[:, :, :], alog[:, :, :], LOG_RATE_MAX, None, ALU.min).then_inc(s_("a_clamped"), 1)
            dve.wait_ge(s_("a_exp"), 1)
            v.tensor_scalar(alog[:, :, :], alog[:, :, :], -1.0, None, ALU.mult).then_inc(s_("a_ready"), 1)
            for b in range(B):
                sl = slice(b * L, (b + 1) * L)
                dve.wait_ge(s_("bc_1"), b + 1)
                v.tensor_tensor(bc_r[0:96, sl], pair[b][0:96, :], bc_parts[0:96, sl], ALU.subtract).then_inc(s_("bc_rest"), 1)
                dve.wait_ge(s_("bc_2"), b + 1)
                dve.wait_ge(s_("bc_rest"), b + 1)
                ch.mark(v.tensor_copy(bc_parts[32:64, sl], bc_p2[32:64, sl]))
                v.tensor_tensor(bc_parts[64:96, sl], bc_r[64:96, sl], bc_p2[64:96, sl], ALU.subtract)\
                    .then_inc(s_("bc_ready"), 1)
            ch.wait()
            for q in range(B * DT):
                bias = biasT[:, BDT_ROW + q % 2:BDT_ROW + q % 2 + 1]
                dve.wait_ge(s_("sp_abs"), q + 1)
                ch.mark(v.tensor_scalar(sp_r[:, q % 2, :], pair[2 + q % 2][:, :], bias, 0.0, ALU.add, ALU.max))
                dve.wait_ge(s_("sp_exp"), q + 1)
                ch(v.tensor_scalar(sp_d[:, q % 2, :], sp_t[:, q % 2, :], 1.0, None, ALU.add))
                v.tensor_scalar(sp_d[:, q % 2, :], sp_d[:, q % 2, :], -1.0, None, ALU.add).then_inc(s_("sp_c"), 1)
                dve.wait_ge(s_("sp_small"), q + 1)
                v.tensor_tensor(delta[:, q, :], sp_r[:, q % 2, :], sp_d[:, q % 2, :], ALU.add).then_inc(s_("delta_ready"), 1)
                dve.wait_ge(s_("delta_ready"), q + 1)
                v.tensor_tensor(du[:, q, :], delta[:, q, :], uu[:, q, :], ALU.mult).then_inc(s_("du_ready"), 1)
            dve.wait_ge(s_("du_ready"), B * DT)

            dve.sem_inc(s_("h_ready"), CREDIT)
            dve.sem_inc(s_("hc_ready"), CREDIT)
            dve.sem_inc(s_("y_read"), 1)
            with dve.Fori(0, B) as bb:
                with dve.Fori(0, DT) as dd:
                    gg = DT * bb + dd

                    def times_c(n):
                        U = CREDIT + ST_N * gg + n + 1
                        dve.wait_ge(s_("h_ready"), U)
                        dve.wait_ge(s_("c_ready"), U - CREDIT)
                        dve.wait_ge(s_("y_added"), U - 2)
                        v.tensor_tensor(hC[:, n % 2, :], hh[:, n % 2, :], pair[1 + n % 2][:, :], ALU.mult)\
                            .then_inc(s_("hc_ready"), 1)

                    for n in range(ST_N):
                        U = CREDIT + ST_N * gg + n + 1
                        dve.wait_ge(s_("dA_ready"), U)
                        dve.wait_ge(s_("dBu_ready"), U)
                        dve.wait_ge(s_("hc_ready"), U - 2)
                        v.tensor_tensor_scan(hh[:, n % 2, :], dA[:, n % 2, :], dBu[:, n % 2, :], 0.0, ALU.mult, ALU.add)\
                            .then_inc(s_("h_ready"), 1)
                        if n > 0:
                            times_c(n - 1)
                    times_c(ST_N - 1)
                    dve.wait_ge(s_("y_added"), CREDIT + ST_N * (gg + 1))
                    one = lambda t: t[:, bass.ds(gg, 1), :].rearrange("p o n -> p (o n)")
                    v.scalar_tensor_tensor(one(uu), one(uu), biasT[:, bass.ds(D_ROW + dd, 1)], pair[3][:, :], ALU.mult, ALU.add)\
                        .then_inc(s_("y_read"), 1)
                    dve.wait_ge(s_("y_read"), gg + 2)
                    v.tensor_tensor(one(gate), one(gate), one(uu), ALU.mult).then_inc(s_("y_ready"), 1)
            for gi in range(4):
                dve.wait_ge(s_("mixer_out"), gi + 1)
                xg = xres[:, 4 * gi:4 * gi + 4, :]
                ch(v.tensor_tensor(xg, xg, bank[gi][:, :].rearrange("p (t c) -> p t c", t=4), ALU.add))
                ln_start(dve, v, ch, 4 * gi, 4)
            for gi in range(4):
                ln_end(dve, v, ch, 4 * gi, 4, 8 + gi + 1, "x3_ready")

            dve.wait_ge(s_("net_loaded"), 14 * 16)
            ch.mark(v.tensor_copy(gw3b[:, :], gw[2][:, 0:1].to_broadcast([32, P])))
            ch(v.tensor_copy(w4b[:, :], cw[3][:, 0:1].to_broadcast([P, P])))
            for b in range(B):
                dve.wait_ge(s_("state_ready"), 2 * b + 2)
                ch(v.tensor_reduce(gmean[:, 0, b:b + 1], xT[:, b * L:(b + 1) * L], AX, ALU.add))
            v.tensor_scalar(gmean[:, 1, :], gmean[:, 0, :], 1.0 / L, None, ALU.mult).then_inc(s_("mean_ready"), 1)
            dve.wait_ge(s_("global_act"), 3)
            ch(v.tensor_scalar(c_in[:, 0, :], gf[:, :], 1.4, -1.0, ALU.mult, ALU.add))
            ch(v.tensor_scalar(c_in[:, 1, :], c_in[:, 0, :], rng[:, :], 0.1, ALU.mult, ALU.add))
            ch(v.tensor_scalar(c_in[:, 2, :], c_in[:, 1, :], sgn[:, :], None, ALU.mult))
            ch(v.tensor_scalar(c_in[:, 3, 0:1], rng[:, :], sgn[:, :], 0.6, ALU.mult, ALU.mult))
            with dve.Fori(0, CYCLES) as i:
                for c in range(NCH):
                    dve.wait_ge(s_("net_act"), 16 * i + 12 + c + 2)
                    v.tensor_scalar(cpl[:, c, :], tf[:, c, :], c_in[:, 3, 0:1], c_in[:, 2, c // 2:c // 2 + 1],
                                    ALU.mult, ALU.add).then_inc(s_("cpl_ready"), 1)
                    dve.wait_ge(s_("cpl_ready"), NCH * i + c + 1)
                    dve.wait_ge(s_(f"twisted{c}"), 64 * (i + 1))
                    v.tensor_tensor(prod[:, c, :], cpl[:, c, :], tw_in[:, c, :], ALU.mult).then_inc(s_("prod_ready"), 1)
                    dve.wait_ge(s_("prod_ready"), NCH * i + c + 1)
                    xc = xT[:, c * CH:(c + 1) * CH]
                    v.tensor_tensor(xc, xc, prod[:, c, :], ALU.add).then_inc(s_("state_ready"), 1)
            for gi in range(4):
                dve.wait_ge(s_("back_done"), gi + 1)
                xg = xres[:, 4 * gi:4 * gi + 4, :]
                ch(v.tensor_tensor(xg, xg, bank[gi][:, :].rearrange("p (t c) -> p t c", t=4), ALU.add))
                ln_start(dve, v, ch, 4 * gi, 4)
            for gi in range(4):
                ln_end(dve, v, ch, 4 * gi, 4, 12 + gi + 1, "x4_ready")

        @block.tensor
        def _(pe):
            t = nc.tensor
            pe.wait_ge(s_("ident_ready"), 3)
            pe.wait_ge(s_("x_loaded"), 32)
            for c in range(NCH):
                for k in range(4):
                    last = t.transpose(bank[c][:, k * P:(k + 1) * P], xres[:, 4 * c + k, :], ident[:])
                last.then_inc(s_("xT_done"), 1)
            pe.wait_ge(s_("wcos_ready"), 1)
            t.transpose(bank[4][:, 0:P], wtmp[:, 2, :], ident[:]).then_inc(s_("wcosT_done"), 1)
            pe.wait_ge(s_("brow_loaded"), 6 * 16)
            t.transpose(bank[5][:, 0:BROWS], brow[:, :], ident[0:BROWS, 0:BROWS]).then_inc(s_("wcosT_done"), 1)
            pe.wait_ge(s_("wcosT_copied"), 1)
            pe.wait_ge(s_("biasT_ready"), 1)
            for j in range(4):
                last = t.matmul(bank[4 + j][:, 256:256 + C], basis[32 * j:32 * j + 32, :], wcosT[32 * j:32 * j + 32, :],
                                start=True, stop=True)
            last.then_inc(s_("weff_done"), 1)
            pe.wait_ge(s_("xT_copied_a"), 2)
            pe.wait_ge(s_("xT_copied_v"), 2)
            pe.wait_ge(s_("weff_copied"), 4)
            for b in range(B):
                for w in range(2):
                    for c in (2 * b, 2 * b + 1):
                        t.matmul(bank[4 * w + c][:, :], weff[:, w, :], xT[:, c * CH:(c + 1) * CH], start=True, stop=True)\
                            .then_inc(s_("qk_done"), 1)
            for c in range(NCH):
                pe.wait_ge(s_("resid_done"), (2, 2, 6, 6)[c])
                for k in range(4):
                    tt = 4 * c + k
                    last = t.matmul(bank[c][:, k * P:(k + 1) * P], xT[:, tt * P:(tt + 1) * P], weff[:, 2, :],
                                    start=True, stop=True)
                last.then_inc(s_("v_done"), 1)

            pe.sem_inc(s_("probs_free"), NPROB)
            pe.sem_inc(s_("st_done"), 1)
            pe.wait_ge(s_("resid_done"), 8)
            pe.wait_ge(s_("v_copied"), 4)

            def s_half(slot, n, bk, k_abs):
                if not isinstance(k_abs, int) or k_abs >= 2:
                    pe.wait_ge(s_("ring_read"), k_abs - 1)
                t.matmul(bk[:, :], qbuf[0:96, slot, (n // 2) * P:(n // 2 + 1) * P], kbuf[0:96, slot, (n % 2) * CH:(n % 2 + 1) * CH],
                         start=True, stop=True).then_inc(s_("ring_full"), 1)

            def max_T(m, mslot, bk, k_abs):
                pe.wait_ge(s_("max_split"), m + 1)
                pe.wait_ge(s_("ring_read"), k_abs - 1)
                t.matmul(bk[0:24, 0:P], mparts[:, mslot, :], ident_b[:], start=True, stop=True)\
                    .then_inc(s_("ring_full"), 1)

            def st_half(slot, kt, h):
                return t.matmul(st_pair[kt % 2][:, h * CH:(h + 1) * CH], kbuf[0:99, slot, kt * P:(kt + 1) * P],
                                qbuf[0:99, slot, h * CH:(h + 1) * CH], start=True, stop=True)

            def pv_half(u_par, kt, h):
                g = 2 * (kt % 2) + h
                return t.matmul(pv_bank[u_par][32 * g:32 * g + 32, :], vst[:, u_par, kt, :],
                                probs[:, kt % NPROB, h * CH:(h + 1) * CH], start=kt < 2, stop=kt >= KT - 2)

            def s_pass_only(v, slot, item0, with_max):
                k = item0
                pe.wait_ge(s_(f"unit_loaded{slot}"), 64)
                for n in range(16):
                    if n == T_AT and with_max:
                        max_T(v - 1, (v - 1) % 2, ring_bank[k % 2], k)
                        k += 1
                    s_half(slot, n, ring_bank[k % 2], k)
                    k += 1

            pe.wait_ge(s_("qk_cleared"), 1)
            s_pass_only(0, 0, 0, False)
            s_pass_only(1, 1, 16, True)
            pe.wait_ge(s_("max_loaded0"), 48 + 16)
            for kt in range(2):
                for h in range(2):
                    last = st_half(0, kt, h)
                last.then_inc(s_("st_done"), 1)

            def unit(i, s, last):
                u = 4 * i + s
                k, par = 33 + ITEMS * u, (33 + ITEMS * s) % 2
                v_slot, u1_slot = (s + 2) % 4, (s + 1) % 4
                scores = not (last and s >= 2)
                if scores:
                    pe.wait_ge(s_(f"unit_loaded{v_slot}"), 64 * (i + (1 if s < 2 else 2)))
                kk = 0
                for j in range(KT):
                    ahead = not (last and s == 3 and j >= KT - 2)
                    for h in range(2):
                        n = 2 * j + h
                        if n == T_AT and not (last and s == 3):
                            max_T(u + 1, (s + 1) % 2, ring_bank[(par + kk) % 2], k + kk)
                            kk += 1
                        if scores:
                            s_half(v_slot, n, ring_bank[(par + kk) % 2], k + kk)
                            kk += 1
                        if ahead:
                            if h == 0:
                                if j == KT - 2:
                                    pe.wait_ge(s_(f"max_loaded{u1_slot}"), 48 * (i + (1 if s < 3 else 2)) + 16)
                                pe.wait_ge(s_("exp_done"), KT * u + j + 1)
                            ins = st_half(s if j < KT - 2 else u1_slot, (j + 2) % KT, h)
                            if h == 1:
                                ins.then_inc(s_("st_done"), 1)
                        if h == 0:
                            if j == 0:
                                pe.wait_ge(s_("v_staged"), u + 1)
                                pe.wait_ge(s_("pv_copied"), u + 1)
                            pe.wait_ge(s_("exp_done"), KT * u + j + 1)
                        ins = pv_half(s % 2, j, h)
                    ins.then_inc(s_("probs_free"), 1)

            with pe.Fori(0, UNITS // 4 - 1) as i:
                for s in range(4):
                    unit(i, s, False)
            for s in range(4):
                unit(UNITS // 4 - 1, s, True)

            pe.wait_ge(s_("recip_ready"), 1)
            pe.wait_ge(s_("pv_copied"), UNITS + 2)
            for c in range(NCH):
                t.matmul(bank[c][:, :], expand[:, :], den[0:HEADS, 1, c * CH:(c + 1) * CH], start=True, stop=True)\
                    .then_inc(s_("recip_spread"), 1)
            for c in range(NCH):
                pe.wait_ge(s_("onorm_ready"), c + 1)
                for k in range(4):
                    last = t.matmul(bank[4 + c][:, k * P:(k + 1) * P], onorm[:, (4 * c + k) * P:(4 * c + k + 1) * P],
                                    weff[:, 3, :], start=True, stop=True)
                last.then_inc(s_("attn_done"), 1)

            for c in range(NCH):
                pe.wait_ge(s_("x1_ready"), 4 * c + 4)
                for k in range(4):
                    last = t.transpose(bank[c][:, k * P:(k + 1) * P], xres[:, 4 * c + k, :], ident[:])
                last.then_inc(s_("x1T_done"), 1)
            pe.wait_ge(s_("ffn_loaded"), 5 * 16)
            for c in range(NCH):
                pe.wait_ge(s_("x1T_copied"), c + 1)
                for tt in range(4 * c, 4 * c + 4):
                    last = t.matmul(bank[4][:, tt * EXP:(tt + 1) * EXP], xT[:, tt * P:(tt + 1) * P], rw[:, :],
                                    start=True, stop=True)
            last.then_inc(s_("logits_done"), 1)

            def shared_up(c):
                for f in range(FT):
                    if c > 0:
                        pe.wait_ge(s_("shared_act"), (c - 1) * FT + f + 1)
                    t.matmul(bank[f][:, :], sw1[:, f * P:(f + 1) * P], xT[:, c * CH:(c + 1) * CH], start=True, stop=True)\
                        .then_inc(s_("shared_up"), 1)

            def shared_down(c):
                pe.wait_ge(s_("shared_act"), (c + 1) * FT)
                for k in range(4):
                    for f in range(FT):
                        last = t.matmul(bank[4 + c][:, k * C:(k + 1) * C], hsT[:, c % 2, f, k * P:(k + 1) * P], sw2[:, f, :],
                                        start=f == 0, stop=f == FT - 1)
                last.then_inc(s_("shared_down"), 1)

            shared_up(0)
            pe.wait_ge(s_("mask_ready"), 1)
            mb = mask_b[:, :, :, :].rearrange("p w e t -> p (w e t)")
            t.matmul(bank[5][:, 0:2 * EXP * NT], before[:, :], mb, start=True, stop=True)
            t.matmul(bank[6][:, 0:2 * EXP * NT], ones_b[:, :], mb, start=True, stop=True).then_inc(s_("places_done"), 1)
            shared_up(1)
            pe.wait_ge(s_("slot_ready"), 1)
            shared_down(0)
            for c in range(1, NCH):
                if c + 1 < NCH:
                    shared_up(c + 1)
                shared_down(c)

            def slots_T(s, count):
                pe.wait_ge(s_(f"slots_loaded{s}"), count)
                for k in range(ST):
                    last = t.transpose(pair[0][:, k * P:(k + 1) * P], xer[:, s, k, :], ident[:])
                last.then_inc(s_("xeT_done"), 1)

            def expert(i, s, last_e):
                e = 2 * i + s
                pe.wait_ge(s_("xeT_ready"), e + 1)
                pe.wait_ge(s_(f"expert_loaded{s}"), 32 * (i + 1))
                for f in range(FT):
                    pe.wait_ge(s_("up_act"), FT * e + f + 2)
                    for h in range(2):
                        last = t.matmul(pair[1 + f % 2][:, h * CH:h * CH + CAP // 2], w1r[:, s, f * P:(f + 1) * P],
                                        xeT[:, s, h * (CAP // 2):(h + 1) * (CAP // 2)], start=True, stop=True)
                    last.then_inc(s_("up_done"), 1)
                if not last_e:
                    slots_T(1 - s, 16 * (i + 1 + s))
                pe.wait_ge(s_("up_act"), FT * (e + 1) + 3)
                pe.wait_ge(s_("ye_ready"), e + 1)
                for k in range(ST):
                    for f in range(FT):
                        last = t.matmul(pair[3][:, k * C:(k + 1) * C], hT[:, f, k * P:(k + 1) * P], w2r[:, s, f, :],
                                        start=f == 0, stop=f == FT - 1)
                last.then_inc(s_("ye_done"), 1)

            pe.wait_ge(s_("shared_act"), NCH * FT)
            pe.wait_ge(s_("shared_done"), NCH)
            pe.sem_inc(s_("up_act"), 3)
            pe.sem_inc(s_("ye_done"), 1)
            slots_T(0, 16)
            with pe.Fori(0, EXP // 2 - 1) as i:
                for s in range(2):
                    expert(i, s, False)
            for s in range(2):
                expert(EXP // 2 - 1, s, s == 1)

            pe.wait_ge(s_("ye_ready"), EXP + 1)
            for c in range(NCH):
                pe.wait_ge(s_("x2_ready"), 4 * c + 4)
                for k in range(4):
                    last = t.transpose(bank[c][:, k * P:(k + 1) * P], xres[:, 4 * c + k, :], ident[:])
                last.then_inc(s_("x2T_done"), 1)
            pe.wait_ge(s_("wconv_ready"), 1)
            pe.wait_ge(s_("x2T_copied"), NCH)
            for q in range(B * DT):
                b, d = q // DT, q % DT
                if q >= 2:
                    pe.wait_ge(s_("u_ready"), q - 1)
                for h in range(2):
                    for k in range(TAPS):
                        last = t.matmul(bank[2 * (q % 2) + h][:, :], wconv[:, k, d * P:(d + 1) * P],
                                        xpad[:, b, h * CH + k:h * CH + k + CH], start=k == 0, stop=k == TAPS - 1)
                last.then_inc(s_("conv_done"), 1)
                if q >= 2:
                    pe.wait_ge(s_("gate_ready"), q - 1)
                for h in range(2):
                    at = TAPS - 1 + h * CH
                    last = t.matmul(bank[4 + 2 * (q % 2) + h][:, :], win[:, DIN + d * P:DIN + (d + 1) * P],
                                    xpad[:, b, at:at + CH], start=True, stop=True)
                last.then_inc(s_("gate_done"), 1)
            pe.wait_ge(s_("wx3_ready"), 1)
            for b in range(B):
                pe.wait_ge(s_("u_ready"), 4 if b else 3)
                for h in range(2):
                    for d in range(DT):
                        last = t.matmul(bank[2 * b + h][0:104, :], wx3[:, d, :], uu[:, DT * b + d, h * CH:(h + 1) * CH],
                                        start=d == 0, stop=d == DT - 1)
                last.then_inc(s_("bc_done"), 1)
            for q in range(B * DT):
                b, d = q // DT, q % DT
                pe.wait_ge(s_("low_ready"), b + 1)
                if q < 2:
                    pe.wait_ge(s_("gate_ready"), 3 + q)
                else:
                    pe.wait_ge(s_("delta_ready"), q - 1)
                for h in range(2):
                    last = t.matmul(bank[4 + 2 * (q % 2) + h][:, :], wdt[96:96 + RANK, d * P:(d + 1) * P],
                                    low[96:96 + RANK, b * L + h * CH:b * L + (h + 1) * CH], start=True, stop=True)
                last.then_inc(s_("delta_done"), 1)

            pe.wait_ge(s_("bc_ready"), B)
            pe.wait_ge(s_("delta_ready"), B * DT)
            pe.sem_inc(s_("y_added"), CREDIT)
            with pe.Fori(0, B) as bb:
                with pe.Fori(0, DT) as dd:
                    gg = DT * bb + dd

                    def spread(row, dst, h):
                        return t.matmul(dst[:, h * CH:(h + 1) * CH], sel[:, row, :],
                                        bc_parts[0:96, bass.ds(bb * L + h * CH, CH)], start=True, stop=True)

                    def add_y(n):
                        pe.wait_ge(s_("hc_ready"), CREDIT + ST_N * gg + n + 1)
                        for h in range(2):
                            ins = t.matmul(pair[3][:, h * CH:(h + 1) * CH], ident[:], hC[:, n % 2, h * CH:(h + 1) * CH],
                                           start=n == 0, stop=n == ST_N - 1)
                        ins.then_inc(s_("y_added"), 1)

                    for n in range(ST_N):
                        U = CREDIT + ST_N * gg + n + 1
                        pe.wait_ge(s_("b_copied"), U - 1)
                        for h in range(2):
                            ins = spread(n, pair[0], h)
                        ins.then_inc(s_("b_ready"), 1)
                        pe.wait_ge(s_("hc_ready"), U - 2)
                        for h in range(2):
                            ins = spread(ST_N + n, pair[1 + n % 2], h)
                        ins.then_inc(s_("c_ready"), 1)
                        if n == 1:
                            pe.wait_ge(s_("y_read"), gg + 1)
                        if n > 0:
                            add_y(n - 1)
                    add_y(ST_N - 1)
            pe.wait_ge(s_("y_ready"), B * DT)
            for c in range(NCH):
                for k in range(4):
                    at = (c % 2) * CH + k * P
                    for d in range(DT):
                        last = t.matmul(bank[c][:, k * P:(k + 1) * P], gate[:, DT * (c // 2) + d, at:at + P], wout[:, d, :],
                                        start=d == 0, stop=d == DT - 1)
                last.then_inc(s_("mixer_out"), 1)

            for c in range(NCH):
                pe.wait_ge(s_("x3_ready"), 4 * c + 4)
                for k in range(4):
                    last = t.transpose(bank[c][:, k * P:(k + 1) * P], xres[:, 4 * c + k, :], ident[:])
                last.then_inc(s_("x3T_done"), 1)
            pe.wait_ge(s_("net_loaded"), 14 * 16)
            pe.wait_ge(s_("mean_ready"), 1)
            t.matmul(bank[4][0:64, 0:B], gw[0][:, :], gmean[:, 1, :], start=True, stop=True).then_inc(s_("global_mm"), 1)
            pe.wait_ge(s_("global_act"), 1)
            t.matmul(bank[5][0:32, 0:B], gw[1][:, :], g1[:, :], start=True, stop=True).then_inc(s_("global_mm"), 1)
            pe.wait_ge(s_("global_act"), 2)
            t.matmul(bank[6][:, 0:B], gw3b[:, :], g2[:, :], start=True, stop=True).then_inc(s_("global_mm"), 1)
            pe.wait_ge(s_("global_act"), 3)
            with pe.Fori(0, CYCLES) as i:
                for st in range(4):
                    for c in range(NCH):
                        src = xT[:, c * CH:(c + 1) * CH] if st == 0 else (m1, m2, m3)[st - 1][:, c, :]
                        w = (cw[0], cw[1], cw[2], w4b)[st]
                        if st == 0:
                            pe.wait_ge(s_("state_ready"), NCH * i + c + 1)
                            pe.wait_ge(s_("net_act"), 16 * i + 1)
                        else:
                            pe.wait_ge(s_("net_act"), 16 * i + 4 * (st - 1) + c + 2)
                        t.matmul(bank[2 * c + st % 2][:, :], w[:, :], src, start=True, stop=True)\
                            .then_inc(s_("net_mm"), 1)
            pe.wait_ge(s_("net_act"), 16 * CYCLES + 1)
            for c in range(NCH):
                pe.wait_ge(s_("state_ready"), NCH * CYCLES + c + 1)
                for k in range(4):
                    last = t.transpose(bank[c][:, k * P:(k + 1) * P], xT[:, c * CH + k * P:c * CH + (k + 1) * P], ident[:])
                last.then_inc(s_("back_done"), 1)


_INS = ["L0_attn_x"] + [f"L0_attn_{w}_{j}" for j in "qkvo" for w in ("basis", "phase", "amp")]
_INS += [f"L0_ffn_{n}" for n in ("router_w", "w1", "b1", "w2", "b2", "sw1", "sb1", "sw2", "sb2")]
_INS += [f"L1_attn_{n}" for n in ("W_in", "conv_w", "conv_b", "W_x", "W_dt", "b_dt", "A_log", "D", "W_out")]
_INS += [f"L1_ffn_cn_{w}{j}" for j in (1, 2, 3, 4) for w in "wb"] + [f"L1_ffn_gc_{w}{j}" for j in (1, 2, 3) for w in "wb"]
_INS += ["L1_ffn_adaptive_range"]
_OUTS = [((B, L, C), "float32")]


def kernel(**inputs):
    import numpy as np
    import concourse.bacc as bacc
    from concourse.bass_utils import run_bass_kernel_spmd

    nc = bacc.Bacc("TRN2", target_bir_lowering=False, num_devices=1)
    arrays = {f"in_{n}": np.ascontiguousarray(inputs[n]) for n in _INS}
    a = {n: nc.dram_tensor(f"in_{n}", arrays[f"in_{n}"].shape, mybir.dt.from_np(arrays[f"in_{n}"].dtype),
                           kind="ExternalInput").ap() for n in _INS}
    shape, dtype = _OUTS[0]
    out = nc.dram_tensor("out_0", shape, mybir.dt.from_np(np.dtype(dtype)), kind="ExternalOutput").ap()
    build(nc, a, out)
    r = run_bass_kernel_spmd(nc, [arrays], core_ids=[0])
    return r.results[0]["out_0"]
```

```python
from contextlib import ExitStack

import concourse.bass as bass
from concourse import mybir

F32 = mybir.dt.float32
BF16 = mybir.dt.bfloat16
I32 = mybir.dt.int32
U32 = mybir.dt.uint32
ALU = mybir.AluOpType
ACT = mybir.ActivationFunctionType
AX = mybir.AxisListType.X

P = 128
B, L, C = 2, 1024, 128
NTOK = B * L
NT = NTOK // P
CH = 512
NCH = NTOK // CH
HEADS, HD, HARM = 16, 8, 32
UNITS = B * HEADS
ROWS = 9 * HD
KT = L // P
SCALE = HD ** -0.5
EPS = 1e-5
TWO_PI = 6.283185307179586
PI_HI = 6.28125
PI_MID = 0.0019350051879882812
PI_LO = TWO_PI - PI_HI - PI_MID
ROUND = 12582912.0
EXP, FF, CAP = 8, 512, 640
FT, ST = FF // P, CAP // P
SLOTS = EXP * CAP
SHARED_SCALE = 0.1
EXP_FLOOR = -87.3
GATE_EPS = 1.1920929e-07
DIN, ST_N, TAPS, RANK = 256, 16, 4, 8
DT = DIN // P
PER_B = DT * ST_N
CREDIT = 4
LOG_RATE_MAX = 80.0
CYCLES = 3
NET_LOADS = 22
NET_STEPS = 11
ARENA = 31 * 1024
B1_ROW, SB1_ROW, CONVB_ROW, BDT_ROW, D_ROW, CNB1_ROW, BROWS = 0, 32, 36, 38, 40, 42, 43
NPROB = 4
ITEMS, T_AT = 17, 4
MAXT_READ = 16 + T_AT + 1
LAST_READ = 16 + ITEMS + ITEMS * (UNITS - 2) + 1


class Chain:

    def __init__(self, eng, sem):
        self.eng, self.sem, self.n = eng, sem, 0

    def __call__(self, ins):
        self.mark(ins)
        self.wait()

    def mark(self, ins):
        ins.then_inc(self.sem, 1)
        self.n += 1
        return ins

    def wait(self):
        self.eng.wait_ge(self.sem, self.n)


def build(nc, a, out):
    ctx = ExitStack()
    with ctx:
        def sb(name, shape, dt=F32):
            return ctx.enter_context(nc.sbuf_tensor(name, shape, dt))

        def sem(name):
            return ctx.enter_context(nc.semaphore(name))

        def dram(name, shape, dt=F32):
            return nc.dram_tensor(name, shape, dt, kind="Internal").ap()

        pair = [ctx.enter_context(nc.psum_tensor(f"pair{i}", [P, 2 * CH], F32)) for i in range(4)]
        bank = [pair[i // 2][:, (i % 2) * CH:(i % 2 + 1) * CH] for i in range(8)]
        ring_bank, pv_bank, st_pair = bank[0:3], bank[3], pair[2:4]

        q_parts_d = dram("q_parts_d", [UNITS, ROWS, L], BF16)
        k_parts_d = dram("k_parts_d", [UNITS, ROWS, L], BF16)
        head_out_d = dram("head_out_d", [UNITS, 2, HD + 1, L])

        slot_x_d = dram("slot_x_d", [SLOTS + NTOK, C])
        slot_y_d = dram("slot_y_d", [SLOTS, C])

        brow = sb("brow", [BROWS, P])
        biasT = sb("biasT", [P, BROWS])
        zero = sb("zero", [P, 1280])
        ident = sb("ident", [P, P])
        ident_b = sb("ident_b", [P, P], BF16)
        xres = sb("xres", [P, NT, C])
        xT = sb("xT", [P, NTOK])
        wph = sb("wph", [P, 4, HARM])
        wam = sb("wam", [P, 4, HARM])
        wtmp = sb("wtmp", [P, 3, P])
        basis = sb("basis", [P, C])
        wcosT = sb("wcosT", [P, P])
        weff = sb("weff", [P, 4, C])
        expand = sb("expand", [P, 4, B, P])
        AR = sb("arena", [P, ARENA])
        used = [0]

        def ar(nfloat):
            at = used[0]
            used[0] += nfloat
            assert used[0] <= ARENA, used[0]
            return AR[:, at:at + nfloat]

        q_split = ar(3 * NTOK // 2).bitcast(BF16).rearrange("p (a n) -> p a n", a=3)
        k_split = ar(3 * NTOK // 2).bitcast(BF16).rearrange("p (a n) -> p a n", a=3)
        resid = ar(NTOK).rearrange("p (c n) -> p c n", c=4)
        vtok = ar(NT * HEADS * HD).rearrange("p (b h k d) -> p b h k d", b=B, h=HEADS, k=KT)
        qbuf = ar(4 * L // 2).bitcast(BF16).rearrange("p (s n) -> p s n", s=4)
        kbuf = ar(4 * L // 2).bitcast(BF16).rearrange("p (s n) -> p s n", s=4)
        probs = ar(NPROB * L).rearrange("p (s n) -> p s n", s=NPROB)
        vst = ar(2 * KT * 32).rearrange("p (s k m) -> p s k m", s=2, k=KT)
        pvs = ar(2 * CH).rearrange("p (s n) -> p s n", s=2)
        mx = ar(2 * 16).rearrange("p (s t h) -> p s t h", s=2, t=KT)
        rowmax = ar(2 * 8).rearrange("p (s n) -> p s n", s=2)
        neg1 = ar(8)
        mneg = ar(4 * 8).rearrange("p (s n) -> p s n", s=4)
        mparts = ar(2 * 12).bitcast(BF16).rearrange("p (s n) -> p s n", s=2)
        mT = ar(2 * 64).bitcast(BF16).rearrange("p (s n) -> p s n", s=2)
        used[0] = 0
        o_par = ar(2 * NTOK).rearrange("p (s n) -> p s n", s=2)
        den = ar(2 * L // 4).rearrange("p (s n) -> p s n", s=2)
        onorm = ar(NTOK)

        used[0] = 7 * NTOK
        acc = ar(NTOK).rearrange("p (t c) -> p t c", t=NT)
        picked = ar(2 * NTOK).rearrange("p (w t c) -> p w t c", w=2, t=NT)
        used[0] = 0
        w1r = ar(2 * FF).rearrange("p (s f) -> p s f", s=2)
        w2r = ar(2 * FT * C).rearrange("p (s f c) -> p s f c", s=2, f=FT)
        xer = ar(2 * ST * C).rearrange("p (s t c) -> p s t c", s=2, t=ST)
        xeT = ar(2 * CAP).rearrange("p (s n) -> p s n", s=2)
        hT = ar(FT * CAP).rearrange("p (f n) -> p f n", f=FT)
        yer = ar(2 * ST * C).rearrange("p (s t c) -> p s t c", s=2, t=ST)
        hsT = ar(2 * FT * CH).rearrange("p (s f n) -> p s f n", s=2, f=FT)
        sw1 = sb("sw1", [P, FF])
        sw2 = sb("sw2", [P, FT, C])
        sb2 = sb("sb2", [P, C])
        b2all = sb("b2all", [P, EXP, C])
        rw = sb("rw", [P, EXP])
        before = sb("before", [P, P], BF16)
        ones_b = sb("ones_b", [P, P], BF16)
        rank = sb("rank", [P, EXP, NT])
        first = sb("first", [P, 2, EXP, NT])
        carry = sb("carry", [P, 2 * EXP * NT])
        spill = sb("spill", [P, 2, NT])
        R = {n: sb("r_" + n, [P, EXP, NT]) for n in ("lg", "ls", "ex", "gates", "t1", "t2")}
        RW = {n: sb("rw_" + n, [P, 2, EXP, NT]) for n in ("mask", "incl", "pos", "keep", "t")}
        mask_b = sb("mask_b", [P, 2, EXP, NT], BF16)
        rt = sb("rt", [P, 6, NT])
        rt2 = sb("rt2", [P, 6, 2, NT])
        cap1 = sb("cap1", [P, EXP])
        slot_i = sb("slot_i", [P, 2, 2, NT], I32)

        used[0] = 0
        uu = ar(B * DT * L).rearrange("p (g n) -> p g n", g=B * DT)
        delta = ar(B * DT * L).rearrange("p (g n) -> p g n", g=B * DT)
        du = ar(B * DT * L).rearrange("p (g n) -> p g n", g=B * DT)
        gate = ar(B * DT * L).rearrange("p (g n) -> p g n", g=B * DT)
        bc_parts = ar(NTOK // 2).bitcast(BF16)
        low = xT[:, :]
        ring0 = used[0]
        dA = ar(2 * L).rearrange("p (s n) -> p s n", s=2)
        Bs = ar(2 * L).rearrange("p (s n) -> p s n", s=2)
        dBu = ar(2 * L).rearrange("p (s n) -> p s n", s=2)
        hh = ar(4 * L).rearrange("p (s n) -> p s n", s=4)
        used[0] = ring0
        sp_l = ar(4 * L).rearrange("p (s n) -> p s n", s=4)
        sp_w = ar(4 * L).rearrange("p (s n) -> p s n", s=4)
        bc_r = ar(NTOK)
        bc_p2 = ar(NTOK // 2).bitcast(BF16)
        used[0] = 0
        m1 = ar(NTOK).rearrange("p (c n) -> p c n", c=NCH)
        m2 = ar(2 * CH).rearrange("p (g n) -> p g n", g=2)
        m3 = ar(CH)
        tf = ar(NTOK).rearrange("p (c n) -> p c n", c=NCH)
        tw_in = ar(NTOK).rearrange("p (c n) -> p c n", c=NCH)
        cpl = ar(NTOK).rearrange("p (c n) -> p c n", c=NCH)
        prod = ar(NTOK).rearrange("p (c n) -> p c n", c=NCH)
        win = sb("win", [P, 2 * DIN])
        convw = sb("convw", [P, DT, TAPS])
        wx = sb("wx", [P, DT, RANK + 2 * ST_N])
        wx3 = sb("wx3", [P, DT, 104])
        wdt = sb("wdt", [P, DIN])
        alog = sb("alog", [P, DT, ST_N])
        wout = sb("wout", [P, DT, C])
        sel = sb("sel", [96, 2 * ST_N, P], BF16)
        cw1, cw2, cw3, cw4 = (sb(f"cw{j + 1}", [P, n]) for j, n in enumerate((P, P // 2, P // 4, 1)))
        cb2, cb3, cb4 = sb("cb2", [P, 1]), sb("cb3", [P, 1]), sb("cb4", [P, 1])
        gw = [sb(f"gw{j}", sh) for j, sh in ((1, [P, 64]), (2, [64, 32]), (3, [32, 1]))]
        gb1, gb2, gb3 = sb("gb1", [64, 1]), sb("gb2", [32, 1]), sb("gb3", [P, 1])
        w4b, gw3b = sb("w4b", [P, P]), sb("gw3b", [32, P])
        rng = sb("rng", [P, 1])
        sgn = sb("sgn", [P, 1])
        gmean = sb("gmean", [P, 2, B])
        g1, g2, gf = sb("g1", [64, B]), sb("g2", [32, B]), sb("gf", [P, B])
        c_in = sb("c_in", [P, 4, B])

        ln_stats = sb("ln_stats", [P, NT, 6])
        lnv = sb("lnv", [P, NT, 2])

        def one(tile, g):
            return tile[:, bass.ds(g, 1), :].rearrange("p o n -> p (o n)")

        S = {}

        def s_(name):
            if name not in S:
                S[name] = sem(name)
            return S[name]

        def ln_start(dve, v, ch, t0, n):
            for t in range(t0, t0 + n):
                ch.mark(v.bn_stats(ln_stats[:, t, :], xres[:, t, :]))
            ch.wait()
            for t in range(t0, t0 + n):
                ch.mark(v.bn_aggr(lnv[:, t, :], ln_stats[:, t, :]))
            ch.wait()
            v.tensor_scalar(lnv[:, t0:t0 + n, 1], lnv[:, t0:t0 + n, 1], EPS, None, ALU.add).then_inc(s_("ln_var"), 1)

        def ln_end(dve, v, ch, t0, n, count, ready):
            dve.wait_ge(s_("ln_sqrt"), count)
            ch(v.reciprocal(lnv[:, t0:t0 + n, 1], lnv[:, t0:t0 + n, 1]))
            for t in range(t0, t0 + n):
                last = v.tensor_scalar(xres[:, t, :], xres[:, t, :], lnv[:, t, 0:1], lnv[:, t, 1:2], ALU.subtract, ALU.mult)
                last.then_inc(s_(ready), 1)

        block = ctx.enter_context(nc.Block())

        @block.sync
        def _(sp):
            for j, n in enumerate("qkvo"):
                sp.dma_start(wph[:, j, :], a[f"L0_attn_phase_{n}"]).then_inc(s_("phase_loaded"), 16)
            for j, n in enumerate("qkvo"):
                sp.dma_start(wam[:, j, :], a[f"L0_attn_amp_{n}"]).then_inc(s_("amp_loaded"), 16)
            for row, n, src in ((B1_ROW, 32, a["L0_ffn_b1"].rearrange("e (f p) -> (e f) p", p=P)),
                                (SB1_ROW, 4, a["L0_ffn_sb1"].rearrange("(f p) -> f p", p=P)),
                                (CONVB_ROW, 2, a["L1_attn_conv_b"].rearrange("(f p) -> f p", p=P)),
                                (BDT_ROW, 2, a["L1_attn_b_dt"].rearrange("(f p) -> f p", p=P)),
                                (D_ROW, 2, a["L1_attn_D"].rearrange("(f p) -> f p", p=P)),
                                (CNB1_ROW, 1, a["L1_ffn_cn_b1"].rearrange("(f p) -> f p", p=P))):
                sp.dma_start(brow[row:row + n, :], src).then_inc(s_("brow_loaded"), 16)
            sp.dma_start(sw1[:, :], a["L0_ffn_sw1"]).then_inc(s_("ffn_loaded"), 16)
            sp.dma_start(sw2[:, :, :], a["L0_ffn_sw2"].rearrange("(f p) c -> p f c", p=P)).then_inc(s_("ffn_loaded"), 16)
            sp.dma_start(sb2[:, :], bass.AP(tensor=a["L0_ffn_sb2"].tensor, offset=0, ap=[[0, P], [1, C]]))\
                .then_inc(s_("ffn_loaded"), 16)
            sp.dma_start(b2all[:, :, :], bass.AP(tensor=a["L0_ffn_b2"].tensor, offset=0, ap=[[0, P], [C, EXP], [1, C]]))\
                .then_inc(s_("ffn_loaded"), 16)
            sp.dma_start(rw[:, :], a["L0_ffn_router_w"]).then_inc(s_("ffn_loaded"), 16)
            m, f = "L1_attn_", "L1_ffn_"
            for dst, src in ((win[:, :], a[m + "W_in"]),
                             (convw[:, :, :], bass.AP(tensor=a[m + "conv_w"].tensor, offset=0, ap=[[TAPS, P], [P * TAPS, DT], [1, TAPS]])),
                             (wx[:, :, :], a[m + "W_x"].rearrange("(t p) c -> p t c", p=P)),
                             (wdt[96:96 + RANK, :], a[m + "W_dt"]),
                             (alog[:, :, :], a[m + "A_log"].rearrange("(t p) c -> p t c", p=P)),
                             (wout[:, :, :], a[m + "W_out"].rearrange("(t p) c -> p t c", p=P))):
                sp.dma_start(dst, src).then_inc(s_("mixer_loaded"), 16)

            def column(t):
                return t.rearrange("(p o) -> p o", o=1)

            def everywhere(t):
                return bass.AP(tensor=t.tensor, offset=0, ap=[[0, P], [1, 1]])

            for dst, src in [(cw1[:, :], a[f + "cn_w1"]), (cw2[:, :], a[f + "cn_w2"])] + \
                    [(cw3[64 * j:64 * j + 64, :], a[f + "cn_w3"]) for j in range(2)] + \
                    [(cw4[32 * j:32 * j + 32, :], a[f + "cn_w4"]) for j in range(4)] + \
                    [(cb2[64 * j:64 * j + 64, :], column(a[f + "cn_b2"])) for j in range(2)] + \
                    [(cb3[32 * j:32 * j + 32, :], column(a[f + "cn_b3"])) for j in range(4)] + \
                    [(gw[j][:, :], a[f + f"gc_w{j + 1}"]) for j in range(3)] + \
                    [(gb1[:, :], column(a[f + "gc_b1"])), (gb2[:, :], column(a[f + "gc_b2"])),
                     (cb4[:, :], everywhere(a[f + "cn_b4"])), (gb3[:, :], everywhere(a[f + "gc_b3"])),
                     (rng[:, :], everywhere(a[f + "adaptive_range"]))]:
                sp.dma_start(dst, src).then_inc(s_("net_loaded"), 16)

            def store_parts(b):
                for which, (split, dst) in enumerate(((q_split, q_parts_d), (k_split, k_parts_d))):
                    sp.wait_ge(s_("split_done"), 4 * b + 2 * which + 2)
                    own, other = ((3, 1), (1, 3))[which]
                    for k in range(3):
                        sp.dma_start(bass.AP(tensor=dst.tensor, offset=(b * HEADS * ROWS + other * k) * L,
                                             ap=[[9 * L, P], [own * L, 3], [1, L]]),
                                     split[:, :, b * L:(b + 1) * L]).then_inc(s_(f"parts_stored{b}"), 16)

            store_parts(0)
            sp.wait_ge(s_("parts_stored0"), 6 * 16)
            sp.wait_ge(s_("qk_cleared"), 1)

            def load_unit(u, slot):
                for buf, parts in ((qbuf, q_parts_d), (kbuf, k_parts_d)):
                    sp.dma_start(buf[0:ROWS, slot, :], bass.AP(tensor=parts.tensor, offset=u * ROWS * L, ap=[[L, ROWS], [1, L]]))\
                        .then_inc(s_(f"unit_loaded{slot}"), 16)

            def load_max(count, slot, m):
                sp.wait_ge(s_("ring_read"), count)
                sp.dma_start(qbuf[96:99, slot, :], mT[0:24, m, :]).then_inc(s_(f"max_loaded{slot}"), 16)

            def store_head(u, s):
                sp.wait_ge(s_("pv_copied"), u + 2)
                for par in range(2):
                    for qh in range(2):
                        g = 2 * par + qh
                        dst = bass.AP(tensor=head_out_d.tensor, offset=((u * 2 + par) * (HD + 1)) * L + qh * CH,
                                      ap=[[L, HD + 1], [1, CH]])
                        sp.dma_start(dst, pvs[32 * g:32 * g + HD + 1, s, :]).then_inc(s_(f"head_stored{s}"), 16)

            for s in range(4):
                sp.sem_inc(s_(f"max_loaded{s}"), 16)
            for s in range(2):
                sp.sem_inc(s_(f"head_stored{s}"), 16)
                sp.sem_inc(s_(f"ye_stored{s}"), 16)
            for u in range(3):
                load_unit(u, u)
            store_parts(1)
            load_max(MAXT_READ, 0, 0)
            sp.wait_ge(s_("zero_ready"), 1)
            for k in range(4):
                sp.dma_start(slot_x_d[k * 1280:(k + 1) * 1280, :].rearrange("(p r) c -> p (r c)", p=P), zero[:, :])\
                    .then_inc(s_("slots_zeroed"), 16)
            sp.wait_ge(s_("parts_stored1"), 6 * 16)
            def unit(i, s, last):
                u = 4 * i + s
                if not (last and s > 0):
                    sp.wait_ge(s_("st_done"), KT * u + 1)
                    load_unit(u + 3, (s + 3) % 4)
                if not (last and s == 3):
                    load_max(LAST_READ if last and s == 2 else MAXT_READ + ITEMS * (u + 1), (s + 1) % 4, (s + 1) % 2)
                store_head(u, s % 2)

            with sp.Fori(0, UNITS // 4 - 1) as i:
                for s in range(4):
                    unit(i, s, False)
            for s in range(4):
                unit(UNITS // 4 - 1, s, True)
            for s in range(2):
                sp.wait_ge(s_(f"head_stored{s}"), 4 * 16 * UNITS // 2 + 16)
            for b in range(B):
                for par in range(2):
                    src = bass.AP(tensor=head_out_d.tensor, offset=(b * HEADS * 2 + par) * (HD + 1) * L,
                                  ap=[[2 * (HD + 1) * L, HEADS], [L, HD], [1, L]])
                    sp.dma_start(o_par[:, par, b * L:(b + 1) * L], src).then_inc(s_("o_loaded"), 16)
            for par in range(2):
                src = bass.AP(tensor=head_out_d.tensor, offset=(par * (HD + 1) + HD) * L,
                              ap=[[L // 4, 4], [2 * (HD + 1) * L, UNITS], [1, L // 4]])
                sp.dma_start(den[:, par, :], src).then_inc(s_("o_loaded"), 16)
            def load_weights(e, s):
                sp.dma_start(w1r[:, s, :], bass.AP(tensor=a["L0_ffn_w1"].tensor, offset=e * C * FF, ap=[[FF, C], [1, FF]]))\
                    .then_inc(s_(f"expert_loaded{s}"), 16)
                sp.dma_start(w2r[:, s, :, :], bass.AP(tensor=a["L0_ffn_w2"].tensor, offset=e * FF * C,
                                                      ap=[[C, P], [P * C, FT], [1, C]])).then_inc(s_(f"expert_loaded{s}"), 16)

            def load_slots(e, s):
                sp.dma_start(xer[:, s, :, :], bass.AP(tensor=slot_x_d.tensor, offset=e * CAP * C,
                                                      ap=[[C, P], [P * C, ST], [1, C]])).then_inc(s_(f"slots_loaded{s}"), 16)

            sp.wait_ge(s_("onorm_ready"), 4)
            for e in range(2):
                load_weights(e, e)
            sp.wait_ge(s_("scattered"), 2 * NT * 16)
            for e in range(2):
                load_slots(e, e)

            def expert_io(i, s, last):
                e = 2 * i + s
                if not last:
                    sp.wait_ge(s_("xeT_done"), e + 1)
                    load_slots(e + 2, s)
                sp.wait_ge(s_("ye_ready"), e + 2)
                sp.dma_start(bass.AP(tensor=slot_y_d.tensor, offset=e * CAP * C, ap=[[C, P], [P * C, ST], [1, C]]),
                             yer[:, s, :, :]).then_inc(s_(f"ye_stored{s}"), 16)
                if not last:
                    load_weights(e + 2, s)

            with sp.Fori(0, EXP // 2 - 1) as i:
                for s in range(2):
                    expert_io(i, s, False)
            for s in range(2):
                expert_io(EXP // 2 - 1, s, True)
            def twist(i, c):
                for dst, src in ((0, 64), (32, 96), (64, 0), (96, 32)):
                    sp.dma_start(tw_in[dst:dst + 32, c, :], xT[src:src + 32, c * CH:(c + 1) * CH])\
                        .then_inc(s_(f"twisted{c}"), 16)

            with sp.Fori(0, CYCLES) as i:
                for c in range(NCH):
                    sp.wait_ge(s_("state_ready"), NCH * i + c + 1)
                    twist(i, c)
            for gi in range(4):
                sp.wait_ge(s_("x4_ready"), 4 * gi + 4)
                sp.dma_start(out[gi // 2, (gi % 2) * CH:(gi % 2 + 1) * CH, :].rearrange("(t p) c -> p t c", p=P),
                             xres[:, 4 * gi:4 * gi + 4, :]).then_inc(s_("out_stored"), 16)
            sp.wait_ge(s_("out_stored"), 4 * 16)

        @block.gpsimd
        def _(pool):
            g = nc.gpsimd
            ch = Chain(pool, s_("pool_chain"))
            ch(g.memset(ident[:], 0.0))
            g.affine_select(out=ident[:], in_=ident[:], compare_op=ALU.not_equal, fill=1.0, base=0,
                            pattern=[[-1, P]], channel_multiplier=1).then_inc(s_("ident_ready"), 1)
            ch(g.memset(ident_b[:], 0.0))
            ch(g.affine_select(out=ident_b[:], in_=ident_b[:], compare_op=ALU.not_equal, fill=1.0, base=0,
                               pattern=[[-1, P]], channel_multiplier=1))
            ch(g.memset(qbuf[64:128, :, :], 0.0))
            ch(g.memset(kbuf[64:96, :, :], 0.0))
            ch(g.memset(kbuf[96:128, :, :], 0.0))
            g.memset(kbuf[96:99, :, :], 1.0).then_inc(s_("qk_cleared"), 1)
            pool.wait_ge(s_("qk_cleared"), 1)
            ch.mark(g.memset(neg1[:, :], -1.0))
            ch(g.memset(vst[:, :, :, :], 0.0))
            ch(g.memset(vst[:, :, :, HD:HD + 1], 1.0))
            def stage_v(u, s):
                src = vtok[:, :, :, :, :].rearrange("p b h k d -> p (b h) k d")
                return g.tensor_copy(vst[:, s, :, 0:HD], src[:, bass.ds(u, 1), :, :].rearrange("p o k d -> p (o k) d"))

            def split_max(v, s, c):
                pool.wait_ge(s_("max_ready"), v + 1)
                c(g.tensor_tensor(mparts[:, s, 0:8], rowmax[:, s, :], neg1[:, :], ALU.mult))
                c(g.tensor_tensor(mneg[:, 1, :], rowmax[:, s, :], mparts[:, s, 0:8], ALU.add))
                c(g.tensor_tensor(mparts[:, s, 8:16], mneg[:, 1, :], neg1[:, :], ALU.mult))
                c(g.tensor_tensor(mneg[:, 2, :], mneg[:, 1, :], mparts[:, s, 8:16], ALU.add))
                g.tensor_tensor(mparts[:, s, 16:24], mneg[:, 2, :], neg1[:, :], ALU.mult)\
                    .then_inc(s_("max_split"), 1)

            pool.wait_ge(s_("v_copied"), 4)
            stage_v(0, 0).then_inc(s_("v_staged"), 1)

            class At:
                def __init__(self, start):
                    self.start, self.n = start, 0

                def __call__(self, ins):
                    ins.then_inc(s_("pool_chain"), 1)
                    self.n += 1
                    pool.wait_ge(s_("pool_chain"), self.start + self.n)

            split_max(0, 0, ch)
            split_max(1, 1, ch)

            ch(g.memset(expand[:], 1.0))
            ch.mark(g.memset(ones_b[:], 1.0))
            g.memset(zero[:], 0.0).then_inc(s_("zero_ready"), 1)
            ch.wait()
            ch.mark(g.affine_select(out=before[:], in_=ones_b[:], compare_op=ALU.is_gt, fill=0.0, base=0,
                                    pattern=[[1, P]], channel_multiplier=-1))
            ch.mark(g.iota(rank[:], pattern=[[-1, EXP], [0, NT]], base=EXP, channel_multiplier=0,
                           allow_small_or_imprecise_dtypes=True))
            ch.mark(g.iota(first[:], pattern=[[0, 2], [CAP, EXP], [0, NT]], base=0, channel_multiplier=0,
                           allow_small_or_imprecise_dtypes=True))
            ch.mark(g.iota(spill[:], pattern=[[0, 2], [P, NT]], base=SLOTS, channel_multiplier=1,
                           allow_small_or_imprecise_dtypes=True))
            ch(g.memset(carry[:], 1.0))
            ch(g.memset(carry[:, :].rearrange("p (w t) -> p w t", t=NT)[:, :, 0:1], 0.0))
            ch.mark(g.memset(sel[:], 0.0))
            ch.wait()
            for at, value in ((0, 1.0), (32, -1.0), (64, -1.0), (96, 1.0)):
                ch(g.memset(sgn[at:at + 32, :], value))
            for q in range(3):
                ch(g.affine_select(out=sel[:], in_=sel[:], compare_op=ALU.not_equal, fill=1.0, base=-32 * q,
                                   pattern=[[-1, 2 * ST_N], [0, P]], channel_multiplier=1))
            flat = expand[:, :, :, :].rearrange("p q b m -> p (q b m)")
            ch(g.affine_select(out=flat, in_=flat, compare_op=ALU.is_ge, fill=0.0, base=0,
                               pattern=[[1, 4 * B * P]], channel_multiplier=-HD))
            ch(g.affine_select(out=flat, in_=flat, compare_op=ALU.is_ge, fill=0.0, base=HD - 1,
                               pattern=[[-1, 4 * B * P]], channel_multiplier=HD))
            pool.sem_inc(s_("expand_ready"), 1)
            base = ch.n - 8

            def unit(i, s, last):
                u = 4 * i + s
                if not (last and s == 3):
                    pool.wait_ge(s_("probs_free"), NPROB + KT * u)
                    stage_v(u + 1, (s + 1) % 2).then_inc(s_("v_staged"), 1)
                if not (last and s > 1):
                    pool.wait_ge(s_("ring_full"), MAXT_READ + ITEMS * u)
                    split_max(u + 2, s % 2, At(base + 8 + 4 * u))

            with pool.Fori(0, UNITS // 4 - 1) as i:
                for s in range(4):
                    unit(i, s, False)
            for s in range(4):
                unit(UNITS // 4 - 1, s, True)
            ch.n = base + 4 * UNITS
            pool.wait_ge(s_("onorm_ready"), 4)
            pool.wait_ge(s_("ffn_loaded"), 5 * 16)
            pool.wait_ge(s_("x1_ready"), NT)
            ch(g.tensor_scalar(sb2[:, :], sb2[:, :], SHARED_SCALE, None, ALU.mult))
            g.tensor_tensor(acc[:, :, :], xres[:, :, :], sb2[:, :].unsqueeze(1).to_broadcast([P, NT, C]), ALU.add)\
                .then_inc(s_("acc_ready"), 1)
            pool.wait_ge(s_("slots_zeroed"), 4 * 16)
            pool.wait_ge(s_("slot_ready"), 1)
            for w in range(2):
                for t in range(NT):
                    g.indirect_dma_start(out=slot_x_d[:, :], out_offset=bass.IndirectOffsetOnAxis(ap=slot_i[:, 0, w, t:t + 1], axis=0),
                                         in_=xres[:, t, :], in_offset=None).then_inc(s_("scattered"), 16)
            for s in range(2):
                pool.wait_ge(s_(f"ye_stored{s}"), EXP // 2 * 16 + 16)
            for t in range(NT):
                for w in range(2):
                    g.indirect_dma_start(out=picked[:, w, t, :], out_offset=None, in_=slot_y_d[:, :],
                                         in_offset=bass.IndirectOffsetOnAxis(ap=slot_i[:, 1, w, t:t + 1], axis=0))\
                        .then_inc(s_(f"picked{t // 4}"), 16)

            pool.wait_ge(s_("mixer_loaded"), 6 * 16)
            for k in range(3):
                ch.mark(g.tensor_copy(wx3[:, :, 32 * k:32 * k + 32], wx[:, :, RANK:RANK + 2 * ST_N]))
            g.tensor_copy(wx3[:, :, 96:104], wx[:, :, 0:RANK]).then_inc(s_("wx3_ready"), 1)
            ch.wait()
            pool.wait_ge(s_("wx3_ready"), 1)
            for q in range(B * DT):
                pool.wait_ge(s_("sp_ln"), q + 1)
                pool.wait_ge(s_("sp_c"), q + 1)
                g.tensor_tensor(sp_l[:, q, :], sp_l[:, q, :], du[:, q, :], ALU.subtract).then_inc(s_("sp_small"), 1)
            pool.wait_ge(s_("sp_small"), B * DT)
            pool.wait_ge(s_("du_ready"), B * DT)
            pool.sem_inc(s_("dBu_ready"), CREDIT)
            with pool.Fori(0, B) as bb:
                for n in range(ST_N):
                    for d in range(DT):
                        U = CREDIT + PER_B * bb + DT * n + d + 1
                        if d == 0:
                            pool.wait_ge(s_("b_copied"), CREDIT + ST_N * bb + n + 1)
                        pool.wait_ge(s_("h_ready"), U - 2)
                        pool.sem_inc(s_("dBu_begun"), 1)
                        g.tensor_tensor(dBu[:, d, :], one(du, DT * bb + d), Bs[:, n % 2, :], ALU.mult)\
                            .then_inc(s_("dBu_ready"), 1)

        @block.scalar
        def _(act):
            sc = nc.scalar
            ch = Chain(act, s_("act_chain"))
            for b in range(B):
                act.dma_start(xres[:, b * 8:b * 8 + 8, :],
                              a["L0_attn_x"][b].rearrange("(t p) c -> p t c", p=P)).then_inc(s_("x_loaded"), 16)
            for j, n in enumerate("qkvo"):
                act.dma_start(basis[32 * j:32 * j + 32, :], a[f"L0_attn_basis_{n}"]).then_inc(s_("basis_loaded"), 16)
            act.wait_ge(s_("args_ready"), 1)
            sc.activation(wtmp[:, 1, :], wtmp[:, 0, :], ACT.Sin).then_inc(s_("sin_done"), 1)
            for c in range(0, NCH, 2):
                act.wait_ge(s_("xT_done"), c + 1)
                sc.copy(xT[:, c * CH:(c + 1) * CH], bank[c][:, :]).then_inc(s_("xT_copied_a"), 1)
            n = 0
            for b in range(B):
                for w, split in ((0, q_split), (1, k_split)):
                    for c in (2 * b, 2 * b + 1):
                        act.wait_ge(s_("qk_done"), n + 1)
                        sc.copy(split[:, 0, c * CH:(c + 1) * CH], bank[4 * w + c][:, :]).then_inc(s_("part1_done"), 1)
                        act.wait_ge(s_("resid_done"), n + 1)
                        sc.copy(split[:, 1, c * CH:(c + 1) * CH], resid[:, n % 4, :]).then_inc(s_("part2_done"), 1)
                        n += 1
            for c in range(NCH):
                act.wait_ge(s_("v_done"), c + 1)
                b, t0 = c // 2, 4 * (c % 2)
                sc.copy(vtok[:, b, :, t0:t0 + 4, :].rearrange("p h k d -> p k h d"),
                        bank[c][:, :].rearrange("p (k h d) -> p k h d", k=4, h=HEADS)).then_inc(s_("v_copied"), 1)

            def exps(G, kt, w):
                act.wait_ge(s_("st_done"), G + 2)
                act.wait_ge(s_("probs_free"), G + 1)
                sc.activation(probs[:, kt % NPROB, :], st_pair[kt % 2][:, :], ACT.Exp, scale=SCALE)\
                    .then_inc(s_("exp_done"), 1)

            act.sem_inc(s_("pv_copied"), 1)
            for G in range(2):
                exps(G, G, 0)

            def unit(i, s, last):
                u = 4 * i + s
                for j in range(KT):
                    if last and s == 3 and j >= KT - 2:
                        continue
                    exps(KT * u + j + 2, j + 2, s)
                act.wait_ge(s_("probs_free"), NPROB + KT * (u + 1))
                act.wait_ge(s_(f"head_stored{s % 2}"), 4 * 16 * (2 * i + s // 2) + 16)
                sc.copy(pvs[:, s % 2, :], pv_bank).then_inc(s_("pv_copied"), 1)

            with act.Fori(0, UNITS // 4 - 1) as i:
                for s in range(4):
                    unit(i, s, False)
            for s in range(4):
                unit(UNITS // 4 - 1, s, True)

            for gi in range(4):
                act.wait_ge(s_("ln_var"), gi + 1)
                sc.activation(lnv[:, 4 * gi:4 * gi + 4, 1], lnv[:, 4 * gi:4 * gi + 4, 1], ACT.Sqrt).then_inc(s_("ln_sqrt"), 1)

            for c in range(NCH):
                act.wait_ge(s_("x1T_done"), c + 1)
                sc.copy(xT[:, c * CH:(c + 1) * CH], bank[c][:, :]).then_inc(s_("x1T_copied"), 1)
            act.wait_ge(s_("biasT_ready"), 1)
            act.wait_ge(s_("logits_shifted"), 1)
            sc.activation(R["ex"][:, :, :], R["ls"][:, :, :], ACT.Exp).then_inc(s_("gate_exp"), 1)
            for c in range(NCH):
                if c >= 2:
                    act.wait_ge(s_("shared_done"), c - 1)
                for f in range(FT):
                    act.wait_ge(s_("shared_up"), c * FT + f + 1)
                    sc.activation(hsT[:, c % 2, f, :], bank[f][:, :], ACT.Silu, bias=biasT[:, SB1_ROW + f:SB1_ROW + f + 1])\
                        .then_inc(s_("shared_act"), 1)

            def expert_act(i, s):
                e = 2 * i + s
                act.wait_ge(s_("ye_done"), e + 1)
                for f in range(FT):
                    act.wait_ge(s_("up_done"), FT * e + f + 1)
                    sc.activation(hT[:, f, :].rearrange("p (h n) -> p h n", h=2),
                                  pair[1 + f % 2][:, :].rearrange("p (h n) -> p h n", h=2)[:, :, 0:CAP // 2],
                                  ACT.Silu, bias=biasT[:, bass.ds(FT * e + f, 1)]).then_inc(s_("up_act"), 1)

            with act.Fori(0, EXP // 2) as i:
                for s in range(2):
                    expert_act(i, s)
            for gi in range(4):
                act.wait_ge(s_("ln_var"), 4 + gi + 1)
                sc.activation(lnv[:, 4 * gi:4 * gi + 4, 1], lnv[:, 4 * gi:4 * gi + 4, 1], ACT.Sqrt).then_inc(s_("ln_sqrt"), 1)

            for c in range(NCH):
                act.wait_ge(s_("x2T_done"), c + 1)
                sc.copy(xT[:, c * CH:(c + 1) * CH], bank[c][:, :]).then_inc(s_("x2T_copied"), 1)

            def silu_u(q):
                act.wait_ge(s_("taps_done"), q + 1)
                sc.activation(uu[:, q, :], uu[:, q, :], ACT.Silu).then_inc(s_("u_ready"), 1)

            for q in range(B * DT):
                d = q % DT
                act.wait_ge(s_("u_in_done"), q + 1)
                sc.activation(uu[:, q, :], pair[q % 2][:, :], ACT.Identity, bias=biasT[:, CONVB_ROW + d:CONVB_ROW + d + 1],
                              scale=convw[:, d, TAPS - 1:TAPS]).then_inc(s_("last_tap"), 1)
                act.wait_ge(s_("gate_done"), q + 1)
                sc.activation(gate[:, q, :], pair[2 + q % 2][:, :], ACT.Silu).then_inc(s_("gate_ready"), 1)
                if q > 0:
                    silu_u(q - 1)
            silu_u(B * DT - 1)
            act.wait_ge(s_("a_clamped"), 1)
            sc.activation(alog[:, :, :], alog[:, :, :], ACT.Exp).then_inc(s_("a_exp"), 1)
            for b in range(B):
                act.wait_ge(s_("bc_done"), b + 1)
                sl = slice(b * L, (b + 1) * L)
                sc.copy(low[96:96 + RANK, sl], pair[b][96:96 + RANK, :]).then_inc(s_("low_ready"), 1)
                sc.copy(bc_parts[0:96, sl], pair[b][0:96, :]).then_inc(s_("bc_1"), 1)
                act.wait_ge(s_("bc_rest"), b + 1)
                sc.copy(bc_p2[0:96, sl], bc_r[0:96, sl]).then_inc(s_("bc_2"), 1)
            for q in range(B * DT):
                act.wait_ge(s_("delta_done"), q + 1)
                bias = biasT[:, BDT_ROW + q % 2:BDT_ROW + q % 2 + 1]
                sc.activation(sp_l[:, q, :], pair[2 + q % 2][:, :], ACT.Abs, bias=bias).then_inc(s_("sp_abs"), 1)
                act.wait_ge(s_("sp_abs"), q + 1)
                sc.activation(du[:, q, :], sp_l[:, q, :], ACT.Exp, scale=-1.0).then_inc(s_("sp_exp"), 1)
            for q in range(B * DT):
                act.wait_ge(s_("sp_exp"), q + 1)
                act.wait_ge(s_("sp_w_ready"), q + 1)
                sc.activation(sp_l[:, q, :], sp_w[:, q, :], ACT.Ln).then_inc(s_("sp_ln"), 1)
            act.wait_ge(s_("a_ready"), 1)
            act.wait_ge(s_("delta_ready"), B * DT)
            act.wait_ge(s_("bc_ready"), B)
            act.sem_inc(s_("b_copied"), CREDIT)
            act.sem_inc(s_("dA_ready"), CREDIT)
            with act.Fori(0, B) as bb:
                for n in range(ST_N):
                    U = CREDIT + PER_B * bb + DT * n + 1
                    act.wait_ge(s_("b_ready"), ST_N * bb + n + 1)
                    act.wait_ge(s_("dBu_ready"), U - 3)
                    sc.copy(Bs[:, n % 2, :], pair[0][:, :]).then_inc(s_("b_copied"), 1)
                    for d in range(DT):
                        act.wait_ge(s_("h_ready"), U + d - 2)
                        act.sem_inc(s_("dA_begun"), 1)
                        sc.activation(dA[:, d, :], one(delta, DT * bb + d), ACT.Exp, scale=alog[:, d, n:n + 1])\
                            .then_inc(s_("dA_ready"), 1)
            for gi in range(4):
                act.wait_ge(s_("ln_var"), 8 + gi + 1)
                sc.activation(lnv[:, 4 * gi:4 * gi + 4, 1], lnv[:, 4 * gi:4 * gi + 4, 1], ACT.Sqrt).then_inc(s_("ln_sqrt"), 1)

            for c in range(NCH):
                act.wait_ge(s_("x3T_done"), c + 1)
                sc.copy(xT[:, c * CH:(c + 1) * CH], bank[c][:, :]).then_inc(s_("state_ready"), 1)
            act.wait_ge(s_("net_loaded"), NET_LOADS * 16)
            act.wait_ge(s_("global_mm"), 1)
            sc.activation(g1[:, :], bank[4][0:64, 0:B], ACT.Gelu, bias=gb1[:, :]).then_inc(s_("global_act"), 1)
            act.wait_ge(s_("global_mm"), 2)
            sc.activation(g2[:, :], bank[5][0:32, 0:B], ACT.Gelu, bias=gb2[:, :]).then_inc(s_("global_act"), 1)
            act.wait_ge(s_("halves_ready"), 1)
            act.wait_ge(s_("global_mm"), 3)
            sc.activation(gf[:, :], bank[6][:, 0:B], ACT.Tanh, bias=gb3[:, :], scale=0.5).then_inc(s_("global_act"), 1)
            with act.Fori(0, CYCLES) as i:
                for c in range(NCH):
                    act.wait_ge(s_("net_mm"), NET_STEPS * i + c + 1)
                    sc.activation(m1[:, c, :], bank[c][:, :], ACT.Gelu, bias=biasT[:, CNB1_ROW:CNB1_ROW + 1])\
                        .then_inc(s_("net_act"), 1)
                for j in range(2):
                    act.wait_ge(s_("net_mm"), NET_STEPS * i + 4 + j + 1)
                    sc.activation(m2[:, j, :], bank[4 + j][:, :], ACT.Gelu, bias=cb2[:, :]).then_inc(s_("net_act"), 1)
                act.wait_ge(s_("net_mm"), NET_STEPS * i + 7)
                sc.activation(m3[:, :], bank[6][:, :], ACT.Gelu, bias=cb3[:, :]).then_inc(s_("net_act"), 1)
                for c in range(NCH):
                    act.wait_ge(s_("net_mm"), NET_STEPS * i + 7 + c + 1)
                    act.wait_ge(s_("state_ready"), NCH * i + c + 1)
                    sc.activation(tf[:, c, :], bank[c][:, :], ACT.Tanh, bias=cb4[:, :], scale=0.5).then_inc(s_("net_act"), 1)
            for gi in range(4):
                act.wait_ge(s_("ln_var"), 12 + gi + 1)
                sc.activation(lnv[:, 4 * gi:4 * gi + 4, 1], lnv[:, 4 * gi:4 * gi + 4, 1], ACT.Sqrt).then_inc(s_("ln_sqrt"), 1)

        @block.vector
        def _(dve):
            v = nc.vector
            ch = Chain(dve, s_("dve_chain"))
            dve.wait_ge(s_("phase_loaded"), 4 * 16)
            ph = wph[:, :, :].rearrange("p j h -> p (j h)")
            ch(v.tensor_scalar(wtmp[:, 1, :], ph, 1.0 / TWO_PI, 0.25, ALU.mult, ALU.add))
            ch(v.tensor_scalar(wtmp[:, 0, :], wtmp[:, 1, :], ROUND, None, ALU.add))
            ch(v.tensor_scalar(wtmp[:, 1, :], wtmp[:, 0, :], ROUND, None, ALU.subtract))
            ch(v.scalar_tensor_tensor(wtmp[:, 0, :], wtmp[:, 1, :], -PI_HI, ph, ALU.mult, ALU.add))
            ch(v.scalar_tensor_tensor(wtmp[:, 2, :], wtmp[:, 1, :], -PI_MID, wtmp[:, 0, :], ALU.mult, ALU.add))
            ch(v.scalar_tensor_tensor(wtmp[:, 0, :], wtmp[:, 1, :], -PI_LO, wtmp[:, 2, :], ALU.mult, ALU.add))
            ch(v.tensor_scalar(wtmp[:, 2, :], wtmp[:, 0, :], TWO_PI / 4, 3.1415925, ALU.add, ALU.min))
            v.tensor_scalar(wtmp[:, 0, :], wtmp[:, 2, :], -3.1415925, None, ALU.max).then_inc(s_("args_ready"), 1)
            for c in range(1, NCH, 2):
                dve.wait_ge(s_("xT_done"), c + 1)
                v.tensor_copy(xT[:, c * CH:(c + 1) * CH], bank[c][:, :]).then_inc(s_("xT_copied_v"), 1)
            dve.wait_ge(s_("sin_done"), 1)
            dve.wait_ge(s_("amp_loaded"), 4 * 16)
            v.tensor_tensor(wtmp[:, 2, :], wtmp[:, 1, :], wam[:, :, :].rearrange("p j h -> p (j h)"), ALU.mult)\
                .then_inc(s_("wcos_ready"), 1)
            dve.wait_ge(s_("wcosT_done"), 1)
            v.tensor_copy(wcosT[:], bank[4][:, 0:P]).then_inc(s_("wcosT_copied"), 1)
            dve.wait_ge(s_("weff_done"), 1)
            for j in range(4):
                v.tensor_copy(weff[:, j, :], bank[4 + j][:, 256:256 + C]).then_inc(s_("weff_copied"), 1)
            n = 0
            for b in range(B):
                for w, split in ((0, q_split), (1, k_split)):
                    for c in (2 * b, 2 * b + 1):
                        dve.wait_ge(s_("part1_done"), n + 1)
                        if n >= 4:
                            dve.wait_ge(s_("split_done"), n - 3)
                        v.tensor_tensor(resid[:, n % 4, :], bank[4 * w + c][:, :], split[:, 0, c * CH:(c + 1) * CH],
                                        ALU.subtract).then_inc(s_("resid_done"), 1)
                        dve.wait_ge(s_("resid_done"), n + 1)
                        dve.wait_ge(s_("part2_done"), n + 1)
                        v.tensor_tensor(split[:, 2, c * CH:(c + 1) * CH], resid[:, n % 4, :],
                                        split[:, 1, c * CH:(c + 1) * CH], ALU.subtract).then_inc(s_("split_done"), 1)
                        n += 1

            def reduce_pass(v_unit, mslot, item0, maxT_slot):
                k = 0
                for n in range(16):
                    if n == T_AT and maxT_slot is not None:
                        dve.wait_ge(s_("ring_full"), item0 + k + 1)
                        v.tensor_copy(mT[0:24, maxT_slot, :], ring_bank[k % 3][0:24, 0:P]).then_inc(s_("ring_read"), 1)
                        k += 1
                    dve.wait_ge(s_("ring_full"), item0 + k + 1)
                    v.reduce_max(mx[:, mslot, n // 2, n % 2:n % 2 + 1], ring_bank[k % 3], AX).then_inc(s_("ring_read"), 1)
                    k += 1
                if not isinstance(v_unit, int) or v_unit >= 2:
                    dve.wait_ge(s_("max_split"), v_unit - 1)
                dve.wait_ge(s_("ring_read"), item0 + k)
                v.tensor_tensor(rowmax[:, mslot, :], mx[:, mslot, :, 0], mx[:, mslot, :, 1], ALU.max)\
                    .then_inc(s_("max_ready"), 1)

            reduce_pass(0, 0, 0, None)
            reduce_pass(1, 1, 16, 0)

            def unit(i, s, last):
                u = 4 * i + s
                dve.wait_ge(s_(f"max_loaded{(s - 1) % 4}"), 16 * (i + (1 if s else 0)) + 16)
                if not (last and s >= 2):
                    reduce_pass(u + 2, s % 2, 33 + ITEMS * u, (s + 1) % 2)
                elif s == 2:
                    dve.wait_ge(s_("ring_full"), 33 + ITEMS * u + 1)
                    v.tensor_copy(mT[0:24, 1, :], ring_bank[0][0:24, 0:P]).then_inc(s_("ring_read"), 1)

            with dve.Fori(0, UNITS // 4 - 1) as i:
                for s in range(4):
                    unit(i, s, False)
            for s in range(4):
                unit(UNITS // 4 - 1, s, True)

            dve.wait_ge(s_("brow_done"), 1)
            v.tensor_copy(biasT[:, :], bank[0][:, 0:BROWS]).then_inc(s_("biasT_ready"), 1)
            dve.wait_ge(s_("o_loaded"), 6 * 16)
            ch(v.tensor_tensor(den[:, 0, :], den[:, 0, :], den[:, 1, :], ALU.add))
            v.reciprocal(den[:, 1, :], den[:, 0, :]).then_inc(s_("recip_ready"), 1)
            ch(v.tensor_tensor(o_par[:, 0, :], o_par[:, 0, :], o_par[:, 1, :], ALU.add))
            for c in range(NCH):
                dve.wait_ge(s_("recip_spread"), c + 1)
                v.tensor_tensor(onorm[:, c * CH:(c + 1) * CH], o_par[:, 0, c * CH:(c + 1) * CH], bank[c][:, :],
                                ALU.mult).then_inc(s_("onorm_ready"), 1)
            for gi in range(4):
                dve.wait_ge(s_("attn_done"), gi + 1)
                xg = xres[:, 4 * gi:4 * gi + 4, :]
                ch(v.tensor_tensor(xg, xg, bank[4 + gi][:, :].rearrange("p (t c) -> p t c", t=4), ALU.add))
                ln_start(dve, v, ch, 4 * gi, 4)
                if gi > 0:
                    ln_end(dve, v, ch, 4 * gi - 4, 4, gi, "x1_ready")
            ln_end(dve, v, ch, 12, 4, 4, "x1_ready")

            et = lambda ap: ap.rearrange("p e t -> p t e")
            over_e = lambda ap: ap.unsqueeze(1).to_broadcast([P, EXP, NT])
            lg, ls, ex, gates, t1, t2 = (R[n][:, :, :] for n in ("lg", "ls", "ex", "gates", "t1", "t2"))
            mask, incl, pos, keep, tw = (RW[n][:, :, :, :] for n in ("mask", "incl", "pos", "keep", "t"))
            dve.wait_ge(s_("logits_done"), 1)
            ch(v.tensor_copy(lg, bank[4][:, 0:NT * EXP].rearrange("p (t e) -> p e t", e=EXP)))
            ch(v.reduce_max(rt[:, 0, :], et(lg), AX))
            v.tensor_tensor(ls, lg, over_e(rt[:, 0, :]), ALU.subtract).then_inc(s_("logits_shifted"), 1)
            dve.wait_ge(s_("logits_shifted"), 1)
            ch(v.scalar_tensor_tensor(t1, ls, 0.0, rank[:, :, :], ALU.is_equal, ALU.mult))
            ch(v.reduce_max(rt[:, 1, :], et(t1), AX))
            ch(v.tensor_tensor(mask[:, 0], t1, over_e(rt[:, 1, :]), ALU.is_equal))
            ch(v.tensor_scalar(t2, ls, EXP_FLOOR, None, ALU.max))
            ch(v.scalar_tensor_tensor(t1, mask[:, 0], EXP_FLOOR, t2, ALU.mult, ALU.add))
            ch(v.reduce_max(rt[:, 2, :], et(t1), AX))
            ch(v.tensor_tensor(t2, t1, over_e(rt[:, 2, :]), ALU.is_equal))
            ch(v.tensor_tensor(t1, t2, rank[:, :, :], ALU.mult))
            ch(v.reduce_max(rt[:, 3, :], et(t1), AX))
            ch(v.tensor_tensor(mask[:, 1], t1, over_e(rt[:, 3, :]), ALU.is_equal))
            v.tensor_copy(mask_b[:, :, :, :], mask).then_inc(s_("mask_ready"), 1)
            dve.wait_ge(s_("gate_exp"), 1)
            ch(v.tensor_reduce(rt[:, 4, :], et(ex), AX, ALU.add))
            ch(v.reciprocal(rt[:, 5, :], rt[:, 4, :]))
            ch(v.tensor_tensor(gates, ex, over_e(rt[:, 5, :]), ALU.mult))
            dve.wait_ge(s_("places_done"), 1)
            wet = lambda ap: ap.rearrange("p (w e t) -> p w e t", w=2, e=EXP)
            flat = lambda ap: ap.rearrange("p w e t -> p (w e t)")
            ch(v.tensor_tensor_scan(flat(incl), carry[:, :], bank[6][:, 0:2 * EXP * NT], 0.0, ALU.mult, ALU.add))
            ch(v.tensor_tensor(tw, incl, wet(bank[6][:, 0:2 * EXP * NT]), ALU.subtract))
            ch(v.tensor_tensor(pos, tw, wet(bank[5][:, 0:2 * EXP * NT]), ALU.add))
            ch(v.tensor_scalar(cap1[:, :], incl[:, 0, :, NT - 1], float(CAP), None, ALU.min))
            ch(v.tensor_tensor(pos[:, 1], pos[:, 1], cap1[:, :].unsqueeze(2).to_broadcast([P, EXP, NT]), ALU.add))
            ch(v.scalar_tensor_tensor(flat(keep), flat(pos), float(CAP), flat(mask), ALU.is_lt, ALU.mult))
            ch(v.tensor_tensor(tw, pos, first[:, :, :, :], ALU.add))
            ch(v.tensor_tensor(tw, tw, keep, ALU.mult))
            wte = lambda ap: ap.rearrange("p w e t -> p w t e")
            ch(v.tensor_reduce(rt2[:, 0], wte(tw), AX, ALU.add))
            ch(v.tensor_reduce(rt2[:, 1], wte(keep), AX, ALU.add))
            ch(v.tensor_scalar(rt2[:, 2], rt2[:, 1], -1.0, 1.0, ALU.mult, ALU.add))
            ch(v.tensor_tensor(rt2[:, 2], rt2[:, 2], spill[:, :, :], ALU.mult))
            ch(v.tensor_tensor(rt2[:, 2], rt2[:, 2], rt2[:, 0], ALU.add))
            ch(v.tensor_copy(slot_i[:, 0], rt2[:, 2]))
            v.tensor_copy(slot_i[:, 1], rt2[:, 0]).then_inc(s_("slot_ready"), 1)
            for w in range(2):
                ch(v.tensor_tensor(tw[:, w], gates, keep[:, w], ALU.mult))
            ch(v.tensor_reduce(rt2[:, 3], wte(tw), AX, ALU.add))
            ch(v.tensor_tensor(rt[:, 0, :], rt2[:, 3, 0, :], rt2[:, 3, 1, :], ALU.add))
            ch(v.tensor_scalar(rt[:, 1, :], rt[:, 0, :], GATE_EPS, None, ALU.max))
            ch(v.reciprocal(rt[:, 2, :], rt[:, 1, :]))
            ch(v.tensor_tensor(rt2[:, 4], rt2[:, 3], rt[:, 2, :].unsqueeze(1).to_broadcast([P, 2, NT]), ALU.mult))

            dve.wait_ge(s_("acc_ready"), 1)
            for c in range(NCH):
                dve.wait_ge(s_("shared_down"), c + 1)
                ag = acc[:, 4 * c:4 * c + 4, :]
                v.scalar_tensor_tensor(ag, bank[4 + c][:, :].rearrange("p (t c) -> p t c", t=4), SHARED_SCALE, ag,
                                       ALU.mult, ALU.add).then_inc(s_("shared_done"), 1)

            def copy_xeT(e, s, i):
                dve.wait_ge(s_("xeT_done"), e + 1)
                v.tensor_copy(xeT[:, s, :], pair[0][:, 0:CAP]).then_inc(s_("xeT_ready"), 1)

            def expert_out(e, s, i):
                dve.wait_ge(s_("ye_done"), e + 2)
                dve.wait_ge(s_(f"ye_stored{s}"), 16 * i + 16)
                v.tensor_tensor(yer[:, s, :, :], pair[3][:, 0:CAP].rearrange("p (t c) -> p t c", t=ST),
                                b2all[:, bass.ds(e, 1), :].to_broadcast([P, ST, C]), ALU.add).then_inc(s_("ye_ready"), 1)

            dve.wait_ge(s_("shared_done"), NCH)
            dve.sem_inc(s_("ye_ready"), 1)
            copy_xeT(0, 0, 0)
            with dve.Fori(0, EXP // 2 - 1) as i:
                for s in range(2):
                    copy_xeT(2 * i + s + 1, 1 - s, i)
                    expert_out(2 * i + s, s, i)
            copy_xeT(EXP - 1, 1, 0)
            expert_out(EXP - 2, 0, EXP // 2 - 1)
            expert_out(EXP - 1, 1, EXP // 2 - 1)

            for gi in range(4):
                dve.wait_ge(s_(f"picked{gi}"), 8 * 16)
                for w in range(2):
                    for t in range(4 * gi, 4 * gi + 4):
                        dst = acc if w == 0 else xres
                        ch.mark(v.scalar_tensor_tensor(dst[:, t, :], picked[:, w, t, :], rt2[:, 4, w, t:t + 1], acc[:, t, :],
                                                       ALU.mult, ALU.add))
                    ch.wait()
                ln_start(dve, v, ch, 4 * gi, 4)
                if gi > 0:
                    ln_end(dve, v, ch, 4 * gi - 4, 4, 4 + gi, "x2_ready")
            ln_end(dve, v, ch, 12, 4, 8, "x2_ready")

            dve.wait_ge(s_("mixer_loaded"), 6 * 16)
            for q in range(B * DT):
                dve.wait_ge(s_("last_tap"), q + 1)
                for j in range(1, TAPS):
                    ins = v.scalar_tensor_tensor(uu[:, q, j:L], pair[q % 2][:, 0:L - j],
                                                 convw[:, q % DT, TAPS - 1 - j:TAPS - j], uu[:, q, j:L], ALU.mult, ALU.add)
                    if j < TAPS - 1:
                        ch(ins)
                ins.then_inc(s_("taps_done"), 1)
            v.tensor_scalar(alog[:, :, :], alog[:, :, :], LOG_RATE_MAX, None, ALU.min).then_inc(s_("a_clamped"), 1)
            dve.wait_ge(s_("a_exp"), 1)
            v.tensor_scalar(alog[:, :, :], alog[:, :, :], -1.0, None, ALU.mult).then_inc(s_("a_ready"), 1)
            for b in range(B):
                sl = slice(b * L, (b + 1) * L)
                dve.wait_ge(s_("bc_1"), b + 1)
                v.tensor_tensor(bc_r[0:96, sl], pair[b][0:96, :], bc_parts[0:96, sl], ALU.subtract).then_inc(s_("bc_rest"), 1)
                dve.wait_ge(s_("bc_2"), b + 1)
                dve.wait_ge(s_("bc_rest"), b + 1)
                ch.mark(v.tensor_copy(bc_parts[32:64, sl], bc_p2[32:64, sl]))
                v.tensor_tensor(bc_parts[64:96, sl], bc_r[64:96, sl], bc_p2[64:96, sl], ALU.subtract)\
                    .then_inc(s_("bc_ready"), 1)
            ch.wait()
            for q in range(B * DT):
                bias = biasT[:, BDT_ROW + q % 2:BDT_ROW + q % 2 + 1]
                dve.wait_ge(s_("sp_abs"), q + 1)
                v.tensor_scalar(delta[:, q, :], pair[2 + q % 2][:, :], bias, 0.0, ALU.add, ALU.max).then_inc(s_("sp_relu"), 1)
                dve.wait_ge(s_("sp_exp"), q + 1)
                v.tensor_scalar(sp_w[:, q, :], du[:, q, :], 1.0, None, ALU.add).then_inc(s_("sp_w_ready"), 1)
                dve.wait_ge(s_("sp_w_ready"), q + 1)
                v.scalar_tensor_tensor(du[:, q, :], sp_w[:, q, :], -1.0, du[:, q, :], ALU.add, ALU.subtract)\
                    .then_inc(s_("sp_c"), 1)
            dve.wait_ge(s_("sp_relu"), B * DT)
            for q in range(B * DT):
                dve.wait_ge(s_("sp_small"), q + 1)
                v.tensor_tensor(delta[:, q, :], delta[:, q, :], sp_l[:, q, :], ALU.add).then_inc(s_("delta_ready"), 1)
                dve.wait_ge(s_("delta_ready"), q + 1)
                v.tensor_tensor(du[:, q, :], delta[:, q, :], uu[:, q, :], ALU.mult).then_inc(s_("du_ready"), 1)
            dve.wait_ge(s_("du_ready"), B * DT)

            dve.sem_inc(s_("h_ready"), CREDIT)
            dve.sem_inc(s_("hc_ready"), CREDIT)
            dve.sem_inc(s_("y_read"), 1)
            with dve.Fori(0, B) as bb:
                for n in range(ST_N):
                    U = CREDIT + PER_B * bb + DT * n + 1
                    at = DT * (n % 2)
                    for d in range(DT):
                        dve.wait_ge(s_("dA_ready"), U + d)
                        dve.wait_ge(s_("dBu_ready"), U + d)
                        dve.wait_ge(s_("y_added"), U + d - 4)
                        v.tensor_tensor_scan(hh[:, at + d, :], dA[:, d, :], dBu[:, d, :], 0.0, ALU.mult, ALU.add)\
                            .then_inc(s_("h_ready"), 1)
                    for d in range(DT):
                        dve.wait_ge(s_("h_ready"), U + d)
                        if d == 0:
                            dve.wait_ge(s_("c_ready"), ST_N * bb + n + 1)
                        v.tensor_tensor(hh[:, at + d, :], hh[:, at + d, :], pair[1][:, :], ALU.mult)\
                            .then_inc(s_("hc_ready"), 1)
                for d in range(DT):
                    gg = DT * bb + d
                    dve.wait_ge(s_("y_added"), CREDIT + PER_B * (bb + 1))
                    v.scalar_tensor_tensor(one(uu, gg), one(uu, gg), biasT[:, D_ROW + d:D_ROW + d + 1], pair[2 + d][:, :],
                                           ALU.mult, ALU.add).then_inc(s_("y_read"), 1)
                    dve.wait_ge(s_("y_read"), gg + 2)
                    v.tensor_tensor(one(gate, gg), one(gate, gg), one(uu, gg), ALU.mult).then_inc(s_("y_ready"), 1)
            for gi in range(4):
                dve.wait_ge(s_("mixer_out"), gi + 1)
                xg = xres[:, 4 * gi:4 * gi + 4, :]
                ch(v.tensor_tensor(xg, xg, bank[gi][:, :].rearrange("p (t c) -> p t c", t=4), ALU.add))
                ln_start(dve, v, ch, 4 * gi, 4)
                if gi > 0:
                    ln_end(dve, v, ch, 4 * gi - 4, 4, 8 + gi, "x3_ready")
            ln_end(dve, v, ch, 12, 4, 12, "x3_ready")

            dve.wait_ge(s_("net_loaded"), NET_LOADS * 16)
            ch.mark(v.tensor_copy(gw3b[:, :], gw[2][:, 0:1].to_broadcast([32, P])))
            ch.mark(v.tensor_copy(w4b[:, :], cw4[:, 0:1].to_broadcast([P, P])))
            ch(v.tensor_scalar(cb4[:, :], cb4[:, :], 0.5, None, ALU.mult))
            v.tensor_scalar(gb3[:, :], gb3[:, :], 0.5, None, ALU.mult).then_inc(s_("halves_ready"), 1)
            for b in range(B):
                dve.wait_ge(s_("state_ready"), 2 * b + 2)
                ch(v.tensor_reduce(gmean[:, 0, b:b + 1], xT[:, b * L:(b + 1) * L], AX, ALU.add))
            v.tensor_scalar(gmean[:, 1, :], gmean[:, 0, :], 1.0 / L, None, ALU.mult).then_inc(s_("mean_ready"), 1)
            dve.wait_ge(s_("global_act"), 3)
            ch(v.tensor_scalar(c_in[:, 0, :], gf[:, :], 0.7, None, ALU.mult))
            ch(v.tensor_scalar(c_in[:, 1, :], c_in[:, 0, :], rng[:, :], 0.1, ALU.mult, ALU.add))
            ch(v.tensor_scalar(c_in[:, 2, :], c_in[:, 1, :], sgn[:, :], None, ALU.mult))
            ch(v.tensor_scalar(c_in[:, 3, 0:1], rng[:, :], sgn[:, :], 0.3, ALU.mult, ALU.mult))
            with dve.Fori(0, CYCLES) as i:
                for c in range(NCH):
                    dve.wait_ge(s_("net_act"), NET_STEPS * i + 7 + c + 1)
                    v.tensor_scalar(cpl[:, c, :], tf[:, c, :], c_in[:, 3, 0:1], c_in[:, 2, c // 2:c // 2 + 1],
                                    ALU.mult, ALU.add).then_inc(s_("cpl_ready"), 1)
                    dve.wait_ge(s_("cpl_ready"), NCH * i + c + 1)
                    dve.wait_ge(s_(f"twisted{c}"), 64 * (i + 1))
                    v.tensor_tensor(prod[:, c, :], cpl[:, c, :], tw_in[:, c, :], ALU.mult).then_inc(s_("prod_ready"), 1)
                    dve.wait_ge(s_("prod_ready"), NCH * i + c + 1)
                    xc = xT[:, c * CH:(c + 1) * CH]
                    v.tensor_tensor(xc, xc, prod[:, c, :], ALU.add).then_inc(s_("state_ready"), 1)
            for gi in range(4):
                dve.wait_ge(s_("back_done"), gi + 1)
                xg = xres[:, 4 * gi:4 * gi + 4, :]
                ch(v.tensor_tensor(xg, xg, bank[gi][:, :].rearrange("p (t c) -> p t c", t=4), ALU.add))
                ln_start(dve, v, ch, 4 * gi, 4)
                if gi > 0:
                    ln_end(dve, v, ch, 4 * gi - 4, 4, 12 + gi, "x4_ready")
            ln_end(dve, v, ch, 12, 4, 16, "x4_ready")

        @block.tensor
        def _(pe):
            t = nc.tensor
            pe.wait_ge(s_("ident_ready"), 1)
            pe.wait_ge(s_("x_loaded"), 32)
            for c in range(NCH):
                for k in range(4):
                    last = t.transpose(bank[c][:, k * P:(k + 1) * P], xres[:, 4 * c + k, :], ident[:])
                last.then_inc(s_("xT_done"), 1)
            pe.wait_ge(s_("wcos_ready"), 1)
            t.transpose(bank[4][:, 0:P], wtmp[:, 2, :], ident[:]).then_inc(s_("wcosT_done"), 1)
            pe.wait_ge(s_("basis_loaded"), 4 * 16)
            pe.wait_ge(s_("wcosT_copied"), 1)
            for j in range(4):
                last = t.matmul(bank[4 + j][:, 256:256 + C], basis[32 * j:32 * j + 32, :], wcosT[32 * j:32 * j + 32, :],
                                start=True, stop=True)
            last.then_inc(s_("weff_done"), 1)
            pe.wait_ge(s_("xT_copied_a"), 2)
            pe.wait_ge(s_("xT_copied_v"), 2)
            pe.wait_ge(s_("weff_copied"), 4)
            for b in range(B):
                for w in range(2):
                    for c in (2 * b, 2 * b + 1):
                        t.matmul(bank[4 * w + c][:, :], weff[:, w, :], xT[:, c * CH:(c + 1) * CH], start=True, stop=True)\
                            .then_inc(s_("qk_done"), 1)
            for c in range(NCH):
                pe.wait_ge(s_("resid_done"), (2, 2, 6, 6)[c])
                for k in range(4):
                    tt = 4 * c + k
                    last = t.matmul(bank[c][:, k * P:(k + 1) * P], xT[:, tt * P:(tt + 1) * P], weff[:, 2, :],
                                    start=True, stop=True)
                last.then_inc(s_("v_done"), 1)

            pe.sem_inc(s_("probs_free"), NPROB)
            pe.sem_inc(s_("st_done"), 1)
            pe.wait_ge(s_("resid_done"), 8)
            pe.wait_ge(s_("v_copied"), 4)

            def ring_wait(item0, k):
                if isinstance(item0, int) and item0 == 0:
                    if k >= 3:
                        pe.wait_ge(s_("ring_read"), k - 2)
                else:
                    pe.wait_ge(s_("ring_read"), item0 + (k - 2 if k >= 3 else 0))

            def s_half(slot, n, item0, k):
                ring_wait(item0, k)
                t.matmul(ring_bank[k % 3], qbuf[0:96, slot, (n // 2) * P:(n // 2 + 1) * P],
                         kbuf[0:96, slot, (n % 2) * CH:(n % 2 + 1) * CH], start=True, stop=True).then_inc(s_("ring_full"), 1)

            def max_T(m, mslot, item0, k):
                pe.wait_ge(s_("max_split"), m + 1)
                ring_wait(item0, k)
                t.matmul(ring_bank[k % 3][0:24, 0:P], mparts[:, mslot, :], ident_b[:], start=True, stop=True)\
                    .then_inc(s_("ring_full"), 1)

            def st_half(slot, kt, h):
                return t.matmul(st_pair[kt % 2][:, h * CH:(h + 1) * CH], kbuf[0:99, slot, kt * P:(kt + 1) * P],
                                qbuf[0:99, slot, h * CH:(h + 1) * CH], start=True, stop=True)

            def score_pass(v, slot, item0, maxT_slot):
                k = 0
                pe.wait_ge(s_(f"unit_loaded{slot}"), 32)
                for n in range(16):
                    if n == T_AT and maxT_slot is not None:
                        max_T(v - 1, maxT_slot, item0, k)
                        k += 1
                    s_half(slot, n, item0, k)
                    k += 1

            pe.wait_ge(s_("qk_cleared"), 1)
            score_pass(0, 0, 0, None)
            score_pass(1, 1, 16, 0)
            pe.wait_ge(s_("max_loaded0"), 16 + 16)
            for kt in range(2):
                for h in range(2):
                    last = st_half(0, kt, h)
                last.then_inc(s_("st_done"), 1)

            def unit(i, s, last):
                u = 4 * i + s
                item0 = 33 + ITEMS * u
                v_slot, u1_slot = (s + 2) % 4, (s + 1) % 4
                scores = not (last and s >= 2)
                if scores:
                    pe.wait_ge(s_(f"unit_loaded{v_slot}"), 32 * (i + (1 if s < 2 else 2)))
                k = 0
                for j in range(KT):
                    for h in range(2):
                        n = 2 * j + h
                        if n == T_AT and not (last and s == 3):
                            max_T(u + 1, (s + 1) % 2, item0, k)
                            k += 1
                        if scores:
                            s_half(v_slot, n, item0, k)
                            k += 1
                        if last and s == 3 and j >= KT - 2:
                            continue
                        if h == 0:
                            if j == KT - 2:
                                pe.wait_ge(s_(f"max_loaded{u1_slot}"), 16 * (i + (1 if s < 3 else 2)) + 16)
                            pe.wait_ge(s_("exp_done"), KT * u + j + 1)
                        ins = st_half(s if j < KT - 2 else u1_slot, (j + 2) % KT, h)
                        if h == 1:
                            ins.then_inc(s_("st_done"), 1)
                    if j % 2 == 0:
                        continue
                    if j == 1:
                        pe.wait_ge(s_("v_staged"), u + 1)
                        pe.wait_ge(s_("pv_copied"), u + 1)
                    pe.wait_ge(s_("exp_done"), KT * u + j + 1)
                    for kt in (j - 1, j):
                        for h in range(2):
                            g = 2 * (kt % 2) + h
                            ins = t.matmul(pv_bank[32 * g:32 * g + 32, :], vst[:, s % 2, kt, :],
                                           probs[:, kt % NPROB, h * CH:(h + 1) * CH], start=kt < 2, stop=kt >= KT - 2)
                    ins.then_inc(s_("probs_free"), 2)

            with pe.Fori(0, UNITS // 4 - 1) as i:
                for s in range(4):
                    unit(i, s, False)
            for s in range(4):
                unit(UNITS // 4 - 1, s, True)

            pe.wait_ge(s_("brow_loaded"), 6 * 16)
            t.transpose(bank[0][:, 0:BROWS], brow[:, :], ident[0:BROWS, 0:BROWS]).then_inc(s_("brow_done"), 1)
            pe.wait_ge(s_("recip_ready"), 1)
            pe.wait_ge(s_("expand_ready"), 1)
            pe.wait_ge(s_("biasT_ready"), 1)
            pe.wait_ge(s_("pv_copied"), UNITS + 1)
            for c in range(NCH):
                for k in range(2):
                    last = t.matmul(bank[c][:, k * (L // 4):(k + 1) * (L // 4)], expand[:, 2 * (c % 2) + k, c // 2, :],
                                    den[:, 1, :], start=True, stop=True)
                last.then_inc(s_("recip_spread"), 1)
            for c in range(NCH):
                pe.wait_ge(s_("onorm_ready"), c + 1)
                for k in range(4):
                    last = t.matmul(bank[4 + c][:, k * P:(k + 1) * P], onorm[:, (4 * c + k) * P:(4 * c + k + 1) * P],
                                    weff[:, 3, :], start=True, stop=True)
                last.then_inc(s_("attn_done"), 1)

            for c in range(NCH):
                pe.wait_ge(s_("x1_ready"), 4 * c + 4)
                for k in range(4):
                    last = t.transpose(bank[c][:, k * P:(k + 1) * P], xres[:, 4 * c + k, :], ident[:])
                last.then_inc(s_("x1T_done"), 1)
            pe.wait_ge(s_("ffn_loaded"), 5 * 16)
            for c in range(NCH):
                pe.wait_ge(s_("x1T_copied"), c + 1)
                for tt in range(4 * c, 4 * c + 4):
                    last = t.matmul(bank[4][:, tt * EXP:(tt + 1) * EXP], xT[:, tt * P:(tt + 1) * P], rw[:, :],
                                    start=True, stop=True)
            last.then_inc(s_("logits_done"), 1)

            def shared_up(c):
                for f in range(FT):
                    if c > 0:
                        pe.wait_ge(s_("shared_act"), (c - 1) * FT + f + 1)
                    t.matmul(bank[f][:, :], sw1[:, f * P:(f + 1) * P], xT[:, c * CH:(c + 1) * CH], start=True, stop=True)\
                        .then_inc(s_("shared_up"), 1)

            def shared_down(c):
                pe.wait_ge(s_("shared_act"), (c + 1) * FT)
                for k in range(4):
                    for f in range(FT):
                        last = t.matmul(bank[4 + c][:, k * C:(k + 1) * C], hsT[:, c % 2, f, k * P:(k + 1) * P], sw2[:, f, :],
                                        start=f == 0, stop=f == FT - 1)
                last.then_inc(s_("shared_down"), 1)

            shared_up(0)
            pe.wait_ge(s_("mask_ready"), 1)
            mb = mask_b[:, :, :, :].rearrange("p w e t -> p (w e t)")
            t.matmul(bank[5][:, 0:2 * EXP * NT], before[:, :], mb, start=True, stop=True)
            t.matmul(bank[6][:, 0:2 * EXP * NT], ones_b[:, :], mb, start=True, stop=True).then_inc(s_("places_done"), 1)
            shared_up(1)
            pe.wait_ge(s_("slot_ready"), 1)
            shared_down(0)
            for c in range(1, NCH):
                if c + 1 < NCH:
                    shared_up(c + 1)
                shared_down(c)

            def slots_T(s, count):
                pe.wait_ge(s_(f"slots_loaded{s}"), count)
                for k in range(ST):
                    last = t.transpose(pair[0][:, k * P:(k + 1) * P], xer[:, s, k, :], ident[:])
                last.then_inc(s_("xeT_done"), 1)

            def expert(i, s, last_e):
                e = 2 * i + s
                pe.wait_ge(s_("xeT_ready"), e + 1)
                pe.wait_ge(s_(f"expert_loaded{s}"), 32 * (i + 1))
                for f in range(FT):
                    pe.wait_ge(s_("up_act"), FT * e + f + 2)
                    for h in range(2):
                        last = t.matmul(pair[1 + f % 2][:, h * CH:h * CH + CAP // 2], w1r[:, s, f * P:(f + 1) * P],
                                        xeT[:, s, h * (CAP // 2):(h + 1) * (CAP // 2)], start=True, stop=True)
                    last.then_inc(s_("up_done"), 1)
                if not last_e:
                    slots_T(1 - s, 16 * (i + 1 + s))
                pe.wait_ge(s_("up_act"), FT * (e + 1) + 3)
                pe.wait_ge(s_("ye_ready"), e + 1)
                for k in range(ST):
                    for f in range(FT):
                        last = t.matmul(pair[3][:, k * C:(k + 1) * C], hT[:, f, k * P:(k + 1) * P], w2r[:, s, f, :],
                                        start=f == 0, stop=f == FT - 1)
                last.then_inc(s_("ye_done"), 1)

            pe.wait_ge(s_("shared_act"), NCH * FT)
            pe.wait_ge(s_("shared_done"), NCH)
            pe.sem_inc(s_("up_act"), 3)
            pe.sem_inc(s_("ye_done"), 1)
            slots_T(0, 16)
            with pe.Fori(0, EXP // 2 - 1) as i:
                for s in range(2):
                    expert(i, s, False)
            for s in range(2):
                expert(EXP // 2 - 1, s, s == 1)

            pe.wait_ge(s_("ye_ready"), EXP + 1)
            for c in range(NCH):
                pe.wait_ge(s_("x2_ready"), 4 * c + 4)
                for k in range(4):
                    last = t.transpose(bank[c][:, k * P:(k + 1) * P], xres[:, 4 * c + k, :], ident[:])
                last.then_inc(s_("x2T_done"), 1)
            pe.wait_ge(s_("mixer_loaded"), 6 * 16)
            pe.wait_ge(s_("x2T_copied"), NCH)
            for q in range(B * DT):
                b, d = q // DT, q % DT
                if q >= 2:
                    pe.wait_ge(s_("taps_done"), q - 1)
                for h in range(2):
                    last = t.matmul(bank[2 * (q % 2) + h][:, :], win[:, d * P:(d + 1) * P],
                                    xT[:, b * L + h * CH:b * L + (h + 1) * CH], start=True, stop=True)
                last.then_inc(s_("u_in_done"), 1)
                if q >= 2:
                    pe.wait_ge(s_("gate_ready"), q - 1)
                for h in range(2):
                    last = t.matmul(bank[4 + 2 * (q % 2) + h][:, :], win[:, DIN + d * P:DIN + (d + 1) * P],
                                    xT[:, b * L + h * CH:b * L + (h + 1) * CH], start=True, stop=True)
                last.then_inc(s_("gate_done"), 1)
            pe.wait_ge(s_("wx3_ready"), 1)
            for b in range(B):
                pe.wait_ge(s_("u_ready"), 4 if b else 3)
                for h in range(2):
                    for d in range(DT):
                        last = t.matmul(bank[2 * b + h][0:104, :], wx3[:, d, :], uu[:, DT * b + d, h * CH:(h + 1) * CH],
                                        start=d == 0, stop=d == DT - 1)
                last.then_inc(s_("bc_done"), 1)
            for q in range(B * DT):
                b, d = q // DT, q % DT
                pe.wait_ge(s_("low_ready"), b + 1)
                if q < 2:
                    pe.wait_ge(s_("gate_ready"), 3 + q)
                else:
                    pe.wait_ge(s_("sp_relu"), q - 1)
                for h in range(2):
                    last = t.matmul(bank[4 + 2 * (q % 2) + h][:, :], wdt[96:96 + RANK, d * P:(d + 1) * P],
                                    low[96:96 + RANK, b * L + h * CH:b * L + (h + 1) * CH], start=True, stop=True)
                last.then_inc(s_("delta_done"), 1)

            pe.wait_ge(s_("bc_ready"), B)
            pe.wait_ge(s_("delta_ready"), B * DT)
            pe.sem_inc(s_("y_added"), CREDIT)
            with pe.Fori(0, B) as bb:
                def spread(row, dst, h):
                    return t.matmul(dst[:, h * CH:(h + 1) * CH], sel[:, row, :],
                                    bc_parts[0:96, bass.ds(bb * L + h * CH, CH)], start=True, stop=True)

                def spread_b(n):
                    pe.wait_ge(s_("b_copied"), CREDIT + ST_N * bb + n)
                    for h in range(2):
                        ins = spread(n, pair[0], h)
                    ins.then_inc(s_("b_ready"), 1)

                def add_y(n):
                    for d in range(DT):
                        pe.wait_ge(s_("hc_ready"), CREDIT + PER_B * bb + DT * n + d + 1)
                        for h in range(2):
                            ins = t.matmul(pair[2 + d][:, h * CH:(h + 1) * CH], ident[:], hh[:, DT * (n % 2) + d, h * CH:(h + 1) * CH],
                                           start=n == 0, stop=n == ST_N - 1)
                        ins.then_inc(s_("y_added"), 1)

                spread_b(0)
                for n in range(ST_N):
                    if n + 1 < ST_N:
                        spread_b(n + 1)
                    pe.wait_ge(s_("hc_ready"), CREDIT + PER_B * bb + DT * n)
                    for h in range(2):
                        ins = spread(ST_N + n, pair[1], h)
                    ins.then_inc(s_("c_ready"), 1)
                    if n == 1:
                        pe.wait_ge(s_("y_read"), DT * bb + 1)
                    if n > 0:
                        add_y(n - 1)
                add_y(ST_N - 1)
            pe.wait_ge(s_("y_ready"), B * DT)
            for c in range(NCH):
                for k in range(4):
                    at = (c % 2) * CH + k * P
                    for d in range(DT):
                        last = t.matmul(bank[c][:, k * P:(k + 1) * P], gate[:, DT * (c // 2) + d, at:at + P], wout[:, d, :],
                                        start=d == 0, stop=d == DT - 1)
                last.then_inc(s_("mixer_out"), 1)

            for c in range(NCH):
                pe.wait_ge(s_("x3_ready"), 4 * c + 4)
                for k in range(4):
                    last = t.transpose(bank[c][:, k * P:(k + 1) * P], xres[:, 4 * c + k, :], ident[:])
                last.then_inc(s_("x3T_done"), 1)
            pe.wait_ge(s_("net_loaded"), NET_LOADS * 16)
            pe.wait_ge(s_("mean_ready"), 1)
            t.matmul(bank[4][0:64, 0:B], gw[0][:, :], gmean[:, 1, :], start=True, stop=True).then_inc(s_("global_mm"), 1)
            pe.wait_ge(s_("global_act"), 1)
            t.matmul(bank[5][0:32, 0:B], gw[1][:, :], g1[:, :], start=True, stop=True).then_inc(s_("global_mm"), 1)
            pe.wait_ge(s_("global_act"), 2)
            t.matmul(bank[6][:, 0:B], gw3b[:, :], g2[:, :], start=True, stop=True).then_inc(s_("global_mm"), 1)
            pe.wait_ge(s_("global_act"), 3)
            with pe.Fori(0, CYCLES) as i:
                for c in range(NCH):
                    pe.wait_ge(s_("state_ready"), NCH * i + c + 1)
                    t.matmul(bank[c][:, :], cw1[:, :], xT[:, c * CH:(c + 1) * CH], start=True, stop=True)\
                        .then_inc(s_("net_mm"), 1)
                for c in range(NCH):
                    pe.wait_ge(s_("net_act"), NET_STEPS * i + c + 1)
                    at = 64 * (c % 2)
                    last = t.matmul(bank[4 + c // 2][at:at + 64, :], cw2[:, :], m1[:, c, :], start=True, stop=True)
                    if c % 2 == 1:
                        last.then_inc(s_("net_mm"), 1)
                pe.wait_ge(s_("net_act"), NET_STEPS * i + 4 + 2)
                pe.sem_inc(s_("layer3_begun"), 1)
                for c in range(NCH):
                    at = 64 * (c % 2)
                    last = t.matmul(bank[6][32 * c:32 * c + 32, :], cw3[at:at + 64, :], m2[at:at + 64, c // 2, :],
                                    start=True, stop=True)
                last.then_inc(s_("net_mm"), 1)
                pe.wait_ge(s_("net_act"), NET_STEPS * i + 7)
                for c in range(NCH):
                    t.matmul(bank[c][:, :], w4b[32 * c:32 * c + 32, :], m3[32 * c:32 * c + 32, :], start=True, stop=True)\
                        .then_inc(s_("net_mm"), 1)
            pe.wait_ge(s_("net_act"), NET_STEPS * CYCLES)
            for c in range(NCH):
                pe.wait_ge(s_("state_ready"), NCH * CYCLES + c + 1)
                for k in range(4):
                    last = t.transpose(bank[c][:, k * P:(k + 1) * P], xT[:, c * CH + k * P:c * CH + (k + 1) * P], ident[:])
                last.then_inc(s_("back_done"), 1)


_INS = ["L0_attn_x"] + [f"L0_attn_{w}_{j}" for j in "qkvo" for w in ("basis", "phase", "amp")]
_INS += [f"L0_ffn_{n}" for n in ("router_w", "w1", "b1", "w2", "b2", "sw1", "sb1", "sw2", "sb2")]
_INS += [f"L1_attn_{n}" for n in ("W_in", "conv_w", "conv_b", "W_x", "W_dt", "b_dt", "A_log", "D", "W_out")]
_INS += [f"L1_ffn_cn_{w}{j}" for j in (1, 2, 3, 4) for w in "wb"] + [f"L1_ffn_gc_{w}{j}" for j in (1, 2, 3) for w in "wb"]
_INS += ["L1_ffn_adaptive_range"]
_OUTS = [((B, L, C), "float32")]


def kernel(**inputs):
    import numpy as np
    import concourse.bacc as bacc
    from concourse.bass_utils import run_bass_kernel_spmd

    nc = bacc.Bacc("TRN2", target_bir_lowering=False, num_devices=1)
    arrays = {f"in_{n}": np.ascontiguousarray(inputs[n]) for n in _INS}
    a = {n: nc.dram_tensor(f"in_{n}", arrays[f"in_{n}"].shape, mybir.dt.from_np(arrays[f"in_{n}"].dtype),
                           kind="ExternalInput").ap() for n in _INS}
    shape, dtype = _OUTS[0]
    out = nc.dram_tensor("out_0", shape, mybir.dt.from_np(np.dtype(dtype)), kind="ExternalOutput").ap()
    build(nc, a, out)
    r = run_bass_kernel_spmd(nc, [arrays], core_ids=[0])
    return r.results[0]["out_0"]
```

```python
from contextlib import ExitStack

import concourse.bass as bass
from concourse import mybir

F32 = mybir.dt.float32
BF16 = mybir.dt.bfloat16
I32 = mybir.dt.int32
ALU = mybir.AluOpType
ACT = mybir.ActivationFunctionType
AX = mybir.AxisListType.X

P = 128
B, L, C = 2, 1024, 128
NTOK = B * L
NT = NTOK // P
CH = 512
NCH = NTOK // CH
HEADS, HD, HARM = 16, 8, 32
UNITS = B * HEADS
ROWS = 9 * HD
KT = L // P
SCALE = HD ** -0.5
EPS = 1e-5
TWO_PI = 6.283185307179586
PI_HI = 6.28125
PI_MID = 0.0019350051879882812
PI_LO = TWO_PI - PI_HI - PI_MID
ROUND = 12582912.0
EXP, FF, CAP = 8, 512, 640
FT, ST = FF // P, CAP // P
SLOTS = EXP * CAP
SHARED_SCALE = 0.1
EXP_FLOOR = -87.3
GATE_EPS = 1.1920929e-07
DIN, ST_N, TAPS, RANK = 256, 16, 4, 8
DT = DIN // P
PER_B = DT * ST_N
CREDIT = 4
LOG_RATE_MAX = 80.0
CYCLES = 3
NET_LOADS = 22
NET_STEPS = 11
ARENA = 31 * 1024
B1_ROW, SB1_ROW, CONVB_ROW, BDT_ROW, D_ROW, CNB1_ROW, BROWS = 0, 32, 36, 38, 40, 42, 43
NPROB = 4
ITEMS, T_AT = 17, 4
MAXT_READ = 16 + T_AT + 1
LAST_READ = 16 + ITEMS + ITEMS * (UNITS - 2) + 1


class Chain:

    def __init__(self, eng, sem):
        self.eng, self.sem, self.n = eng, sem, 0

    def __call__(self, ins):
        self.mark(ins)
        self.wait()

    def mark(self, ins):
        ins.then_inc(self.sem, 1)
        self.n += 1
        return ins

    def wait(self):
        self.eng.wait_ge(self.sem, self.n)


def build(nc, a, out):
    ctx = ExitStack()
    with ctx:
        def sb(name, shape, dt=F32):
            return ctx.enter_context(nc.sbuf_tensor(name, shape, dt))

        def sem(name):
            return ctx.enter_context(nc.semaphore(name))

        def dram(name, shape, dt=F32):
            return nc.dram_tensor(name, shape, dt, kind="Internal").ap()

        pair = [ctx.enter_context(nc.psum_tensor(f"pair{i}", [P, 2 * CH], F32)) for i in range(4)]
        bank = [pair[i // 2][:, (i % 2) * CH:(i % 2 + 1) * CH] for i in range(8)]
        ring_bank, pv_bank, st_pair = bank[0:3], bank[3], pair[2:4]

        q_parts_d = dram("q_parts_d", [UNITS, 3, HD, L], BF16)
        k_parts_d = dram("k_parts_d", [UNITS, HD, 3, L], BF16)
        head_out_d = dram("head_out_d", [UNITS, 2, HD + 1, L])

        slot_x_d = dram("slot_x_d", [SLOTS + NTOK, C + 1])
        picked_d = dram("picked_d", [2 * NTOK + SLOTS, C])

        brow = sb("brow", [BROWS, P])
        biasT = sb("biasT", [P, BROWS])
        zero = sb("zero", [P, SLOTS // P // 4 * (C + 1)])
        ident = sb("ident", [P, P])
        ident_b = sb("ident_b", [P, P], BF16)
        xnum = sb("xnum", [P, NT, C + 1])
        xres = xnum[:, :, 0:C]
        xT = sb("xT", [P, NTOK])
        wph = sb("wph", [P, 4, HARM])
        wam = sb("wam", [P, 4, HARM])
        wtmp = sb("wtmp", [P, 3, P])
        basis = sb("basis", [P, C])
        wcosT = sb("wcosT", [P, P])
        weff = sb("weff", [P, 4, C])
        expand = sb("expand", [P, B * 4, P])
        AR = sb("arena", [P, ARENA])
        used = [0]

        def ar(nfloat):
            at = used[0]
            used[0] += nfloat
            assert used[0] <= ARENA, used[0]
            return AR[:, at:at + nfloat]

        q_split = ar(3 * NTOK // 2).bitcast(BF16).rearrange("p (a n) -> p a n", a=3)
        k_split = ar(3 * NTOK // 2).bitcast(BF16).rearrange("p (a n) -> p a n", a=3)
        resid = ar(NTOK).rearrange("p (c n) -> p c n", c=4)
        vtok = ar(NT * HEADS * HD).rearrange("p (b h k d) -> p b h k d", b=B, h=HEADS, k=KT)
        qbuf = ar(4 * L // 2).bitcast(BF16).rearrange("p (s n) -> p s n", s=4)
        kbuf = ar(4 * L // 2).bitcast(BF16).rearrange("p (s n) -> p s n", s=4)
        probs = ar(NPROB * L).rearrange("p (s n) -> p s n", s=NPROB)
        vst = ar(2 * KT * 32).rearrange("p (s k m) -> p s k m", s=2, k=KT)
        pvs = ar(2 * CH).rearrange("p (s n) -> p s n", s=2)
        mx = ar(2 * 16).rearrange("p (s t h) -> p s t h", s=2, t=KT)
        rowmax = ar(2 * 8).rearrange("p (s n) -> p s n", s=2)
        neg1 = ar(8)
        mneg = ar(4 * 8).rearrange("p (s n) -> p s n", s=4)
        mparts = ar(2 * 12).bitcast(BF16).rearrange("p (s n) -> p s n", s=2)
        mT = ar(2 * 64).bitcast(BF16).rearrange("p (s n) -> p s n", s=2)
        used[0] = 0
        o_par = ar(2 * NTOK).rearrange("p (s n) -> p s n", s=2)
        den = ar(2 * L // 4).rearrange("p (s n) -> p s n", s=2)
        onorm = ar(NTOK)

        used[0] = 7 * NTOK
        acc = ar(NTOK).rearrange("p (t c) -> p t c", t=NT)
        picked = ar(2 * NTOK).rearrange("p (w t c) -> p w t c", w=2, t=NT)
        used[0] = 0
        w1r = ar(2 * FF).rearrange("p (s f) -> p s f", s=2)
        w2r = ar(2 * FT * C).rearrange("p (s f c) -> p s f c", s=2, f=FT)
        xer = ar(2 * ST * (C + 1)).rearrange("p (s t c) -> p s t c", s=2, t=ST)
        xeT = ar(2 * CAP).rearrange("p (s n) -> p s n", s=2)
        hT = ar(FT * CAP).rearrange("p (f n) -> p f n", f=FT)
        yer = ar(2 * ST * C).rearrange("p (s t c) -> p s t c", s=2, t=ST)
        hsT = ar(2 * FT * CH).rearrange("p (s f n) -> p s f n", s=2, f=FT)
        sw1 = sb("sw1", [P, FF])
        sw2 = sb("sw2", [P, FT, C])
        sb2 = sb("sb2", [P, C])
        b2all = sb("b2all", [P, EXP, C])
        rw = sb("rw", [P, EXP])
        before = sb("before", [P, P], BF16)
        ones_b = sb("ones_b", [P, P], BF16)
        rank = sb("rank", [P, EXP, NT])
        first = sb("first", [P, EXP, NT])
        carry = sb("carry", [P, EXP * NT])
        spill = sb("spill", [P, NT])
        R = {n: sb("r_" + n, [P, EXP, NT]) for n in ("lg", "ls", "ex", "gates", "t1", "t2")}
        RW = {n: sb("rw_" + n, [P, 2, EXP, NT]) for n in ("mask", "incl", "pos", "keep", "t")}
        mask_b = sb("mask_b", [P, 2, EXP, NT], BF16)
        rt = sb("rt", [P, 6, NT])
        rt2 = sb("rt2", [P, 6, 2, NT])
        cap1 = sb("cap1", [P, EXP])
        slot_i = sb("slot_i", [P, 2, NT], I32)
        slot_n = sb("slot_n", [P, EXP, ST])
        second = sb("second", [P, EXP, ST])
        vacant = sb("vacant", [P, EXP, ST])
        number = sb("number", [P, 2, ST])
        vrow = sb("vrow", [P, ST])
        back_i = sb("back_i", [P, 2, ST], I32)

        used[0] = 0
        uu = ar(B * DT * L).rearrange("p (g n) -> p g n", g=B * DT)
        delta = ar(B * DT * L).rearrange("p (g n) -> p g n", g=B * DT)
        du = ar(B * DT * L).rearrange("p (g n) -> p g n", g=B * DT)
        gate = ar(B * DT * L).rearrange("p (g n) -> p g n", g=B * DT)
        bc_parts = ar(NTOK // 2).bitcast(BF16)
        low = xT[:, :]
        ring0 = used[0]
        sp_l = ar(4 * L).rearrange("p (s n) -> p s n", s=4)
        sp_w = ar(4 * L).rearrange("p (s n) -> p s n", s=4)
        bc_r = ar(NTOK)
        bc_p2 = ar(NTOK // 2).bitcast(BF16)
        used[0] = ring0
        dA = ar(2 * L).rearrange("p (s n) -> p s n", s=2)
        used[0] = ring0 + 4 * L
        Bs = ar(2 * L).rearrange("p (s n) -> p s n", s=2)
        hh = ar(4 * L).rearrange("p (s n) -> p s n", s=4)
        dBu = ar(4 * L).rearrange("p (s n) -> p s n", s=4)
        used[0] = 0
        m1 = ar(NTOK).rearrange("p (c n) -> p c n", c=NCH)
        m2 = ar(2 * CH).rearrange("p (g n) -> p g n", g=2)
        m3 = ar(CH)
        tf = ar(NTOK).rearrange("p (c n) -> p c n", c=NCH)
        tw_in = ar(NTOK).rearrange("p (c n) -> p c n", c=NCH)
        tw_s = ar(NTOK).rearrange("p (c n) -> p c n", c=NCH)
        base = ar(NTOK).rearrange("p (c n) -> p c n", c=NCH)
        prod = ar(NTOK).rearrange("p (c n) -> p c n", c=NCH)
        U_PAIR, GATE_PAIR, DELTA_PAIR, BC_PAIR = (0, 1, 0, 3), (2, 3, 2, 2), (0, 3, 2, 0), (1, 1)
        win = sb("win", [P, 2 * DIN])
        convw = sb("convw", [P, DT, TAPS])
        wx = sb("wx", [P, DT, RANK + 2 * ST_N])
        wx3 = sb("wx3", [P, DT, 104])
        wdt = sb("wdt", [P, DIN])
        alog = sb("alog", [P, DT, ST_N])
        wout = sb("wout", [P, DT, C])
        sel = sb("sel", [96, 2 * ST_N, P], BF16)
        cw1, cw2, cw3, cw4 = (sb(f"cw{j + 1}", [P, n]) for j, n in enumerate((P, P // 2, P // 4, 1)))
        cb2, cb3, cb4 = sb("cb2", [P, 1]), sb("cb3", [P, 1]), sb("cb4", [P, 1])
        gw = [sb(f"gw{j}", sh) for j, sh in ((1, [P, 64]), (2, [64, 32]), (3, [32, 1]))]
        gb1, gb2, gb3 = sb("gb1", [64, 1]), sb("gb2", [32, 1]), sb("gb3", [P, 1])
        w4b, gw3b = sb("w4b", [P, P]), sb("gw3b", [32, P])
        rng = sb("rng", [P, 1])
        sgn = sb("sgn", [P, 1])
        gmean = sb("gmean", [P, 2, B])
        g1, g2, gf = sb("g1", [64, B]), sb("g2", [32, B]), sb("gf", [P, B])
        c_in = sb("c_in", [P, 4, B])

        ln_stats = sb("ln_stats", [P, NT, 6])
        lnv = sb("lnv", [P, NT, 2])

        def one(tile, g):
            return tile[:, bass.ds(g, 1), :].rearrange("p o n -> p (o n)")

        S = {}

        def s_(name):
            if name not in S:
                S[name] = sem(name)
            return S[name]

        def ln_start(dve, v, ch, t0, n):
            for t in range(t0, t0 + n):
                ch.mark(v.bn_stats(ln_stats[:, t, :], xres[:, t, :]))
            ch.wait()
            for t in range(t0, t0 + n):
                ch.mark(v.bn_aggr(lnv[:, t, :], ln_stats[:, t, :]))
            ch.wait()
            v.tensor_scalar(lnv[:, t0:t0 + n, 1], lnv[:, t0:t0 + n, 1], EPS, None, ALU.add).then_inc(s_("ln_var"), 1)

        def ln_end(dve, v, ch, t0, n, count, ready):
            dve.wait_ge(s_("ln_sqrt"), count)
            ch(v.reciprocal(lnv[:, t0:t0 + n, 1], lnv[:, t0:t0 + n, 1]))
            for t in range(t0, t0 + n):
                last = v.tensor_scalar(xres[:, t, :], xres[:, t, :], lnv[:, t, 0:1], lnv[:, t, 1:2], ALU.subtract, ALU.mult)
                last.then_inc(s_(ready), 1)

        block = ctx.enter_context(nc.Block())

        @block.sync
        def _(sp):
            for j, n in enumerate("qkvo"):
                sp.dma_start(wph[:, j, :], a[f"L0_attn_phase_{n}"]).then_inc(s_("phase_loaded"), 16)
            for j, n in enumerate("qkvo"):
                sp.dma_start(wam[:, j, :], a[f"L0_attn_amp_{n}"]).then_inc(s_("amp_loaded"), 16)
            for row, n, src in ((B1_ROW, 32, a["L0_ffn_b1"].rearrange("e (f p) -> (e f) p", p=P)),
                                (SB1_ROW, 4, a["L0_ffn_sb1"].rearrange("(f p) -> f p", p=P)),
                                (CONVB_ROW, 2, a["L1_attn_conv_b"].rearrange("(f p) -> f p", p=P)),
                                (BDT_ROW, 2, a["L1_attn_b_dt"].rearrange("(f p) -> f p", p=P)),
                                (D_ROW, 2, a["L1_attn_D"].rearrange("(f p) -> f p", p=P)),
                                (CNB1_ROW, 1, a["L1_ffn_cn_b1"].rearrange("(f p) -> f p", p=P))):
                sp.dma_start(brow[row:row + n, :], src).then_inc(s_("brow_loaded"), 16)
            sp.dma_start(sw1[:, :], a["L0_ffn_sw1"]).then_inc(s_("ffn_loaded"), 16)
            sp.dma_start(sw2[:, :, :], a["L0_ffn_sw2"].rearrange("(f p) c -> p f c", p=P)).then_inc(s_("ffn_loaded"), 16)
            sp.dma_start(sb2[:, :], bass.AP(tensor=a["L0_ffn_sb2"].tensor, offset=0, ap=[[0, P], [1, C]]))\
                .then_inc(s_("ffn_loaded"), 16)
            sp.dma_start(b2all[:, :, :], bass.AP(tensor=a["L0_ffn_b2"].tensor, offset=0, ap=[[0, P], [C, EXP], [1, C]]))\
                .then_inc(s_("ffn_loaded"), 16)
            sp.dma_start(rw[:, :], a["L0_ffn_router_w"]).then_inc(s_("ffn_loaded"), 16)
            m, f = "L1_attn_", "L1_ffn_"
            for dst, src in ((win[:, :], a[m + "W_in"]),
                             (convw[:, :, :], bass.AP(tensor=a[m + "conv_w"].tensor, offset=0, ap=[[TAPS, P], [P * TAPS, DT], [1, TAPS]])),
                             (wx[:, :, :], a[m + "W_x"].rearrange("(t p) c -> p t c", p=P)),
                             (wdt[96:96 + RANK, :], a[m + "W_dt"]),
                             (alog[:, :, :], a[m + "A_log"].rearrange("(t p) c -> p t c", p=P)),
                             (wout[:, :, :], a[m + "W_out"].rearrange("(t p) c -> p t c", p=P))):
                sp.dma_start(dst, src).then_inc(s_("mixer_loaded"), 16)

            def column(t):
                return t.rearrange("(p o) -> p o", o=1)

            def everywhere(t):
                return bass.AP(tensor=t.tensor, offset=0, ap=[[0, P], [1, 1]])

            for dst, src in [(cw1[:, :], a[f + "cn_w1"]), (cw2[:, :], a[f + "cn_w2"])] + \
                    [(cw3[64 * j:64 * j + 64, :], a[f + "cn_w3"]) for j in range(2)] + \
                    [(cw4[32 * j:32 * j + 32, :], a[f + "cn_w4"]) for j in range(4)] + \
                    [(cb2[64 * j:64 * j + 64, :], column(a[f + "cn_b2"])) for j in range(2)] + \
                    [(cb3[32 * j:32 * j + 32, :], column(a[f + "cn_b3"])) for j in range(4)] + \
                    [(gw[j][:, :], a[f + f"gc_w{j + 1}"]) for j in range(3)] + \
                    [(gb1[:, :], column(a[f + "gc_b1"])), (gb2[:, :], column(a[f + "gc_b2"])),
                     (cb4[:, :], everywhere(a[f + "cn_b4"])), (gb3[:, :], everywhere(a[f + "gc_b3"])),
                     (rng[:, :], everywhere(a[f + "adaptive_range"]))]:
                sp.dma_start(dst, src).then_inc(s_("net_loaded"), 16)

            def store_parts(b):
                sp.wait_ge(s_("split_done"), 4 * b + 2)
                for part in range(3):
                    sp.dma_start(bass.AP(tensor=q_parts_d.tensor, offset=(b * HEADS * 3 + part) * HD * L,
                                         ap=[[3 * HD * L, HEADS], [L, HD], [1, L]]),
                                 q_split[:, part, b * L:(b + 1) * L]).then_inc(s_(f"parts_stored{b}"), 16)
                sp.wait_ge(s_("split_done"), 4 * b + 4)
                sp.dma_start(bass.AP(tensor=k_parts_d.tensor, offset=b * HEADS * HD * 3 * L, ap=[[3 * L, P], [1, 3 * L]]),
                             k_split[:, :, b * L:(b + 1) * L]).then_inc(s_(f"parts_stored{b}"), 16)

            store_parts(0)
            sp.wait_ge(s_("parts_stored0"), 4 * 16)
            sp.wait_ge(s_("qk_cleared"), 1)

            def load_unit(u, slot):
                for buf, parts, ap in ((qbuf, q_parts_d, [[L, 3 * HD], [0, 3], [1, L]]),
                                       (kbuf, k_parts_d, [[0, 3], [L, 3 * HD], [1, L]])):
                    sp.dma_start(buf[0:ROWS, slot, :], bass.AP(tensor=parts.tensor, offset=u * HD * 3 * L, ap=ap))\
                        .then_inc(s_(f"unit_loaded{slot}"), 16)

            def load_max(count, slot, m):
                sp.wait_ge(s_("ring_read"), count)
                sp.dma_start(qbuf[96:99, slot, :], mT[0:24, m, :]).then_inc(s_(f"max_loaded{slot}"), 16)

            def load_heads(u, n, loaded):
                row, b = (u % HEADS) * HD, u // HEADS
                for par in range(2):
                    src = bass.AP(tensor=head_out_d.tensor, offset=(u * 2 + par) * (HD + 1) * L,
                                  ap=[[2 * (HD + 1) * L, n], [L, HD], [1, L]])
                    sp.dma_start(o_par[row:row + n * HD, par, b * L:(b + 1) * L], src).then_inc(s_(loaded), 16)

            def load_dens(b, loaded):
                for par in range(2):
                    src = bass.AP(tensor=head_out_d.tensor, offset=((b * HEADS * 2 + par) * (HD + 1) + HD) * L,
                                  ap=[[L // 4, 4], [2 * (HD + 1) * L, HEADS], [1, L // 4]])
                    sp.dma_start(den[64 * b:64 * b + 64, par, :], src).then_inc(s_(loaded), 16)

            def store_head(u, s, pars=range(2)):
                sp.wait_ge(s_("pv_copied"), u + 2)
                for par in pars:
                    for qh in range(2):
                        g = 2 * par + qh
                        dst = bass.AP(tensor=head_out_d.tensor, offset=((u * 2 + par) * (HD + 1)) * L + qh * CH,
                                      ap=[[L, HD + 1], [1, CH]])
                        sp.dma_start(dst, pvs[32 * g:32 * g + HD + 1, s, :]).then_inc(s_(f"head_stored{s}"), 16)

            for s in range(4):
                sp.sem_inc(s_(f"max_loaded{s}"), 16)
            for s in range(2):
                sp.sem_inc(s_(f"head_stored{s}"), 16)
            for u in range(3):
                load_unit(u, u)
            store_parts(1)
            load_max(MAXT_READ, 0, 0)
            sp.wait_ge(s_("constants_ready"), 1)
            for k in range(4):
                sp.dma_start(slot_x_d[k * (SLOTS // 4):(k + 1) * (SLOTS // 4), :].rearrange("(p r) c -> p (r c)", p=P),
                             zero[:, :]).then_inc(s_("rows_zeroed"), 16)
            for k in range(4):
                sp.dma_start(picked_d[k * (NTOK // 2):(k + 1) * (NTOK // 2), :].rearrange("(p r) c -> p (r c)", p=P),
                             zero[:, 0:NTOK // 2 // P * C]).then_inc(s_("rows_zeroed"), 16)
            sp.wait_ge(s_("parts_stored1"), 4 * 16)
            def unit(i, s, last):
                u = 4 * i + s
                if not (last and s > 0):
                    sp.wait_ge(s_("st_done"), KT * u + 1)
                    load_unit(u + 3, (s + 3) % 4)
                if not (last and s == 3):
                    load_max(LAST_READ if last and s == 2 else MAXT_READ + ITEMS * (u + 1), (s + 1) % 4, (s + 1) % 2)
                store_head(u, s % 2, range(1) if last and s == 3 else range(2))
                if last and s == 1:
                    for parity in range(2):
                        sp.wait_ge(s_(f"head_stored{parity}"), 4 * 16 * (UNITS // 2 - 2) + 16)
                    load_heads(HEADS, HEADS - 4, "o_loaded1")

            with sp.Fori(0, UNITS // 4 - 1) as i:
                for s in range(4):
                    unit(i, s, False)
            for parity in range(2):
                sp.wait_ge(s_(f"head_stored{parity}"), 4 * 16 * (HEADS // 2) + 16)
            load_dens(0, "o_loaded0")
            load_heads(0, HEADS, "o_loaded0")
            for s in range(4):
                unit(UNITS // 4 - 1, s, True)
            for s in range(2):
                sp.wait_ge(s_(f"head_stored{s}"), 4 * 16 * UNITS // 2 + 16)
            load_dens(1, "den_loaded1")
            load_heads(UNITS - 4, 4, "o_loaded1")
            def load_weights(e, s):
                sp.dma_start(w1r[:, s, :], bass.AP(tensor=a["L0_ffn_w1"].tensor, offset=e * C * FF, ap=[[FF, C], [1, FF]]))\
                    .then_inc(s_(f"expert_loaded{s}"), 16)
                sp.dma_start(w2r[:, s, :, :], bass.AP(tensor=a["L0_ffn_w2"].tensor, offset=e * FF * C,
                                                      ap=[[C, P], [P * C, FT], [1, C]])).then_inc(s_(f"expert_loaded{s}"), 16)

            def load_slots(e, s):
                sp.dma_start(xer[:, s, :, :], bass.AP(tensor=slot_x_d.tensor, offset=e * CAP * (C + 1),
                                                      ap=[[C + 1, P], [P * (C + 1), ST], [1, C + 1]]))\
                    .then_inc(s_(f"slots_loaded{s}"), 16)

            sp.wait_ge(s_("onorm_ready"), 4)
            for e in range(2):
                load_weights(e, e)
            sp.wait_ge(s_("scattered"), 2 * NT * 16)
            for e in range(2):
                load_slots(e, e)

            def expert_io(i, s):
                e = 2 * i + s
                sp.wait_ge(s_("xeT_done"), e + 1)
                sp.wait_ge(s_("number_kept"), e + 1)
                load_slots(e + 2, s)
                sp.wait_ge(s_("ye_ready"), e + 2)
                load_weights(e + 2, s)

            with sp.Fori(0, EXP // 2 - 1) as i:
                for s in range(2):
                    expert_io(i, s)
            for s in range(2):
                sp.wait_ge(s_(f"ye_stored{s}"), EXP // 2 * ST * 16)
            for gi in range(4):
                for w in range(2):
                    sp.dma_start(picked[:, w, 4 * gi:4 * gi + 4, :],
                                 picked_d[w * NTOK + gi * CH:w * NTOK + (gi + 1) * CH, :].rearrange("(t p) c -> p t c", p=P))\
                        .then_inc(s_(f"picked{gi}"), 16)
            def twist(i, c):
                for dst, src in ((0, 64), (32, 96), (64, 0), (96, 32)):
                    sp.dma_start(tw_in[dst:dst + 32, c, :], xT[src:src + 32, c * CH:(c + 1) * CH])\
                        .then_inc(s_(f"twisted{c}"), 16)

            with sp.Fori(0, CYCLES) as i:
                for c in range(NCH):
                    sp.wait_ge(s_("state_ready"), NCH * i + c + 1)
                    twist(i, c)
            for gi in range(4):
                sp.wait_ge(s_("x4_ready"), 4 * gi + 4)
                sp.dma_start(out[gi // 2, (gi % 2) * CH:(gi % 2 + 1) * CH, :].rearrange("(t p) c -> p t c", p=P),
                             xres[:, 4 * gi:4 * gi + 4, :]).then_inc(s_("out_stored"), 16)
            sp.wait_ge(s_("out_stored"), 4 * 16)

        @block.gpsimd
        def _(pool):
            g = nc.gpsimd
            ch = Chain(pool, s_("pool_chain"))
            ch(g.memset(ident[:], 0.0))
            g.affine_select(out=ident[:], in_=ident[:], compare_op=ALU.not_equal, fill=1.0, base=0,
                            pattern=[[-1, P]], channel_multiplier=1).then_inc(s_("ident_ready"), 1)
            ch(g.memset(ident_b[:], 0.0))
            ch(g.affine_select(out=ident_b[:], in_=ident_b[:], compare_op=ALU.not_equal, fill=1.0, base=0,
                               pattern=[[-1, P]], channel_multiplier=1))
            ch(g.iota(xnum[:, :, C:C + 1].rearrange("p t o -> p (t o)"), pattern=[[P, NT]], base=1, channel_multiplier=1,
                      allow_small_or_imprecise_dtypes=True))
            ch(g.memset(qbuf[64:128, :, :], 0.0))
            ch(g.memset(kbuf[64:96, :, :], 0.0))
            ch(g.memset(kbuf[96:128, :, :], 0.0))
            g.memset(kbuf[96:99, :, :], 1.0).then_inc(s_("qk_cleared"), 1)
            pool.wait_ge(s_("qk_cleared"), 1)
            ch.mark(g.memset(neg1[:, :], -1.0))
            ch(g.memset(vst[:, :, :, :], 0.0))
            ch(g.memset(vst[:, :, :, HD:HD + 1], 1.0))
            def stage_v(u, s):
                src = vtok[:, :, :, :, :].rearrange("p b h k d -> p (b h) k d")
                return g.tensor_copy(vst[:, s, :, 0:HD], src[:, bass.ds(u, 1), :, :].rearrange("p o k d -> p (o k) d"))

            def split_max(v, s, c):
                pool.wait_ge(s_("max_ready"), v + 1)
                c(g.tensor_tensor(mparts[:, s, 0:8], rowmax[:, s, :], neg1[:, :], ALU.mult))
                c(g.tensor_tensor(mneg[:, 1, :], rowmax[:, s, :], mparts[:, s, 0:8], ALU.add))
                c(g.tensor_tensor(mparts[:, s, 8:16], mneg[:, 1, :], neg1[:, :], ALU.mult))
                c(g.tensor_tensor(mneg[:, 2, :], mneg[:, 1, :], mparts[:, s, 8:16], ALU.add))
                g.tensor_tensor(mparts[:, s, 16:24], mneg[:, 2, :], neg1[:, :], ALU.mult)\
                    .then_inc(s_("max_split"), 1)

            ch(g.memset(expand[:], 1.0))
            ch.mark(g.memset(ones_b[:], 1.0))
            ch.mark(g.memset(zero[:], 0.0))
            ch.wait()
            ch.mark(g.affine_select(out=before[:], in_=ones_b[:], compare_op=ALU.is_gt, fill=0.0, base=0,
                                    pattern=[[1, P]], channel_multiplier=-1))
            ch.mark(g.iota(rank[:], pattern=[[-1, EXP], [0, NT]], base=EXP, channel_multiplier=0,
                           allow_small_or_imprecise_dtypes=True))
            ch.mark(g.iota(first[:], pattern=[[CAP, EXP], [-P, NT]], base=-SLOTS, channel_multiplier=-1,
                           allow_small_or_imprecise_dtypes=True))
            ch.mark(g.iota(spill[:], pattern=[[P, NT]], base=SLOTS, channel_multiplier=1,
                           allow_small_or_imprecise_dtypes=True))
            ch.mark(g.iota(slot_n[:], pattern=[[0, EXP], [P, ST]], base=0, channel_multiplier=1,
                           allow_small_or_imprecise_dtypes=True))
            ch.mark(g.iota(vacant[:], pattern=[[CAP, EXP], [P, ST]], base=NTOK + 1, channel_multiplier=1,
                           allow_small_or_imprecise_dtypes=True))
            ch(g.memset(carry[:], 1.0))
            ch(g.memset(carry[:, :].rearrange("p (w t) -> p w t", t=NT)[:, :, 0:1], 0.0))
            ch.mark(g.memset(sel[:], 0.0))
            ch.wait()
            for at, value in ((0, 1.0), (32, -1.0), (64, -1.0), (96, 1.0)):
                ch(g.memset(sgn[at:at + 32, :], value))
            for q in range(3):
                ch(g.affine_select(out=sel[:], in_=sel[:], compare_op=ALU.not_equal, fill=1.0, base=-32 * q,
                                   pattern=[[-1, 2 * ST_N], [0, P]], channel_multiplier=1))
            flat = expand[:, :, :].rearrange("p q m -> p (q m)")
            ch(g.affine_select(out=flat, in_=flat, compare_op=ALU.is_ge, fill=0.0, base=0,
                               pattern=[[1, 4 * B * P]], channel_multiplier=-HD))
            ch(g.affine_select(out=flat, in_=flat, compare_op=ALU.is_ge, fill=0.0, base=HD - 1,
                               pattern=[[-1, 4 * B * P]], channel_multiplier=HD))
            pool.sem_inc(s_("constants_ready"), 1)
            pool.wait_ge(s_("v_copied"), 4)
            stage_v(0, 0).then_inc(s_("v_staged"), 1)

            class At:
                def __init__(self, start):
                    self.start, self.n = start, 0

                def __call__(self, ins):
                    ins.then_inc(s_("pool_chain"), 1)
                    self.n += 1
                    pool.wait_ge(s_("pool_chain"), self.start + self.n)

            split_max(0, 0, ch)
            split_max(1, 1, ch)

            base = ch.n - 8

            def unit(i, s, last):
                u = 4 * i + s
                if not (last and s == 3):
                    pool.wait_ge(s_("probs_free"), NPROB + KT * u)
                    stage_v(u + 1, (s + 1) % 2).then_inc(s_("v_staged"), 1)
                if not (last and s > 1):
                    pool.wait_ge(s_("ring_full"), MAXT_READ + ITEMS * u)
                    split_max(u + 2, s % 2, At(base + 8 + 4 * u))

            with pool.Fori(0, UNITS // 4 - 1) as i:
                for s in range(4):
                    unit(i, s, False)
            for s in range(4):
                unit(UNITS // 4 - 1, s, True)
            ch.n = base + 4 * UNITS
            pool.wait_ge(s_("onorm_ready"), 4)
            pool.wait_ge(s_("ffn_loaded"), 5 * 16)
            pool.wait_ge(s_("x1_ready"), NT)
            ch(g.tensor_scalar(sb2[:, :], sb2[:, :], SHARED_SCALE, None, ALU.mult))
            g.tensor_tensor(acc[:, :, :], xres[:, :, :], sb2[:, :].unsqueeze(1).to_broadcast([P, NT, C]), ALU.add)\
                .then_inc(s_("acc_ready"), 1)
            pool.wait_ge(s_("rows_zeroed"), 8 * 16)
            for w in range(2):
                pool.wait_ge(s_("slot_ready"), w + 1)
                for t in range(NT):
                    g.indirect_dma_start(out=slot_x_d[:, :], out_offset=bass.IndirectOffsetOnAxis(ap=slot_i[:, w, t:t + 1], axis=0),
                                         in_=xnum[:, t, :], in_offset=None).then_inc(s_("scattered"), 16)
            def scatter_y(s, k):
                g.indirect_dma_start(out=picked_d[:, :],
                                     out_offset=bass.IndirectOffsetOnAxis(ap=back_i[:, s, k:k + 1], axis=0),
                                     in_=yer[:, s, k, :], in_offset=None).then_inc(s_(f"ye_stored{s}"), 16)

            def scatter_expert(i, s):
                pool.wait_ge(s_("back_ready"), 2 * i + s + 2)
                pool.wait_ge(s_("ye_ready"), 2 * i + s + 2)
                pool.sem_inc(s_("pool_waited"), 1)
                for k in range(ST):
                    scatter_y(s, k)
                pool.wait_ge(s_(f"ye_stored{s}"), ST * 16 * (i + 1))
                pool.sem_inc(s_("ye_left"), 1)

            with pool.Fori(0, EXP // 2 - 1) as i:
                for s in range(2):
                    scatter_expert(i, s)
            scatter_expert(EXP // 2 - 1, 0)
            pool.wait_ge(s_("back_ready"), EXP + 1)
            for k in range(ST):
                pool.wait_ge(s_("ye_ready"), EXP + 1 + k)
                scatter_y(1, k)

            for gi in range(1, 4):
                pool.wait_ge(s_("first_scaled"), gi)
                ag = acc[:, 4 * gi:4 * gi + 4, :]
                g.tensor_tensor(ag, ag, picked[:, 0, 4 * gi:4 * gi + 4, :], ALU.add).then_inc(s_("first_added"), 1)

            pool.wait_ge(s_("mixer_loaded"), 6 * 16)
            for k in range(3):
                ch.mark(g.tensor_copy(wx3[:, :, 32 * k:32 * k + 32], wx[:, :, RANK:RANK + 2 * ST_N]))
            g.tensor_copy(wx3[:, :, 96:104], wx[:, :, 0:RANK]).then_inc(s_("wx3_ready"), 1)
            ch.wait()
            pool.wait_ge(s_("wx3_ready"), 1)
            pool.sem_inc(s_("dBu_ready"), CREDIT)
            for q in range(B * DT):
                pool.wait_ge(s_("sp_ln"), q + 1)
                pool.wait_ge(s_("sp_c"), q + 1)
                g.tensor_tensor(sp_l[:, q, :], sp_l[:, q, :], du[:, q, :], ALU.subtract).then_inc(s_("sp_small"), 1)
            pool.wait_ge(s_("sp_small"), B * DT)
            pool.wait_ge(s_("bc_ready"), B)
            with pool.Fori(0, B) as bb:
                for n in range(ST_N):
                    for d in range(DT):
                        U = CREDIT + PER_B * bb + DT * n + d + 1
                        if n == 0 and d == 0:
                            pool.wait_ge(s_("du_ready"), DT * bb + DT)
                            pool.sem_inc(s_("pool_waited"), 1)
                        if d == 0:
                            pool.wait_ge(s_("b_copied"), CREDIT + ST_N * bb + n + 1)
                        pool.wait_ge(s_("h_ready"), U - 4)
                        pool.sem_inc(s_("pool_waited"), 1)
                        g.tensor_tensor(dBu[:, DT * (n % 2) + d, :], one(du, DT * bb + d), Bs[:, n % 2, :], ALU.mult)\
                            .then_inc(s_("dBu_ready"), 1)

        @block.scalar
        def _(act):
            sc = nc.scalar
            ch = Chain(act, s_("act_chain"))
            for b in range(B):
                act.dma_start(xres[:, b * 8:b * 8 + 8, :],
                              a["L0_attn_x"][b].rearrange("(t p) c -> p t c", p=P)).then_inc(s_("x_loaded"), 16)
            for j, n in enumerate("qkvo"):
                act.dma_start(basis[32 * j:32 * j + 32, :], a[f"L0_attn_basis_{n}"]).then_inc(s_("basis_loaded"), 16)
            act.wait_ge(s_("args_ready"), 1)
            sc.activation(wtmp[:, 1, :], wtmp[:, 0, :], ACT.Sin).then_inc(s_("sin_done"), 1)
            for c in range(0, NCH, 2):
                act.wait_ge(s_("xT_done"), c + 1)
                sc.copy(xT[:, c * CH:(c + 1) * CH], bank[c][:, :]).then_inc(s_("xT_copied_a"), 1)
            n = 0
            for b in range(B):
                for w, split in ((0, q_split), (1, k_split)):
                    for c in (2 * b, 2 * b + 1):
                        act.wait_ge(s_("qk_done"), n + 1)
                        sc.copy(split[:, 0, c * CH:(c + 1) * CH], bank[4 * w + c][:, :]).then_inc(s_("part1_done"), 1)
                        act.wait_ge(s_("resid_done"), n + 1)
                        sc.copy(split[:, 1, c * CH:(c + 1) * CH], resid[:, n % 4, :]).then_inc(s_("part2_done"), 1)
                        n += 1
            for c in range(NCH):
                act.wait_ge(s_("v_done"), c + 1)
                b, t0 = c // 2, 4 * (c % 2)
                sc.copy(vtok[:, b, :, t0:t0 + 4, :].rearrange("p h k d -> p k h d"),
                        bank[c][:, :].rearrange("p (k h d) -> p k h d", k=4, h=HEADS)).then_inc(s_("v_copied"), 1)

            def exps(G, kt, w):
                act.wait_ge(s_("st_done"), G + 2)
                act.wait_ge(s_("probs_free"), G + 1)
                sc.activation(probs[:, kt % NPROB, :], st_pair[kt % 2][:, :], ACT.Exp, scale=SCALE)\
                    .then_inc(s_("exp_done"), 1)

            act.sem_inc(s_("pv_copied"), 1)
            for G in range(2):
                exps(G, G, 0)

            def unit(i, s, last):
                u = 4 * i + s
                for j in range(KT):
                    if last and s == 3 and j >= KT - 2:
                        continue
                    exps(KT * u + j + 2, j + 2, s)
                act.wait_ge(s_("probs_free"), NPROB + KT * (u + 1))
                act.wait_ge(s_(f"head_stored{s % 2}"), 4 * 16 * (2 * i + s // 2) + 16)
                sc.copy(pvs[:, s % 2, :], pv_bank).then_inc(s_("pv_copied"), 1)
                if last and s == 3:
                    act.wait_ge(s_("pv_copied"), UNITS + 1)
                    for qh in range(2):
                        dst = bass.AP(tensor=head_out_d.tensor, offset=(u * 2 + 1) * (HD + 1) * L + qh * CH,
                                      ap=[[L, HD + 1], [1, CH]])
                        act.dma_start(dst, pvs[64 + 32 * qh:64 + 32 * qh + HD + 1, 1, :]).then_inc(s_("head_stored1"), 16)

            with act.Fori(0, UNITS // 4 - 1) as i:
                for s in range(4):
                    unit(i, s, False)
            for s in range(4):
                unit(UNITS // 4 - 1, s, True)

            for b in range(B):
                for gi in (2 * b, 2 * b + 1):
                    act.wait_ge(s_("ln_var"), gi + 1)
                    sc.activation(lnv[:, 4 * gi:4 * gi + 4, 1], lnv[:, 4 * gi:4 * gi + 4, 1], ACT.Sqrt).then_inc(s_("ln_sqrt"), 1)
                for c in (2 * b, 2 * b + 1):
                    act.wait_ge(s_("x1T_done"), c + 1)
                    sc.copy(xT[:, c * CH:(c + 1) * CH], bank[c][:, :]).then_inc(s_("x1T_copied"), 1)

            act.wait_ge(s_("biasT_ready"), 1)
            act.wait_ge(s_("logits_shifted"), 1)
            sc.activation(R["ex"][:, :, :], R["ls"][:, :, :], ACT.Exp).then_inc(s_("gate_exp"), 1)
            for c in range(NCH):
                if c >= 2:
                    act.wait_ge(s_("shared_done"), c - 1)
                for f in range(FT):
                    act.wait_ge(s_("shared_up"), c * FT + f + 1)
                    sc.activation(hsT[:, c % 2, f, :], bank[f][:, :], ACT.Silu, bias=biasT[:, SB1_ROW + f:SB1_ROW + f + 1])\
                        .then_inc(s_("shared_act"), 1)

            def expert_act(i, s):
                e = 2 * i + s
                act.wait_ge(s_("ye_done"), e + 1)
                for f in range(FT):
                    act.wait_ge(s_("up_done"), FT * e + f + 1)
                    sc.activation(hT[:, f, :].rearrange("p (h n) -> p h n", h=2),
                                  pair[1 + f % 2][:, :].rearrange("p (h n) -> p h n", h=2)[:, :, 0:CAP // 2],
                                  ACT.Silu, bias=biasT[:, bass.ds(FT * e + f, 1)]).then_inc(s_("up_act"), 1)

            with act.Fori(0, EXP // 2) as i:
                for s in range(2):
                    expert_act(i, s)

            act.wait_ge(s_("mask_ready"), 3)
            for gi in range(1, 4):
                act.wait_ge(s_(f"picked{gi}"), 2 * 16)
                for tt in range(4 * gi, 4 * gi + 4):
                    ins = sc.activation(picked[:, 0, tt, :], picked[:, 0, tt, :], ACT.Identity, scale=rt2[:, 4, 0, tt:tt + 1])
                ins.then_inc(s_("first_scaled"), 1)

            def copy_x2T(c):
                act.wait_ge(s_("x2T_done"), c + 1)
                sc.copy(xT[:, c * CH:(c + 1) * CH], bank[c][:, :]).then_inc(s_("x2T_copied"), 1)

            for gi in range(4):
                act.wait_ge(s_("ln_var"), 4 + gi + 1)
                sc.activation(lnv[:, 4 * gi:4 * gi + 4, 1], lnv[:, 4 * gi:4 * gi + 4, 1], ACT.Sqrt).then_inc(s_("ln_sqrt"), 1)
                if gi >= 2:
                    copy_x2T(gi - 2)

            def last_tap(q):
                d = q % DT
                act.wait_ge(s_("u_in_done"), q + 1)
                sc.activation(uu[:, q, :], pair[U_PAIR[q]][:, :], ACT.Identity, bias=biasT[:, CONVB_ROW + d:CONVB_ROW + d + 1],
                              scale=convw[:, d, TAPS - 1:TAPS]).then_inc(s_("last_tap"), 1)

            def silu_gate(q):
                act.wait_ge(s_("gate_done"), q + 1)
                sc.activation(gate[:, q, :], pair[GATE_PAIR[q]][:, :], ACT.Silu).then_inc(s_("gate_ready"), 1)

            def silu_u(q):
                act.wait_ge(s_("taps_done"), q + 1)
                sc.activation(uu[:, q, :], uu[:, q, :], ACT.Silu).then_inc(s_("u_ready"), 1)

            def bc_part1(b):
                act.wait_ge(s_("bc_done"), b + 1)
                sl, src = slice(b * L, (b + 1) * L), pair[BC_PAIR[b]]
                sc.copy(low[96:96 + RANK, sl], src[96:96 + RANK, :]).then_inc(s_("low_ready"), 1)
                sc.copy(bc_parts[0:96, sl], src[0:96, :]).then_inc(s_("bc_1"), 1)

            def bc_part2(b):
                act.wait_ge(s_("bc_rest"), b + 1)
                sl = slice(b * L, (b + 1) * L)
                sc.copy(bc_p2[0:96, sl], bc_r[0:96, sl]).then_inc(s_("bc_2"), 1)

            def exp_abs(q):
                act.wait_ge(s_("delta_done"), q + 1)
                bias = biasT[:, BDT_ROW + q % 2:BDT_ROW + q % 2 + 1]
                sc.activation(sp_l[:, q, :], pair[DELTA_PAIR[q]][:, :], ACT.Abs, bias=bias).then_inc(s_("sp_abs"), 1)
                act.wait_ge(s_("sp_abs"), q + 1)
                sc.activation(du[:, q, :], sp_l[:, q, :], ACT.Exp, scale=-1.0).then_inc(s_("sp_exp"), 1)

            last_tap(0)
            copy_x2T(2)
            copy_x2T(3)
            silu_gate(0)
            last_tap(1)
            silu_u(0)
            silu_gate(1)
            last_tap(2)
            silu_gate(2)
            silu_u(1)
            last_tap(3)
            silu_u(2)
            bc_part1(0)
            silu_gate(3)
            silu_u(3)
            bc_part2(0)
            act.wait_ge(s_("rate_step"), 1)
            sc.activation(alog[:, :, :], alog[:, :, :], ACT.Exp).then_inc(s_("rate_step"), 1)
            exp_abs(0)
            bc_part1(1)
            exp_abs(1)
            exp_abs(2)
            bc_part2(1)
            exp_abs(3)
            for q in range(B * DT):
                act.wait_ge(s_("sp_exp"), q + 1)
                act.wait_ge(s_("sp_w_ready"), q + 1)
                sc.activation(sp_l[:, q, :], sp_w[:, q, :], ACT.Ln).then_inc(s_("sp_ln"), 1)
            act.wait_ge(s_("rate_step"), 3)
            act.wait_ge(s_("bc_ready"), B)
            act.wait_ge(s_("sp_c"), B * DT)
            act.sem_inc(s_("b_copied"), CREDIT)
            act.sem_inc(s_("dA_ready"), CREDIT)
            with act.Fori(0, B) as bb:
                for n in range(ST_N):
                    U = CREDIT + PER_B * bb + DT * n + 1
                    if n == 0:
                        act.wait_ge(s_("delta_ready"), DT * bb + DT)
                        act.sem_inc(s_("act_waited"), 1)
                    act.wait_ge(s_("b_ready"), ST_N * bb + n + 1)
                    act.wait_ge(s_("dBu_ready"), U - 3)
                    sc.copy(Bs[:, n % 2, :], pair[0][:, :]).then_inc(s_("b_copied"), 1)
                    for d in range(DT):
                        act.wait_ge(s_("h_ready"), U + d - 2)
                        act.sem_inc(s_("act_waited"), 1)
                        sc.activation(dA[:, d, :], one(delta, DT * bb + d), ACT.Exp, scale=alog[:, d, n:n + 1])\
                            .then_inc(s_("dA_ready"), 1)
            def copy_x3T(c):
                act.wait_ge(s_("x3T_done"), c + 1)
                sc.copy(xT[:, c * CH:(c + 1) * CH], bank[c][:, :]).then_inc(s_("state_ready"), 1)

            for gi in range(4):
                act.wait_ge(s_("ln_var"), 8 + gi + 1)
                sc.activation(lnv[:, 4 * gi:4 * gi + 4, 1], lnv[:, 4 * gi:4 * gi + 4, 1], ACT.Sqrt).then_inc(s_("ln_sqrt"), 1)
                if gi >= 2:
                    copy_x3T(gi - 2)
            copy_x3T(2)
            copy_x3T(3)
            act.wait_ge(s_("net_loaded"), NET_LOADS * 16)

            def global_act(n, dst, src, function, bias, scale=1.0):
                act.wait_ge(s_("global_mm"), n + 1)
                sc.activation(dst, src, function, bias=bias, scale=scale).then_inc(s_("global_act"), 1)

            def cycle(i, first):
                for c in range(NCH):
                    act.wait_ge(s_("net_mm"), NET_STEPS * i + c + 1)
                    sc.activation(m1[:, c, :], bank[c][:, :], ACT.Gelu, bias=biasT[:, CNB1_ROW:CNB1_ROW + 1])\
                        .then_inc(s_("net_act"), 1)
                if first:
                    act.wait_ge(s_("mean_ready"), 1)
                    global_act(0, g1[:, :], bank[7][0:64, 0:B], ACT.Gelu, gb1[:, :])
                for j in range(2):
                    act.wait_ge(s_("net_mm"), NET_STEPS * i + 4 + j + 1)
                    sc.activation(m2[:, j, :], bank[4 + j][:, :], ACT.Gelu, bias=cb2[:, :]).then_inc(s_("net_act"), 1)
                if first:
                    global_act(1, g2[:, :], bank[7][0:32, 0:B], ACT.Gelu, gb2[:, :])
                act.wait_ge(s_("net_mm"), NET_STEPS * i + 7)
                sc.activation(m3[:, :], bank[6][:, :], ACT.Gelu, bias=cb3[:, :]).then_inc(s_("net_act"), 1)
                if first:
                    global_act(2, gf[:, :], bank[7][:, 0:B], ACT.Tanh, gb3[:, :], 0.5)
                for c in range(NCH):
                    act.wait_ge(s_("net_mm"), NET_STEPS * i + 7 + c + 1)
                    act.wait_ge(s_("state_ready"), NCH * i + c + 1)
                    sc.activation(tf[:, c, :], bank[c][:, :], ACT.Tanh, bias=cb4[:, :], scale=0.5).then_inc(s_("net_act"), 1)

            cycle(0, True)
            with act.Fori(1, CYCLES) as i:
                cycle(i, False)
            for gi in range(4):
                act.wait_ge(s_("ln_var"), 12 + gi + 1)
                sc.activation(lnv[:, 4 * gi:4 * gi + 4, 1], lnv[:, 4 * gi:4 * gi + 4, 1], ACT.Sqrt).then_inc(s_("ln_sqrt"), 1)

        @block.vector
        def _(dve):
            v = nc.vector
            ch = Chain(dve, s_("dve_chain"))
            dve.wait_ge(s_("phase_loaded"), 4 * 16)
            ph = wph[:, :, :].rearrange("p j h -> p (j h)")
            ch(v.tensor_scalar(wtmp[:, 1, :], ph, 1.0 / TWO_PI, 0.25, ALU.mult, ALU.add))
            ch(v.tensor_scalar(wtmp[:, 0, :], wtmp[:, 1, :], ROUND, None, ALU.add))
            ch(v.tensor_scalar(wtmp[:, 1, :], wtmp[:, 0, :], ROUND, None, ALU.subtract))
            ch(v.scalar_tensor_tensor(wtmp[:, 0, :], wtmp[:, 1, :], -PI_HI, ph, ALU.mult, ALU.add))
            ch(v.scalar_tensor_tensor(wtmp[:, 2, :], wtmp[:, 1, :], -PI_MID, wtmp[:, 0, :], ALU.mult, ALU.add))
            ch(v.scalar_tensor_tensor(wtmp[:, 0, :], wtmp[:, 1, :], -PI_LO, wtmp[:, 2, :], ALU.mult, ALU.add))
            ch(v.tensor_scalar(wtmp[:, 2, :], wtmp[:, 0, :], TWO_PI / 4, 3.1415925, ALU.add, ALU.min))
            v.tensor_scalar(wtmp[:, 0, :], wtmp[:, 2, :], -3.1415925, None, ALU.max).then_inc(s_("args_ready"), 1)
            for c in range(1, NCH, 2):
                dve.wait_ge(s_("xT_done"), c + 1)
                v.tensor_copy(xT[:, c * CH:(c + 1) * CH], bank[c][:, :]).then_inc(s_("xT_copied_v"), 1)
            dve.wait_ge(s_("sin_done"), 1)
            dve.wait_ge(s_("amp_loaded"), 4 * 16)
            v.tensor_tensor(wtmp[:, 2, :], wtmp[:, 1, :], wam[:, :, :].rearrange("p j h -> p (j h)"), ALU.mult)\
                .then_inc(s_("wcos_ready"), 1)
            dve.wait_ge(s_("wcosT_done"), 1)
            v.tensor_copy(wcosT[:], bank[4][:, 0:P]).then_inc(s_("wcos_ready"), 1)
            dve.wait_ge(s_("weff_done"), 1)
            for j in range(4):
                v.tensor_copy(weff[:, j, :], bank[4 + j][:, 256:256 + C]).then_inc(s_("weff_copied"), 1)
            dve.wait_ge(s_("weff_done"), 2)
            v.tensor_copy(biasT[:, :], bank[5][:, 0:BROWS]).then_inc(s_("biasT_ready"), 1)
            n = 0
            for b in range(B):
                for w, split in ((0, q_split), (1, k_split)):
                    for c in (2 * b, 2 * b + 1):
                        dve.wait_ge(s_("part1_done"), n + 1)
                        if n >= 4:
                            dve.wait_ge(s_("split_done"), n - 3)
                        v.tensor_tensor(resid[:, n % 4, :], bank[4 * w + c][:, :], split[:, 0, c * CH:(c + 1) * CH],
                                        ALU.subtract).then_inc(s_("resid_done"), 1)
                        dve.wait_ge(s_("resid_done"), n + 1)
                        dve.wait_ge(s_("part2_done"), n + 1)
                        v.tensor_tensor(split[:, 2, c * CH:(c + 1) * CH], resid[:, n % 4, :],
                                        split[:, 1, c * CH:(c + 1) * CH], ALU.subtract).then_inc(s_("split_done"), 1)
                        n += 1

            def reduce_pass(v_unit, mslot, item0, maxT_slot):
                k = 0
                for n in range(16):
                    if n == T_AT and maxT_slot is not None:
                        dve.wait_ge(s_("ring_full"), item0 + k + 1)
                        v.tensor_copy(mT[0:24, maxT_slot, :], ring_bank[k % 3][0:24, 0:P]).then_inc(s_("ring_read"), 1)
                        k += 1
                    dve.wait_ge(s_("ring_full"), item0 + k + 1)
                    v.reduce_max(mx[:, mslot, n // 2, n % 2:n % 2 + 1], ring_bank[k % 3], AX).then_inc(s_("ring_read"), 1)
                    k += 1
                if not isinstance(v_unit, int) or v_unit >= 2:
                    dve.wait_ge(s_("max_split"), v_unit - 1)
                dve.wait_ge(s_("ring_read"), item0 + k)
                v.tensor_tensor(rowmax[:, mslot, :], mx[:, mslot, :, 0], mx[:, mslot, :, 1], ALU.max)\
                    .then_inc(s_("max_ready"), 1)

            reduce_pass(0, 0, 0, None)
            reduce_pass(1, 1, 16, 0)

            def normalise(b, dens, spread_banks):
                rows, sl = slice(64 * b, 64 * b + 64), slice(b * L, (b + 1) * L)
                dve.wait_ge(s_(dens), (4, 2)[b] * 16)
                ch(v.tensor_tensor(den[rows, 0, :], den[rows, 0, :], den[rows, 1, :], ALU.add))
                v.reciprocal(den[rows, 1, :], den[rows, 0, :]).then_inc(s_("recip_ready"), 1)
                dve.wait_ge(s_(f"o_loaded{b}"), 4 * 16)
                ch(v.tensor_tensor(o_par[:, 0, sl], o_par[:, 0, sl], o_par[:, 1, sl], ALU.add))
                for h in range(2):
                    c = 2 * b + h
                    dve.wait_ge(s_("recip_spread"), c + 1)
                    v.tensor_tensor(onorm[:, c * CH:(c + 1) * CH], o_par[:, 0, c * CH:(c + 1) * CH], spread_banks[h],
                                    ALU.mult).then_inc(s_("onorm_ready"), 1)

            def project(b, out_banks):
                for h in range(2):
                    gi = 2 * b + h
                    dve.wait_ge(s_("attn_done"), gi + 1)
                    xg = xres[:, 4 * gi:4 * gi + 4, :]
                    ch(v.tensor_tensor(xg, xg, out_banks[h].rearrange("p (t c) -> p t c", t=4), ALU.add))
                    ln_start(dve, v, ch, 4 * gi, 4)

            def unit(i, s, last):
                u = 4 * i + s
                dve.wait_ge(s_(f"max_loaded{(s - 1) % 4}"), 16 * (i + (1 if s else 0)) + 16)
                if not (last and s >= 2):
                    reduce_pass(u + 2, s % 2, 33 + ITEMS * u, (s + 1) % 2)
                elif s == 2:
                    dve.wait_ge(s_("ring_full"), 33 + ITEMS * u + 1)
                    v.tensor_copy(mT[0:24, 1, :], ring_bank[0][0:24, 0:P]).then_inc(s_("ring_read"), 1)
                    normalise(0, "o_loaded0", bank[1:3])
                else:
                    project(0, bank[0:2])

            with dve.Fori(0, UNITS // 4 - 1) as i:
                for s in range(4):
                    unit(i, s, False)
            for s in range(4):
                unit(UNITS // 4 - 1, s, True)

            for gi in range(2):
                ln_end(dve, v, ch, 4 * gi, 4, gi + 1, "x1_ready")
            normalise(1, "den_loaded1", bank[5:7])
            project(1, (bank[7], bank[5]))
            for gi in range(2, 4):
                ln_end(dve, v, ch, 4 * gi, 4, gi + 1, "x1_ready")

            et = lambda ap: ap.rearrange("p e t -> p t e")
            over_e = lambda ap: ap.unsqueeze(1).to_broadcast([P, EXP, NT])
            lg, ls, ex, gates, t1, t2 = (R[n][:, :, :] for n in ("lg", "ls", "ex", "gates", "t1", "t2"))
            mask, incl, pos, keep, tw = (RW[n][:, :, :, :] for n in ("mask", "incl", "pos", "keep", "t"))
            dve.wait_ge(s_("logits_done"), 1)
            ch(v.tensor_copy(lg, bank[4][:, 0:NT * EXP].rearrange("p (t e) -> p e t", e=EXP)))
            ch(v.reduce_max(rt[:, 0, :], et(lg), AX))
            v.tensor_tensor(ls, lg, over_e(rt[:, 0, :]), ALU.subtract).then_inc(s_("logits_shifted"), 1)
            dve.wait_ge(s_("logits_shifted"), 1)
            ch(v.scalar_tensor_tensor(t1, ls, 0.0, rank[:, :, :], ALU.is_equal, ALU.mult))
            ch(v.reduce_max(rt[:, 1, :], et(t1), AX))
            ch(v.tensor_tensor(mask[:, 0], t1, over_e(rt[:, 1, :]), ALU.is_equal))
            v.tensor_copy(mask_b[:, 0], mask[:, 0]).then_inc(s_("mask_ready"), 1)

            def place(w):
                et2 = lambda ap: ap.rearrange("p (e t) -> p e t", e=EXP)
                flat = lambda ap: ap.rearrange("p e t -> p (e t)")
                earlier, totals = bank[5 + 2 * w][:, 0:EXP * NT], bank[5 + 2 * w][:, EXP * NT:2 * EXP * NT]
                dve.wait_ge(s_("places_done"), w + 1)
                ch(v.tensor_tensor_scan(flat(incl[:, w]), carry[:, :], totals, 0.0, ALU.mult, ALU.add))
                ch(v.tensor_tensor(tw[:, w], incl[:, w], et2(totals), ALU.subtract))
                ch(v.tensor_tensor(pos[:, w], tw[:, w], et2(earlier), ALU.add))
                if w == 0:
                    ch.mark(v.tensor_scalar(cap1[:, :], incl[:, 0, :, NT - 1], float(CAP), None, ALU.min))
                else:
                    ch(v.tensor_tensor(pos[:, 1], pos[:, 1], cap1[:, :].unsqueeze(2).to_broadcast([P, EXP, NT]), ALU.add))
                ch.mark(v.scalar_tensor_tensor(flat(keep[:, w]), flat(pos[:, w]), float(CAP), flat(mask[:, w]), ALU.is_lt, ALU.mult))
                ch(v.tensor_tensor(tw[:, w], pos[:, w], first[:, :, :], ALU.add))
                ch(v.tensor_tensor(tw[:, w], tw[:, w], keep[:, w], ALU.mult))
                ch(v.tensor_reduce(rt2[:, 0, w], et(tw[:, w]), AX, ALU.add))
                v.tensor_tensor(slot_i[:, w], rt2[:, 0, w], spill[:, :], ALU.add).then_inc(s_("slot_ready"), 1)

            place(0)
            ch(v.tensor_scalar(t2, ls, EXP_FLOOR, None, ALU.max))
            ch(v.scalar_tensor_tensor(t1, mask[:, 0], EXP_FLOOR, t2, ALU.mult, ALU.add))
            ch(v.reduce_max(rt[:, 2, :], et(t1), AX))
            ch(v.tensor_tensor(t2, t1, over_e(rt[:, 2, :]), ALU.is_equal))
            ch(v.tensor_tensor(t1, t2, rank[:, :, :], ALU.mult))
            ch(v.reduce_max(rt[:, 3, :], et(t1), AX))
            ch(v.tensor_tensor(mask[:, 1], t1, over_e(rt[:, 3, :]), ALU.is_equal))
            v.tensor_copy(mask_b[:, 1], mask[:, 1]).then_inc(s_("mask_ready"), 1)
            dve.wait_ge(s_("gate_exp"), 1)
            ch(v.tensor_reduce(rt[:, 4, :], et(ex), AX, ALU.add))
            ch(v.reciprocal(rt[:, 5, :], rt[:, 4, :]))
            ch(v.tensor_tensor(gates, ex, over_e(rt[:, 5, :]), ALU.mult))
            place(1)
            ch(v.tensor_tensor(second[:, :, :], slot_n[:, :, :], cap1[:, :].unsqueeze(2).to_broadcast([P, EXP, ST]), ALU.is_ge))
            ch(v.tensor_scalar(second[:, :, :], second[:, :, :], float(NTOK), -1.0, ALU.mult, ALU.add))
            wte = lambda ap: ap.rearrange("p w e t -> p w t e")
            for w in range(2):
                ch(v.tensor_tensor(tw[:, w], gates, keep[:, w], ALU.mult))
            ch(v.tensor_reduce(rt2[:, 3], wte(tw), AX, ALU.add))
            ch(v.tensor_tensor(rt[:, 0, :], rt2[:, 3, 0, :], rt2[:, 3, 1, :], ALU.add))
            ch(v.tensor_scalar(rt[:, 1, :], rt[:, 0, :], GATE_EPS, None, ALU.max))
            ch(v.reciprocal(rt[:, 2, :], rt[:, 1, :]))
            v.tensor_tensor(rt2[:, 4], rt2[:, 3], rt[:, 2, :].unsqueeze(1).to_broadcast([P, 2, NT]), ALU.mult)\
                .then_inc(s_("mask_ready"), 1)

            dve.wait_ge(s_("acc_ready"), 1)
            for c in range(NCH):
                dve.wait_ge(s_("shared_down"), c + 1)
                ag = acc[:, 4 * c:4 * c + 4, :]
                v.scalar_tensor_tensor(ag, bank[4 + c][:, :].rearrange("p (t c) -> p t c", t=4), SHARED_SCALE, ag,
                                       ALU.mult, ALU.add).then_inc(s_("shared_done"), 1)

            def copy_xeT(e, s, i, first):
                dve.wait_ge(s_("xeT_done"), e + 1)
                v.tensor_copy(xeT[:, s, :], pair[0][:, 0:CAP]).then_inc(s_("xeT_ready"), 1)
                dve.wait_ge(s_(f"slots_loaded{s}"), 16 * i + 16)
                if not first:
                    dve.wait_ge(s_("back_ready"), e)
                v.tensor_copy(number[:, s, :], xer[:, s, :, C:C + 1].rearrange("p t o -> p (t o)"))\
                    .then_inc(s_("number_kept"), 1)

            def expert_out(e, s, i, last=False):
                dve.wait_ge(s_("number_kept"), e + 1)
                dve.wait_ge(s_("back_ready"), e + 1)
                v.scalar_tensor_tensor(vrow[:, :], number[:, s, :], 0.0, one(vacant, e), ALU.is_equal, ALU.mult)\
                    .then_inc(s_("vrow_ready"), 1)
                dve.wait_ge(s_("vrow_ready"), 2 * e + 1)
                v.tensor_tensor(vrow[:, :], vrow[:, :], one(second, e), ALU.add).then_inc(s_("vrow_ready"), 1)
                dve.wait_ge(s_("vrow_ready"), 2 * e + 2)
                dve.wait_ge(s_("ye_left"), e + 1)
                v.tensor_tensor(back_i[:, s, :], vrow[:, :], number[:, s, :], ALU.add).then_inc(s_("back_ready"), 1)
                if last:
                    for k in range(ST):
                        dve.wait_ge(s_("ye_done"), e + 2 + k)
                        v.tensor_tensor(yer[:, s, k, :], bank[2 + k][:, 0:C], b2all[:, e, :], ALU.add).then_inc(s_("ye_ready"), 1)
                    return
                dve.wait_ge(s_("ye_done"), e + 2)
                v.tensor_tensor(yer[:, s, :, :], pair[3][:, 0:CAP].rearrange("p (t c) -> p t c", t=ST),
                                b2all[:, bass.ds(e, 1), :].to_broadcast([P, ST, C]), ALU.add).then_inc(s_("ye_ready"), 1)

            dve.wait_ge(s_("shared_done"), NCH)
            dve.sem_inc(s_("ye_ready"), 1)
            dve.sem_inc(s_("ye_left"), 2)
            dve.sem_inc(s_("back_ready"), 1)
            copy_xeT(0, 0, 0, True)
            with dve.Fori(0, EXP // 2 - 1) as i:
                for s in range(2):
                    copy_xeT(2 * i + s + 1, 1 - s, i + s, False)
                    expert_out(2 * i + s, s, i)
            copy_xeT(EXP - 1, 1, EXP // 2 - 1, False)
            expert_out(EXP - 2, 0, EXP // 2 - 1)
            expert_out(EXP - 1, 1, EXP // 2 - 1, True)

            dve.wait_ge(s_("mask_ready"), 3)
            for gi in range(4):
                dve.wait_ge(s_(f"picked{gi}"), 2 * 16)
                if gi > 0:
                    dve.wait_ge(s_("first_added"), gi)
                for w in range(1 if gi > 0 else 0, 2):
                    for t in range(4 * gi, 4 * gi + 4):
                        dst = acc if w == 0 else xres
                        ch.mark(v.scalar_tensor_tensor(dst[:, t, :], picked[:, w, t, :], rt2[:, 4, w, t:t + 1], acc[:, t, :],
                                                       ALU.mult, ALU.add))
                    ch.wait()
                ln_start(dve, v, ch, 4 * gi, 4)
                if gi > 0:
                    ln_end(dve, v, ch, 4 * gi - 4, 4, 4 + gi, "x2_ready")
            ln_end(dve, v, ch, 12, 4, 8, "x2_ready")

            dve.sem_inc(s_("h_ready"), CREDIT)
            dve.sem_inc(s_("hc_ready"), CREDIT)
            dve.sem_inc(s_("y_read"), 1)
            dve.wait_ge(s_("mixer_loaded"), 6 * 16)
            v.tensor_scalar(alog[:, :, :], alog[:, :, :], LOG_RATE_MAX, None, ALU.min).then_inc(s_("rate_step"), 1)

            def other_taps(q):
                dve.wait_ge(s_("last_tap"), q + 1)
                for j in range(1, TAPS):
                    ins = v.scalar_tensor_tensor(uu[:, q, j:L], pair[U_PAIR[q]][:, 0:L - j],
                                                 convw[:, q % DT, TAPS - 1 - j:TAPS - j], uu[:, q, j:L], ALU.mult, ALU.add)
                    if j < TAPS - 1:
                        ch(ins)
                ins.then_inc(s_("taps_done"), 1)

            def bc_rest(b):
                sl = slice(b * L, (b + 1) * L)
                dve.wait_ge(s_("bc_1"), b + 1)
                v.tensor_tensor(bc_r[0:96, sl], pair[BC_PAIR[b]][0:96, :], bc_parts[0:96, sl], ALU.subtract)\
                    .then_inc(s_("bc_rest"), 1)

            def bc_split(b):
                sl = slice(b * L, (b + 1) * L)
                dve.wait_ge(s_("bc_2"), b + 1)
                dve.wait_ge(s_("bc_rest"), b + 1)
                ch(v.tensor_copy(bc_parts[32:64, sl], bc_p2[32:64, sl]))
                v.tensor_tensor(bc_parts[64:96, sl], bc_r[64:96, sl], bc_p2[64:96, sl], ALU.subtract)\
                    .then_inc(s_("bc_ready"), 1)

            def log_terms(q):
                bias = biasT[:, BDT_ROW + q % 2:BDT_ROW + q % 2 + 1]
                dve.wait_ge(s_("sp_abs"), q + 1)
                v.tensor_scalar(delta[:, q, :], pair[DELTA_PAIR[q]][:, :], bias, 0.0, ALU.add, ALU.max)\
                    .then_inc(s_("sp_relu"), 1)
                dve.wait_ge(s_("sp_exp"), q + 1)
                v.tensor_scalar(sp_w[:, q, :], du[:, q, :], 1.0, None, ALU.add).then_inc(s_("sp_w_ready"), 1)
                dve.wait_ge(s_("sp_w_ready"), q + 1)
                v.scalar_tensor_tensor(du[:, q, :], sp_w[:, q, :], -1.0, du[:, q, :], ALU.add, ALU.subtract)\
                    .then_inc(s_("sp_c"), 1)

            for q in range(B * DT):
                other_taps(q)
            bc_rest(0)
            bc_split(0)
            log_terms(0)
            dve.wait_ge(s_("rate_step"), 2)
            v.tensor_scalar(alog[:, :, :], alog[:, :, :], -1.0, None, ALU.mult).then_inc(s_("rate_step"), 1)
            bc_rest(1)
            log_terms(1)
            log_terms(2)
            bc_split(1)
            log_terms(3)
            dve.wait_ge(s_("sp_relu"), B * DT)
            for q in range(B * DT):
                dve.wait_ge(s_("sp_small"), q + 1)
                v.tensor_tensor(delta[:, q, :], delta[:, q, :], sp_l[:, q, :], ALU.add).then_inc(s_("delta_ready"), 1)
                dve.wait_ge(s_("delta_ready"), q + 1)
                v.tensor_tensor(du[:, q, :], delta[:, q, :], uu[:, q, :], ALU.mult).then_inc(s_("du_ready"), 1)
            dve.wait_ge(s_("du_ready"), B * DT)

            with dve.Fori(0, B) as bb:
                for n in range(ST_N):
                    U = CREDIT + PER_B * bb + DT * n + 1
                    at = DT * (n % 2)
                    for d in range(DT):
                        dve.wait_ge(s_("dA_ready"), U + d)
                        dve.wait_ge(s_("dBu_ready"), U + d)
                        dve.wait_ge(s_("y_added"), U + d - 4)
                        v.tensor_tensor_scan(hh[:, at + d, :], dA[:, d, :], dBu[:, at + d, :], 0.0, ALU.mult, ALU.add)\
                            .then_inc(s_("h_ready"), 1)
                    for d in range(DT):
                        dve.wait_ge(s_("h_ready"), U + d)
                        if d == 0:
                            dve.wait_ge(s_("c_ready"), ST_N * bb + n + 1)
                        v.tensor_tensor(hh[:, at + d, :], hh[:, at + d, :], pair[1][:, :], ALU.mult)\
                            .then_inc(s_("hc_ready"), 1)
                for d in range(DT):
                    gg = DT * bb + d
                    dve.wait_ge(s_("y_added"), CREDIT + PER_B * (bb + 1))
                    v.scalar_tensor_tensor(one(uu, gg), one(uu, gg), biasT[:, D_ROW + d:D_ROW + d + 1], pair[2 + d][:, :],
                                           ALU.mult, ALU.add).then_inc(s_("y_read"), 1)
                    dve.wait_ge(s_("y_read"), gg + 2)
                    v.tensor_tensor(one(gate, gg), one(gate, gg), one(uu, gg), ALU.mult).then_inc(s_("y_ready"), 1)
            for gi in range(4):
                dve.wait_ge(s_("mixer_out"), gi + 1)
                xg = xres[:, 4 * gi:4 * gi + 4, :]
                ch(v.tensor_tensor(xg, xg, bank[gi][:, :].rearrange("p (t c) -> p t c", t=4), ALU.add))
                ln_start(dve, v, ch, 4 * gi, 4)
                if gi > 0:
                    ln_end(dve, v, ch, 4 * gi - 4, 4, 8 + gi, "x3_ready")
            ln_end(dve, v, ch, 12, 4, 12, "x3_ready")

            dve.wait_ge(s_("net_loaded"), NET_LOADS * 16)
            ch.mark(v.tensor_copy(gw3b[:, :], gw[2][:, 0:1].to_broadcast([32, P])))
            ch.mark(v.tensor_copy(w4b[:, :], cw4[:, 0:1].to_broadcast([P, P])))
            ch(v.tensor_scalar(cb4[:, :], cb4[:, :], 0.5, None, ALU.mult))
            ch(v.tensor_scalar(gb3[:, :], gb3[:, :], 0.5, None, ALU.mult))
            for b in range(B):
                dve.wait_ge(s_("state_ready"), 2 * b + 2)
                ch(v.tensor_reduce(gmean[:, 0, b:b + 1], xT[:, b * L:(b + 1) * L], AX, ALU.add))
            v.tensor_scalar(gmean[:, 1, :], gmean[:, 0, :], 1.0 / L, None, ALU.mult).then_inc(s_("mean_ready"), 1)
            ch(v.tensor_scalar(c_in[:, 3, 0:1], rng[:, :], sgn[:, :], 0.3, ALU.mult, ALU.mult))

            def cycle(i, first):
                for c in range(NCH):
                    dve.wait_ge(s_(f"twisted{c}"), 64 * (i + 1))
                    v.tensor_scalar(tw_s[:, c, :], tw_in[:, c, :], c_in[:, 3, 0:1], None, ALU.mult)\
                        .then_inc(s_("coupled"), 1)
                if first:
                    dve.wait_ge(s_("global_act"), 3)
                    ch(v.tensor_scalar(c_in[:, 0, :], gf[:, :], 0.7, None, ALU.mult))
                    ch(v.tensor_scalar(c_in[:, 1, :], c_in[:, 0, :], rng[:, :], 0.1, ALU.mult, ALU.add))
                    ch(v.tensor_scalar(c_in[:, 2, :], c_in[:, 1, :], sgn[:, :], None, ALU.mult))
                dve.wait_ge(s_("state_ready"), NCH * (i + 1))
                for c in range(NCH):
                    v.scalar_tensor_tensor(base[:, c, :], tw_in[:, c, :], c_in[:, 2, c // 2:c // 2 + 1],
                                           xT[:, c * CH:(c + 1) * CH], ALU.mult, ALU.add).then_inc(s_("coupled"), 1)
                for c in range(NCH):
                    dve.wait_ge(s_("net_act"), NET_STEPS * i + 7 + c + 1)
                    dve.wait_ge(s_("coupled"), 3 * NCH * i + 2 * NCH)
                    v.tensor_tensor(prod[:, c, :], tf[:, c, :], tw_s[:, c, :], ALU.mult).then_inc(s_("coupled"), 1)
                    dve.wait_ge(s_("coupled"), 3 * NCH * i + 2 * NCH + c + 1)
                    v.tensor_tensor(xT[:, c * CH:(c + 1) * CH], base[:, c, :], prod[:, c, :], ALU.add)\
                        .then_inc(s_("state_ready"), 1)

            cycle(0, True)
            with dve.Fori(1, CYCLES) as i:
                cycle(i, False)
            for gi in range(4):
                dve.wait_ge(s_("back_done"), gi + 1)
                xg = xres[:, 4 * gi:4 * gi + 4, :]
                ch(v.tensor_tensor(xg, xg, bank[gi][:, :].rearrange("p (t c) -> p t c", t=4), ALU.add))
                ln_start(dve, v, ch, 4 * gi, 4)
                if gi > 0:
                    ln_end(dve, v, ch, 4 * gi - 4, 4, 12 + gi, "x4_ready")
            ln_end(dve, v, ch, 12, 4, 16, "x4_ready")

        @block.tensor
        def _(pe):
            t = nc.tensor
            pe.wait_ge(s_("ident_ready"), 1)
            pe.wait_ge(s_("x_loaded"), 32)
            for c in range(NCH):
                for k in range(4):
                    last = t.transpose(bank[c][:, k * P:(k + 1) * P], xres[:, 4 * c + k, :], ident[:])
                last.then_inc(s_("xT_done"), 1)
            pe.wait_ge(s_("wcos_ready"), 1)
            t.transpose(bank[4][:, 0:P], wtmp[:, 2, :], ident[:]).then_inc(s_("wcosT_done"), 1)
            pe.wait_ge(s_("basis_loaded"), 4 * 16)
            pe.wait_ge(s_("wcos_ready"), 2)
            for j in range(4):
                last = t.matmul(bank[4 + j][:, 256:256 + C], basis[32 * j:32 * j + 32, :], wcosT[32 * j:32 * j + 32, :],
                                start=True, stop=True)
            last.then_inc(s_("weff_done"), 1)
            pe.wait_ge(s_("xT_copied_a"), 2)
            pe.wait_ge(s_("xT_copied_v"), 2)
            pe.wait_ge(s_("weff_copied"), 4)
            pe.wait_ge(s_("brow_loaded"), 6 * 16)
            t.transpose(bank[5][:, 0:BROWS], brow[:, :], ident[0:BROWS, 0:BROWS]).then_inc(s_("weff_done"), 1)
            pe.wait_ge(s_("biasT_ready"), 1)
            for b in range(B):
                for w in range(2):
                    for c in (2 * b, 2 * b + 1):
                        t.matmul(bank[4 * w + c][:, :], weff[:, w, :], xT[:, c * CH:(c + 1) * CH], start=True, stop=True)\
                            .then_inc(s_("qk_done"), 1)
            for c in range(NCH):
                pe.wait_ge(s_("resid_done"), (2, 2, 6, 6)[c])
                for k in range(4):
                    tt = 4 * c + k
                    last = t.matmul(bank[c][:, k * P:(k + 1) * P], xT[:, tt * P:(tt + 1) * P], weff[:, 2, :],
                                    start=True, stop=True)
                last.then_inc(s_("v_done"), 1)

            pe.sem_inc(s_("probs_free"), NPROB)
            pe.sem_inc(s_("st_done"), 1)
            pe.wait_ge(s_("resid_done"), 8)
            pe.wait_ge(s_("v_copied"), 4)

            def ring_wait(item0, k):
                if isinstance(item0, int) and item0 == 0:
                    if k >= 3:
                        pe.wait_ge(s_("ring_read"), k - 2)
                else:
                    pe.wait_ge(s_("ring_read"), item0 + (k - 2 if k >= 3 else 0))

            def s_half(slot, n, item0, k):
                ring_wait(item0, k)
                t.matmul(ring_bank[k % 3], qbuf[0:96, slot, (n // 2) * P:(n // 2 + 1) * P],
                         kbuf[0:96, slot, (n % 2) * CH:(n % 2 + 1) * CH], start=True, stop=True).then_inc(s_("ring_full"), 1)

            def max_T(m, mslot, item0, k):
                pe.wait_ge(s_("max_split"), m + 1)
                ring_wait(item0, k)
                t.matmul(ring_bank[k % 3][0:24, 0:P], mparts[:, mslot, :], ident_b[:], start=True, stop=True)\
                    .then_inc(s_("ring_full"), 1)

            def st_half(slot, kt, h):
                return t.matmul(st_pair[kt % 2][:, h * CH:(h + 1) * CH], kbuf[0:99, slot, kt * P:(kt + 1) * P],
                                qbuf[0:99, slot, h * CH:(h + 1) * CH], start=True, stop=True)

            def score_pass(v, slot, item0, maxT_slot):
                k = 0
                pe.wait_ge(s_(f"unit_loaded{slot}"), 32)
                for n in range(16):
                    if n == T_AT and maxT_slot is not None:
                        max_T(v - 1, maxT_slot, item0, k)
                        k += 1
                    s_half(slot, n, item0, k)
                    k += 1

            pe.wait_ge(s_("qk_cleared"), 1)
            score_pass(0, 0, 0, None)
            score_pass(1, 1, 16, 0)
            pe.wait_ge(s_("max_loaded0"), 16 + 16)
            for kt in range(2):
                for h in range(2):
                    last = st_half(0, kt, h)
                last.then_inc(s_("st_done"), 1)

            def spread_recip(b, banks):
                pe.wait_ge(s_("recip_ready"), b + 1)
                pe.wait_ge(s_("constants_ready"), 1)
                for h in range(2):
                    for k in range(2):
                        last = t.matmul(banks[h][:, k * (L // 4):(k + 1) * (L // 4)],
                                        expand[64 * b:64 * b + 64, 4 * b + 2 * h + k, :], den[64 * b:64 * b + 64, 1, :],
                                        start=True, stop=True)
                    last.then_inc(s_("recip_spread"), 1)

            def project(c, dst):
                pe.wait_ge(s_("onorm_ready"), c + 1)
                for k in range(4):
                    last = t.matmul(dst[:, k * P:(k + 1) * P], onorm[:, (4 * c + k) * P:(4 * c + k + 1) * P],
                                    weff[:, 3, :], start=True, stop=True)
                last.then_inc(s_("attn_done"), 1)

            def unit(i, s, last):
                u = 4 * i + s
                item0 = 33 + ITEMS * u
                v_slot, u1_slot = (s + 2) % 4, (s + 1) % 4
                scores = not (last and s >= 2)
                if scores:
                    pe.wait_ge(s_(f"unit_loaded{v_slot}"), 32 * (i + (1 if s < 2 else 2)))
                k = 0
                for j in range(KT):
                    for h in range(2):
                        n = 2 * j + h
                        if n == T_AT and not (last and s == 3):
                            max_T(u + 1, (s + 1) % 2, item0, k)
                            k += 1
                        if scores:
                            s_half(v_slot, n, item0, k)
                            k += 1
                        if last and s == 3 and j >= KT - 2:
                            continue
                        if h == 0:
                            if j == KT - 2:
                                pe.wait_ge(s_(f"max_loaded{u1_slot}"), 16 * (i + (1 if s < 3 else 2)) + 16)
                            pe.wait_ge(s_("exp_done"), KT * u + j + 1)
                        ins = st_half(s if j < KT - 2 else u1_slot, (j + 2) % KT, h)
                        if h == 1:
                            ins.then_inc(s_("st_done"), 1)
                    if j % 2 == 0:
                        continue
                    if j == 1:
                        pe.wait_ge(s_("v_staged"), u + 1)
                        pe.wait_ge(s_("pv_copied"), u + 1)
                    pe.wait_ge(s_("exp_done"), KT * u + j + 1)
                    for kt in (j - 1, j):
                        for h in range(2):
                            g = 2 * (kt % 2) + h
                            ins = t.matmul(pv_bank[32 * g:32 * g + 32, :], vst[:, s % 2, kt, :],
                                           probs[:, kt % NPROB, h * CH:(h + 1) * CH], start=kt < 2, stop=kt >= KT - 2)
                    ins.then_inc(s_("probs_free"), 2)
                    if last and s == 2 and j == 5:
                        spread_recip(0, bank[1:3])
                    if last and s == 3 and j in (1, 3):
                        project(j // 2, bank[j // 2])

            with pe.Fori(0, UNITS // 4 - 1) as i:
                for s in range(4):
                    unit(i, s, False)
            for s in range(4):
                unit(UNITS // 4 - 1, s, True)

            def x1_T(c):
                pe.wait_ge(s_("x1_ready"), 4 * c + 4)
                for k in range(4):
                    last = t.transpose(bank[c][:, k * P:(k + 1) * P], xres[:, 4 * c + k, :], ident[:])
                last.then_inc(s_("x1T_done"), 1)

            def logits(c):
                pe.wait_ge(s_("x1T_copied"), c + 1)
                for tt in range(4 * c, 4 * c + 4):
                    last = t.matmul(bank[4][:, tt * EXP:(tt + 1) * EXP], xT[:, tt * P:(tt + 1) * P], rw[:, :],
                                    start=True, stop=True)
                return last

            pe.wait_ge(s_("ffn_loaded"), 5 * 16)
            pe.wait_ge(s_("pv_copied"), UNITS + 1)
            x1_T(0)
            x1_T(1)
            logits(0)
            spread_recip(1, bank[5:7])
            logits(1)
            project(2, bank[7])
            project(3, bank[5])
            x1_T(2)
            x1_T(3)
            logits(2)
            logits(3).then_inc(s_("logits_done"), 1)

            def shared_up(c):
                for f in range(FT):
                    if c > 0:
                        pe.wait_ge(s_("shared_act"), (c - 1) * FT + f + 1)
                    t.matmul(bank[f][:, :], sw1[:, f * P:(f + 1) * P], xT[:, c * CH:(c + 1) * CH], start=True, stop=True)\
                        .then_inc(s_("shared_up"), 1)

            def shared_down(c):
                pe.wait_ge(s_("shared_act"), (c + 1) * FT)
                for k in range(4):
                    for f in range(FT):
                        last = t.matmul(bank[4 + c][:, k * C:(k + 1) * C], hsT[:, c % 2, f, k * P:(k + 1) * P], sw2[:, f, :],
                                        start=f == 0, stop=f == FT - 1)
                last.then_inc(s_("shared_down"), 1)

            def places(w):
                pe.wait_ge(s_("mask_ready"), w + 1)
                mb = mask_b[:, w].rearrange("p e t -> p (e t)")
                t.matmul(bank[5 + 2 * w][:, 0:EXP * NT], before[:, :], mb, start=True, stop=True)
                t.matmul(bank[5 + 2 * w][:, EXP * NT:2 * EXP * NT], ones_b[:, :], mb, start=True, stop=True)\
                    .then_inc(s_("places_done"), 1)

            places(0)
            shared_up(0)
            places(1)
            shared_up(1)
            pe.wait_ge(s_("slot_ready"), 2)
            shared_down(0)
            for c in range(1, NCH):
                if c + 1 < NCH:
                    shared_up(c + 1)
                shared_down(c)

            def slots_T(s, count):
                pe.wait_ge(s_(f"slots_loaded{s}"), count)
                for k in range(ST):
                    last = t.transpose(pair[0][:, k * P:(k + 1) * P], xer[:, s, k, 0:C], ident[:])
                last.then_inc(s_("xeT_done"), 1)

            def expert(i, s, last_e):
                e = 2 * i + s
                pe.wait_ge(s_("xeT_ready"), e + 1)
                pe.wait_ge(s_(f"expert_loaded{s}"), 32 * (i + 1))
                for f in range(FT):
                    pe.wait_ge(s_("up_act"), FT * e + f + 2)
                    for h in range(2):
                        last = t.matmul(pair[1 + f % 2][:, h * CH:h * CH + CAP // 2], w1r[:, s, f * P:(f + 1) * P],
                                        xeT[:, s, h * (CAP // 2):(h + 1) * (CAP // 2)], start=True, stop=True)
                    last.then_inc(s_("up_done"), 1)
                if not last_e:
                    slots_T(1 - s, 16 * (i + 1 + s))
                pe.wait_ge(s_("up_act"), FT * (e + 1) + 3)
                pe.wait_ge(s_("ye_ready"), e + 1)
                for k in range(ST):
                    dst = bank[2 + k][:, 0:C] if last_e else pair[3][:, k * C:(k + 1) * C]
                    for f in range(FT):
                        last = t.matmul(dst, hT[:, f, k * P:(k + 1) * P], w2r[:, s, f, :], start=f == 0, stop=f == FT - 1)
                    if last_e or k == ST - 1:
                        last.then_inc(s_("ye_done"), 1)

            pe.wait_ge(s_("shared_act"), NCH * FT)
            pe.wait_ge(s_("shared_done"), NCH)
            pe.sem_inc(s_("up_act"), 3)
            pe.sem_inc(s_("ye_done"), 1)
            slots_T(0, 16)
            with pe.Fori(0, EXP // 2 - 1) as i:
                for s in range(2):
                    expert(i, s, False)
            for s in range(2):
                expert(EXP // 2 - 1, s, s == 1)

            pe.wait_ge(s_("ye_ready"), EXP + ST)
            def x2_T(c):
                pe.wait_ge(s_("x2_ready"), 4 * c + 4)
                for k in range(4):
                    last = t.transpose(bank[c][:, k * P:(k + 1) * P], xres[:, 4 * c + k, :], ident[:])
                last.then_inc(s_("x2T_done"), 1)

            x2_T(0)
            x2_T(1)
            pe.wait_ge(s_("mixer_loaded"), 6 * 16)
            pe.wait_ge(s_("x2T_copied"), 2)

            def tokens(q, h):
                at = (q // DT) * L + h * CH
                return slice(at, at + CH)

            def u_in(q):
                for h in range(2):
                    last = t.matmul(pair[U_PAIR[q]][:, h * CH:(h + 1) * CH], win[:, (q % DT) * P:(q % DT + 1) * P],
                                    xT[:, tokens(q, h)], start=True, stop=True)
                last.then_inc(s_("u_in_done"), 1)

            def gate_in(q):
                for h in range(2):
                    last = t.matmul(pair[GATE_PAIR[q]][:, h * CH:(h + 1) * CH],
                                    win[:, DIN + (q % DT) * P:DIN + (q % DT + 1) * P], xT[:, tokens(q, h)],
                                    start=True, stop=True)
                last.then_inc(s_("gate_done"), 1)

            def bc(b):
                pe.wait_ge(s_("u_ready"), DT * b + DT)
                for h in range(2):
                    for d in range(DT):
                        last = t.matmul(pair[BC_PAIR[b]][0:104, h * CH:(h + 1) * CH], wx3[:, d, :],
                                        uu[:, DT * b + d, h * CH:(h + 1) * CH], start=d == 0, stop=d == DT - 1)
                last.then_inc(s_("bc_done"), 1)

            def delta_in(q):
                pe.wait_ge(s_("low_ready"), q // DT + 1)
                for h in range(2):
                    last = t.matmul(pair[DELTA_PAIR[q]][:, h * CH:(h + 1) * CH],
                                    wdt[96:96 + RANK, (q % DT) * P:(q % DT + 1) * P], low[96:96 + RANK, tokens(q, h)],
                                    start=True, stop=True)
                last.then_inc(s_("delta_done"), 1)

            u_in(0)
            x2_T(2)
            x2_T(3)
            gate_in(0)
            pe.wait_ge(s_("x2T_copied"), 4)
            u_in(1)
            gate_in(1)
            pe.wait_ge(s_("taps_done"), 1)
            u_in(2)
            pe.wait_ge(s_("gate_ready"), 1)
            gate_in(2)
            pe.wait_ge(s_("gate_ready"), 2)
            u_in(3)
            pe.wait_ge(s_("wx3_ready"), 1)
            pe.wait_ge(s_("taps_done"), 2)
            bc(0)
            pe.wait_ge(s_("gate_ready"), 3)
            gate_in(3)
            pe.wait_ge(s_("taps_done"), 3)
            delta_in(0)
            pe.wait_ge(s_("bc_rest"), 1)
            bc(1)
            pe.wait_ge(s_("taps_done"), 4)
            delta_in(1)
            pe.wait_ge(s_("gate_ready"), 4)
            delta_in(2)
            pe.wait_ge(s_("sp_relu"), 1)
            delta_in(3)

            pe.wait_ge(s_("bc_ready"), B)
            pe.wait_ge(s_("sp_relu"), B * DT)
            pe.sem_inc(s_("y_added"), CREDIT)
            def spread(row, dst, at):
                for h in range(2):
                    ins = t.matmul(dst[:, h * CH:(h + 1) * CH], sel[:, row, :], bc_parts[0:96, bass.ds(at + h * CH, CH)],
                                   start=True, stop=True)
                return ins

            spread(0, pair[0], 0).then_inc(s_("b_ready"), 1)
            with pe.Fori(0, B) as bb:
                def add_y(n):
                    for d in range(DT):
                        pe.wait_ge(s_("hc_ready"), CREDIT + PER_B * bb + DT * n + d + 1)
                        for h in range(2):
                            ins = t.matmul(pair[2 + d][:, h * CH:(h + 1) * CH], ident[:], hh[:, DT * (n % 2) + d, h * CH:(h + 1) * CH],
                                           start=n == 0, stop=n == ST_N - 1)
                        ins.then_inc(s_("y_added"), 1)

                for n in range(ST_N):
                    pe.wait_ge(s_("b_copied"), CREDIT + ST_N * bb + n + 1)
                    if n + 1 < ST_N:
                        ins = spread(n + 1, pair[0], bb * L)
                    else:
                        pe.sem_inc(s_("pe_waited"), 1)
                        ins = spread(0, pair[0], (B - 1) * L - bb * L)
                    ins.then_inc(s_("b_ready"), 1)
                    pe.wait_ge(s_("hc_ready"), CREDIT + PER_B * bb + DT * n)
                    spread(ST_N + n, pair[1], bb * L).then_inc(s_("c_ready"), 1)
                    if n == 1:
                        pe.wait_ge(s_("y_read"), DT * bb + 1)
                    if n > 0:
                        add_y(n - 1)
                add_y(ST_N - 1)
            for c in range(NCH):
                pe.wait_ge(s_("y_ready"), DT * (c // 2) + DT)
                pe.wait_ge(s_("hc_ready"), CREDIT + B * PER_B)
                for k in range(4):
                    at = (c % 2) * CH + k * P
                    for d in range(DT):
                        last = t.matmul(bank[c][:, k * P:(k + 1) * P], gate[:, DT * (c // 2) + d, at:at + P], wout[:, d, :],
                                        start=d == 0, stop=d == DT - 1)
                last.then_inc(s_("mixer_out"), 1)

            for c in range(NCH):
                pe.wait_ge(s_("x3_ready"), 4 * c + 4)
                for k in range(4):
                    last = t.transpose(bank[c][:, k * P:(k + 1) * P], xres[:, 4 * c + k, :], ident[:])
                last.then_inc(s_("x3T_done"), 1)
            pe.wait_ge(s_("net_loaded"), NET_LOADS * 16)

            def global_layer(n, w, src, dst):
                if n:
                    pe.wait_ge(s_("global_act"), n)
                else:
                    pe.wait_ge(s_("mean_ready"), 1)
                t.matmul(dst, w, src, start=True, stop=True).then_inc(s_("global_mm"), 1)

            def cycle(i, first):
                for c in range(NCH):
                    pe.wait_ge(s_("state_ready"), NCH * i + c + 1)
                    t.matmul(bank[c][:, :], cw1[:, :], xT[:, c * CH:(c + 1) * CH], start=True, stop=True)\
                        .then_inc(s_("net_mm"), 1)
                if first:
                    global_layer(0, gw[0][:, :], gmean[:, 1, :], bank[7][0:64, 0:B])
                for c in range(NCH):
                    pe.wait_ge(s_("net_act"), NET_STEPS * i + c + 1)
                    at = 64 * (c % 2)
                    last = t.matmul(bank[4 + c // 2][at:at + 64, :], cw2[:, :], m1[:, c, :], start=True, stop=True)
                    if c % 2 == 1:
                        last.then_inc(s_("net_mm"), 1)
                if first:
                    global_layer(1, gw[1][:, :], g1[:, :], bank[7][0:32, 0:B])
                pe.wait_ge(s_("net_act"), NET_STEPS * i + 4 + 2)
                pe.sem_inc(s_("pe_waited"), 1)
                for c in range(NCH):
                    at = 64 * (c % 2)
                    last = t.matmul(bank[6][32 * c:32 * c + 32, :], cw3[at:at + 64, :], m2[at:at + 64, c // 2, :],
                                    start=True, stop=True)
                last.then_inc(s_("net_mm"), 1)
                if first:
                    global_layer(2, gw3b[:, :], g2[:, :], bank[7][:, 0:B])
                pe.wait_ge(s_("net_act"), NET_STEPS * i + 7)
                for c in range(NCH):
                    t.matmul(bank[c][:, :], w4b[32 * c:32 * c + 32, :], m3[32 * c:32 * c + 32, :], start=True, stop=True)\
                        .then_inc(s_("net_mm"), 1)

            cycle(0, True)
            with pe.Fori(1, CYCLES) as i:
                cycle(i, False)
            pe.wait_ge(s_("net_act"), NET_STEPS * CYCLES)
            for c in range(NCH):
                pe.wait_ge(s_("state_ready"), NCH * CYCLES + c + 1)
                for k in range(4):
                    last = t.transpose(bank[c][:, k * P:(k + 1) * P], xT[:, c * CH + k * P:c * CH + (k + 1) * P], ident[:])
                last.then_inc(s_("back_done"), 1)


_INS = ["L0_attn_x"] + [f"L0_attn_{w}_{j}" for j in "qkvo" for w in ("basis", "phase", "amp")]
_INS += [f"L0_ffn_{n}" for n in ("router_w", "w1", "b1", "w2", "b2", "sw1", "sb1", "sw2", "sb2")]
_INS += [f"L1_attn_{n}" for n in ("W_in", "conv_w", "conv_b", "W_x", "W_dt", "b_dt", "A_log", "D", "W_out")]
_INS += [f"L1_ffn_cn_{w}{j}" for j in (1, 2, 3, 4) for w in "wb"] + [f"L1_ffn_gc_{w}{j}" for j in (1, 2, 3) for w in "wb"]
_INS += ["L1_ffn_adaptive_range"]
_OUTS = [((B, L, C), "float32")]


def kernel(**inputs):
    import numpy as np
    import concourse.bacc as bacc
    from concourse.bass_utils import run_bass_kernel_spmd

    nc = bacc.Bacc("TRN2", target_bir_lowering=False, num_devices=1)
    arrays = {f"in_{n}": np.ascontiguousarray(inputs[n]) for n in _INS}
    a = {n: nc.dram_tensor(f"in_{n}", arrays[f"in_{n}"].shape, mybir.dt.from_np(arrays[f"in_{n}"].dtype),
                           kind="ExternalInput").ap() for n in _INS}
    shape, dtype = _OUTS[0]
    out = nc.dram_tensor("out_0", shape, mybir.dt.from_np(np.dtype(dtype)), kind="ExternalOutput").ap()
    build(nc, a, out)
    r = run_bass_kernel_spmd(nc, [arrays], core_ids=[0])
    return r.results[0]["out_0"]
```
